# Optimizing a Trainium2 kernel written in Bass

```python
import numpy as np
import jax
import jax.numpy as jnp

def _softmax(x, axis=-1):
    return jax.nn.softmax(x, axis=axis)

def _gelu(x):
    return jax.nn.gelu(x, approximate=True)

def _silu(x):
    return jax.nn.silu(x)

def _sigmoid(x):
    return jax.nn.sigmoid(x)

def _layernorm(x, axis=-1, eps=1e-05):
    m = jnp.mean(x, axis=axis, keepdims=True)
    v = jnp.var(x, axis=axis, keepdims=True)
    return (x - m) / jnp.sqrt(v + eps)

def _scatter_add(tgt, idx, src, axis=0):
    return tgt.at[idx].add(src)

def _segment_sum(src, seg, n):
    return jax.ops.segment_sum(src, seg, n)
kernel_name = 'mk_seq_preln_d2_jaxref_r8_e33370'

def setup_inputs(seed: int=0):
    np.random.seed(seed)
    _w = jnp.asarray

    def _L0_attn_setup():
        import jax, jax.numpy as jnp
        import numpy as np
        D_MODEL = 128
        D_STATE = 16
        D_CONV = 4
        EXPAND = 2
        D_INNER = D_MODEL * EXPAND
        DT_RANK = max(D_MODEL // 16, 1)
        B, L = (2, 256)

        def _layernorm(x, w, b, eps=1e-05):
            mu = jnp.mean(x, axis=-1, keepdims=True)
            var = jnp.mean(jnp.square(x - mu), axis=-1, keepdims=True)
            return (x - mu) * jax.lax.rsqrt(var + eps) * w + b

        def _causal_depthwise_conv1d(x_cl, conv_w, conv_b):
            out = jax.lax.conv_general_dilated(x_cl, conv_w[:, None, :], window_strides=(1,), padding=[(D_CONV - 1, 0)], dimension_numbers=('NCH', 'OIH', 'NCH'), feature_group_count=D_INNER)
            return out + conv_b[None, :, None]

        def _reference_tuple_inner(x, ln_w, ln_b, in_proj_w, conv_w, conv_b, x_proj_w, dt_proj_w, dt_proj_b, A_log, D_param, out_proj_w, res_scale):
            residual = x
            xn = _layernorm(x, ln_w, ln_b)
            xz = xn @ in_proj_w
            x_main, z = jnp.split(xz, 2, axis=-1)
            x_conv = _causal_depthwise_conv1d(jnp.swapaxes(x_main, 1, 2), conv_w, conv_b)
            new_conv_state = jnp.swapaxes(x_main, 1, 2)[:, :, -(D_CONV - 1):]
            x_main = jax.nn.silu(jnp.swapaxes(x_conv, 1, 2))
            A = -jnp.exp(A_log)
            x_dbl = x_main @ x_proj_w
            dt, B_ssm, C_ssm = jnp.split(x_dbl, [DT_RANK, DT_RANK + D_STATE], axis=-1)
            dt = jax.nn.softplus(dt @ dt_proj_w + dt_proj_b)
            dA = jnp.exp(A[None, None] * dt[..., None])
            dBx = dt[..., None] * B_ssm[:, :, None, :] * x_main[..., None]

            def scan_fn(h, inp):
                dA_t, dBx_t, C_t = inp
                h = dA_t * h + dBx_t
                y_t = jnp.einsum('bdn,bn->bd', h, C_t)
                return (h, y_t)
            h0 = jnp.zeros((x.shape[0], D_INNER, D_STATE), x.dtype)
            new_ssm_state, ys = jax.lax.scan(scan_fn, h0, (jnp.swapaxes(dA, 0, 1), jnp.swapaxes(dBx, 0, 1), jnp.swapaxes(C_ssm, 0, 1)))
            y = jnp.swapaxes(ys, 0, 1)
            y = y + x_main * D_param[None, None, :]
            y = y * jax.nn.silu(z)
            out = res_scale * (y @ out_proj_w) + residual
            return (out, new_ssm_state, new_conv_state)
        key = jax.random.key(seed)
        ks = jax.random.split(key, 10)
        s = lambda fan_in: 1.0 / np.sqrt(fan_in)
        x = jax.random.normal(ks[0], (B, L, D_MODEL), dtype=jnp.float32)
        ln_w = jnp.ones((D_MODEL,), jnp.float32)
        ln_b = jnp.zeros((D_MODEL,), jnp.float32)
        in_proj_w = jax.random.normal(ks[1], (D_MODEL, 2 * D_INNER), jnp.float32) * s(D_MODEL)
        conv_w = jax.random.normal(ks[2], (D_INNER, D_CONV), jnp.float32) * s(D_CONV)
        conv_b = jnp.zeros((D_INNER,), jnp.float32)
        x_proj_w = jax.random.normal(ks[3], (D_INNER, DT_RANK + 2 * D_STATE), jnp.float32) * s(D_INNER)
        dt_proj_w = jax.random.normal(ks[4], (DT_RANK, D_INNER), jnp.float32) * s(DT_RANK)
        dt_proj_b = jax.random.normal(ks[5], (D_INNER,), jnp.float32) * 0.1
        A_log = jnp.broadcast_to(jnp.log(jnp.arange(1, D_STATE + 1, dtype=jnp.float32))[None, :], (D_INNER, D_STATE)).copy()
        D_param = jnp.ones((D_INNER,), jnp.float32)
        out_proj_w = jax.random.normal(ks[6], (D_INNER, D_MODEL), jnp.float32) * s(D_INNER)
        res_scale = jnp.ones((1,), jnp.float32)
        return dict(x=x, ln_w=ln_w, ln_b=ln_b, in_proj_w=in_proj_w, conv_w=conv_w, conv_b=conv_b, x_proj_w=x_proj_w, dt_proj_w=dt_proj_w, dt_proj_b=dt_proj_b, A_log=A_log, D_param=D_param, out_proj_w=out_proj_w, res_scale=res_scale)
    _L0_attn_in = _L0_attn_setup()

    def _L0_ffn_setup():
        import jax, jax.numpy as jnp
        import numpy as np
        D_MODEL = 128
        HIDDEN = 256
        E_ROUTED = 14
        E_SHARED = 2
        TOP_K = 2
        EPS = 1e-09
        RMS_EPS = 1.1920929e-07

        def _ffn(xn, rw, W1, W2):
            ms = jnp.mean(xn * xn, axis=-1, keepdims=True)
            h = xn * jax.lax.rsqrt(ms + RMS_EPS) * rw
            return jax.nn.silu(h @ W1) @ W2
        key = jax.random.key(seed)
        ks = jax.random.split(key, 9)
        B, T = (2, 128)
        x = jax.random.normal(ks[0], (B, T, D_MODEL), dtype=jnp.float32)
        router_w = jax.random.normal(ks[1], (D_MODEL, E_ROUTED), dtype=jnp.float32) * 0.006
        rms_w = jnp.ones((E_ROUTED, D_MODEL), dtype=jnp.float32)
        w1 = jax.random.normal(ks[2], (E_ROUTED, D_MODEL, HIDDEN), dtype=jnp.float32) * 0.02
        w2 = jax.random.normal(ks[3], (E_ROUTED, HIDDEN, D_MODEL), dtype=jnp.float32) * 0.02
        rms_w_s = jnp.ones((E_SHARED, D_MODEL), dtype=jnp.float32)
        w1_s = jax.random.normal(ks[4], (E_SHARED, D_MODEL, HIDDEN), dtype=jnp.float32) * 0.02
        w2_s = jax.random.normal(ks[5], (E_SHARED, HIDDEN, D_MODEL), dtype=jnp.float32) * 0.02
        return {'x': x, 'router_w': router_w, 'rms_w': rms_w, 'w1': w1, 'w2': w2, 'rms_w_s': rms_w_s, 'w1_s': w1_s, 'w2_s': w2_s}
    _L0_ffn_in = _L0_ffn_setup()

    def _L1_attn_setup():
        import jax, jax.numpy as jnp
        import numpy as np
        EMB, KDIM, B, S = (128, 64, 8, 256)
        key = jax.random.key(seed)
        kx, kq, kk, kv1, kv2 = jax.random.split(key, 5)

        def xavier(k, shape):
            fan_in, fan_out = shape
            lim = (6.0 / (fan_in + fan_out)) ** 0.5
            return jax.random.uniform(k, shape, jnp.float32, -lim, lim)
        return {'x': jax.random.normal(kx, (B, S, EMB), jnp.float32), 'w_q': xavier(kq, (EMB, KDIM)), 'w_k': xavier(kk, (EMB, KDIM)), 'w_v1': xavier(kv1, (EMB, KDIM)), 'w_v2': xavier(kv2, (KDIM, EMB))}
    _L1_attn_in = _L1_attn_setup()

    def _L1_ffn_setup():
        import jax, jax.numpy as jnp
        import numpy as np
        EPS = 1e-05
        LN_EPS = 1e-05
        NUM_EXPERTS = 8
        TOP_K = 2
        HIDDEN = 128
        INTER = 256

        def _swiglu(x, wg, wu, wd):
            return jax.nn.silu(x @ wg) * (x @ wu) @ wd
        key = jax.random.key(seed)
        ks = jax.random.split(key, 10)
        B, S, H, I, E = (8, 512, HIDDEN, INTER, NUM_EXPERTS)
        std_h = 1.0 / np.sqrt(H)
        std_i = 1.0 / np.sqrt(I)
        return {'x': jax.random.normal(ks[0], (B, S, H), dtype=jnp.float32), 'ln_scale': jnp.ones((H,), dtype=jnp.float32), 'ln_bias': jnp.zeros((H,), dtype=jnp.float32), 'gate_w': jax.random.normal(ks[1], (E, H), dtype=jnp.float32) * 0.01, 'Wg': jax.random.normal(ks[2], (E, H, I), dtype=jnp.float32) * std_h, 'Wu': jax.random.normal(ks[3], (E, H, I), dtype=jnp.float32) * std_h, 'Wd': jax.random.normal(ks[4], (E, I, H), dtype=jnp.float32) * std_i, 'sWg': jax.random.normal(ks[5], (H, I), dtype=jnp.float32) * std_h, 'sWu': jax.random.normal(ks[6], (H, I), dtype=jnp.float32) * std_h, 'sWd': jax.random.normal(ks[7], (I, H), dtype=jnp.float32) * std_i}
    _L1_ffn_in = _L1_ffn_setup()
    _d = {'L0_attn_x': _L0_attn_in['x'], 'L0_attn_ln_w': _L0_attn_in['ln_w'], 'L0_attn_ln_b': _L0_attn_in['ln_b'], 'L0_attn_in_proj_w': _L0_attn_in['in_proj_w'], 'L0_attn_conv_w': _L0_attn_in['conv_w'], 'L0_attn_conv_b': _L0_attn_in['conv_b'], 'L0_attn_x_proj_w': _L0_attn_in['x_proj_w'], 'L0_attn_dt_proj_w': _L0_attn_in['dt_proj_w'], 'L0_attn_dt_proj_b': _L0_attn_in['dt_proj_b'], 'L0_attn_A_log': _L0_attn_in['A_log'], 'L0_attn_D_param': _L0_attn_in['D_param'], 'L0_attn_out_proj_w': _L0_attn_in['out_proj_w'], 'L0_attn_res_scale': _L0_attn_in['res_scale'], 'L0_ffn_router_w': _L0_ffn_in['router_w'], 'L0_ffn_rms_w': _L0_ffn_in['rms_w'], 'L0_ffn_w1': _L0_ffn_in['w1'], 'L0_ffn_w2': _L0_ffn_in['w2'], 'L0_ffn_rms_w_s': _L0_ffn_in['rms_w_s'], 'L0_ffn_w1_s': _L0_ffn_in['w1_s'], 'L0_ffn_w2_s': _L0_ffn_in['w2_s'], 'L1_attn_w_q': _L1_attn_in['w_q'], 'L1_attn_w_k': _L1_attn_in['w_k'], 'L1_attn_w_v1': _L1_attn_in['w_v1'], 'L1_attn_w_v2': _L1_attn_in['w_v2'], 'L1_ffn_ln_scale': _L1_ffn_in['ln_scale'], 'L1_ffn_ln_bias': _L1_ffn_in['ln_bias'], 'L1_ffn_gate_w': _L1_ffn_in['gate_w'], 'L1_ffn_Wg': _L1_ffn_in['Wg'], 'L1_ffn_Wu': _L1_ffn_in['Wu'], 'L1_ffn_Wd': _L1_ffn_in['Wd'], 'L1_ffn_sWg': _L1_ffn_in['sWg'], 'L1_ffn_sWu': _L1_ffn_in['sWu'], 'L1_ffn_sWd': _L1_ffn_in['sWd']}
    _x0 = _d['L0_attn_x']
    _d['L0_attn_x'] = jax.random.normal(jax.random.fold_in(jax.random.key(seed), 1), (8, 512, 128), dtype=_x0.dtype)
    del _x0
    return _d

def reference(L0_attn_x, L0_attn_ln_w, L0_attn_ln_b, L0_attn_in_proj_w, L0_attn_conv_w, L0_attn_conv_b, L0_attn_x_proj_w, L0_attn_dt_proj_w, L0_attn_dt_proj_b, L0_attn_A_log, L0_attn_D_param, L0_attn_out_proj_w, L0_attn_res_scale, L0_ffn_router_w, L0_ffn_rms_w, L0_ffn_w1, L0_ffn_w2, L0_ffn_rms_w_s, L0_ffn_w1_s, L0_ffn_w2_s, L1_attn_w_q, L1_attn_w_k, L1_attn_w_v1, L1_attn_w_v2, L1_ffn_ln_scale, L1_ffn_ln_bias, L1_ffn_gate_w, L1_ffn_Wg, L1_ffn_Wu, L1_ffn_Wd, L1_ffn_sWg, L1_ffn_sWu, L1_ffn_sWd):

    def _L0_attn_ref(x, ln_w, ln_b, in_proj_w, conv_w, conv_b, x_proj_w, dt_proj_w, dt_proj_b, A_log, D_param, out_proj_w, res_scale):
        import jax, jax.numpy as jnp
        import numpy as np
        D_MODEL = 128
        D_STATE = 16
        D_CONV = 4
        EXPAND = 2
        D_INNER = D_MODEL * EXPAND
        DT_RANK = max(D_MODEL // 16, 1)
        B, L = (2, 256)

        def _layernorm(x, w, b, eps=1e-05):
            mu = jnp.mean(x, axis=-1, keepdims=True)
            var = jnp.mean(jnp.square(x - mu), axis=-1, keepdims=True)
            return (x - mu) * jax.lax.rsqrt(var + eps) * w + b

        def _causal_depthwise_conv1d(x_cl, conv_w, conv_b):
            out = jax.lax.conv_general_dilated(x_cl, conv_w[:, None, :], window_strides=(1,), padding=[(D_CONV - 1, 0)], dimension_numbers=('NCH', 'OIH', 'NCH'), feature_group_count=D_INNER)
            return out + conv_b[None, :, None]

        def _reference_tuple_inner(x, ln_w, ln_b, in_proj_w, conv_w, conv_b, x_proj_w, dt_proj_w, dt_proj_b, A_log, D_param, out_proj_w, res_scale):
            residual = x
            xn = _layernorm(x, ln_w, ln_b)
            xz = xn @ in_proj_w
            x_main, z = jnp.split(xz, 2, axis=-1)
            x_conv = _causal_depthwise_conv1d(jnp.swapaxes(x_main, 1, 2), conv_w, conv_b)
            new_conv_state = jnp.swapaxes(x_main, 1, 2)[:, :, -(D_CONV - 1):]
            x_main = jax.nn.silu(jnp.swapaxes(x_conv, 1, 2))
            A = -jnp.exp(A_log)
            x_dbl = x_main @ x_proj_w
            dt, B_ssm, C_ssm = jnp.split(x_dbl, [DT_RANK, DT_RANK + D_STATE], axis=-1)
            dt = jax.nn.softplus(dt @ dt_proj_w + dt_proj_b)
            dA = jnp.exp(A[None, None] * dt[..., None])
            dBx = dt[..., None] * B_ssm[:, :, None, :] * x_main[..., None]

            def scan_fn(h, inp):
                dA_t, dBx_t, C_t = inp
                h = dA_t * h + dBx_t
                y_t = jnp.einsum('bdn,bn->bd', h, C_t)
                return (h, y_t)
            h0 = jnp.zeros((x.shape[0], D_INNER, D_STATE), x.dtype)
            new_ssm_state, ys = jax.lax.scan(scan_fn, h0, (jnp.swapaxes(dA, 0, 1), jnp.swapaxes(dBx, 0, 1), jnp.swapaxes(C_ssm, 0, 1)))
            y = jnp.swapaxes(ys, 0, 1)
            y = y + x_main * D_param[None, None, :]
            y = y * jax.nn.silu(z)
            out = res_scale * (y @ out_proj_w) + residual
            return (out, new_ssm_state, new_conv_state)
        return _reference_tuple_inner(x, ln_w, ln_b, in_proj_w, conv_w, conv_b, x_proj_w, dt_proj_w, dt_proj_b, A_log, D_param, out_proj_w, res_scale)[0]

    def _L0_ffn_ref(x, router_w, rms_w, w1, w2, rms_w_s, w1_s, w2_s):
        import jax, jax.numpy as jnp
        import numpy as np
        D_MODEL = 128
        HIDDEN = 256
        E_ROUTED = 14
        E_SHARED = 2
        TOP_K = 2
        EPS = 1e-09
        RMS_EPS = 1.1920929e-07

        def _ffn(xn, rw, W1, W2):
            ms = jnp.mean(xn * xn, axis=-1, keepdims=True)
            h = xn * jax.lax.rsqrt(ms + RMS_EPS) * rw
            return jax.nn.silu(h @ W1) @ W2
        B, T, D = x.shape
        N = B * T
        xf = x.reshape(N, D)
        gates = jax.nn.softmax(xf @ router_w, axis=-1)
        top_v, top_i = jax.lax.top_k(gates, TOP_K)
        masked = jnp.zeros_like(gates).at[jnp.arange(N)[:, None], top_i].set(top_v)
        masked = masked / (masked.sum(axis=-1, keepdims=True) + EPS)
        routed = jax.vmap(lambda rw_, W1_, W2_: _ffn(xf, rw_, W1_, W2_))(rms_w, w1, w2)
        routed_out = jnp.einsum('end,ne->nd', routed, masked)
        shared = jax.vmap(lambda rw_, W1_, W2_: _ffn(xf, rw_, W1_, W2_))(rms_w_s, w1_s, w2_s).sum(0)
        return (routed_out + shared).reshape(B, T, D)

    def _L1_attn_ref(x, w_q, w_k, w_v1, w_v2):
        import jax, jax.numpy as jnp
        import numpy as np
        EMB, KDIM, B, S = (128, 64, 8, 256)
        seq = x.shape[1]
        queries = jnp.einsum('bse,ek->bsk', x, w_q)
        keys = jnp.einsum('bse,ek->bsk', x, w_k)
        scale = w_q.shape[1] ** (-0.5)
        scores = jnp.einsum('bqk,bsk->bqs', queries, keys) * scale
        causal = jnp.tril(jnp.ones((seq, seq), dtype=bool))
        scores = jnp.where(causal[None, :, :], scores, -jnp.inf)
        attn = jax.nn.softmax(scores, axis=-1)
        values = jnp.einsum('bsk,ke->bse', jnp.einsum('bse,ek->bsk', x, w_v1), w_v2)
        return jnp.einsum('bqs,bse->bqe', attn, values)

    def _L1_ffn_ref(x, ln_scale, ln_bias, gate_w, Wg, Wu, Wd, sWg, sWu, sWd):
        import jax, jax.numpy as jnp
        import numpy as np
        EPS = 1e-05
        LN_EPS = 1e-05
        NUM_EXPERTS = 8
        TOP_K = 2
        HIDDEN = 128
        INTER = 256

        def _swiglu(x, wg, wu, wd):
            return jax.nn.silu(x @ wg) * (x @ wu) @ wd
        B, S, H = x.shape
        xf = x.reshape(-1, H)
        mu = jnp.mean(xf, axis=-1, keepdims=True)
        var = jnp.var(xf, axis=-1, keepdims=True)
        xn = (xf - mu) * jax.lax.rsqrt(var + LN_EPS) * ln_scale + ln_bias
        logits = xn @ gate_w.T
        probs = jax.nn.softmax(logits, axis=-1)
        tk_probs, tk_idx = jax.lax.top_k(probs, TOP_K)
        tk_probs = tk_probs / (jnp.sum(tk_probs, axis=-1, keepdims=True) + EPS)
        onehot = tk_idx[..., None] == jnp.arange(NUM_EXPERTS)[None, None, :]
        w = jnp.sum(tk_probs[..., None] * onehot.astype(tk_probs.dtype), axis=1)
        out = _swiglu(xf, sWg, sWu, sWd)
        for e in range(NUM_EXPERTS):
            out = out + w[:, e:e + 1] * _swiglu(xf, Wg[e], Wu[e], Wd[e])
        return out.reshape(B, S, H)
    x = L0_attn_x
    x = x + _L0_attn_ref(_layernorm(x, axis=-1), L0_attn_ln_w, L0_attn_ln_b, L0_attn_in_proj_w, L0_attn_conv_w, L0_attn_conv_b, L0_attn_x_proj_w, L0_attn_dt_proj_w, L0_attn_dt_proj_b, L0_attn_A_log, L0_attn_D_param, L0_attn_out_proj_w, L0_attn_res_scale)
    x = x + _L0_ffn_ref(_layernorm(x, axis=-1), L0_ffn_router_w, L0_ffn_rms_w, L0_ffn_w1, L0_ffn_w2, L0_ffn_rms_w_s, L0_ffn_w1_s, L0_ffn_w2_s)
    x = x + _L1_attn_ref(_layernorm(x, axis=-1), L1_attn_w_q, L1_attn_w_k, L1_attn_w_v1, L1_attn_w_v2)
    x = x + _L1_ffn_ref(_layernorm(x, axis=-1), L1_ffn_ln_scale, L1_ffn_ln_bias, L1_ffn_gate_w, L1_ffn_Wg, L1_ffn_Wu, L1_ffn_Wd, L1_ffn_sWg, L1_ffn_sWu, L1_ffn_sWd)
    return x

_drawn_inputs = setup_inputs


def setup_inputs(seed=0):
    import zlib

    import numpy as np

    out = dict(_drawn_inputs(seed))
    spreads = {'L0_attn_ln_w': (1.0, 0.2),
     'L0_attn_ln_b': (0.0, 0.1),
     'L0_attn_conv_b': (0.0, 0.1),
     'L0_attn_D_param': (1.0, 0.2),
     'L0_ffn_rms_w': (1.0, 0.6),
     'L0_ffn_rms_w_s': (1.0, 0.6),
     'L1_ffn_ln_scale': (1.0, 0.2),
     'L1_ffn_ln_bias': (0.0, 0.1)}
    factors = {}
    for name, (base, spread) in spreads.items():
        noise = np.random.default_rng([zlib.crc32(name.encode()), seed]).standard_normal(out[name].shape)
        drawn = base * np.exp(spread * noise) if base else spread * noise
        out[name] = jnp.asarray(drawn.astype(out[name].dtype))
    for name, factor in factors.items():
        out[name] = (out[name] * factor).astype(out[name].dtype)
    return out
```

```python
import concourse.bass as bass
from concourse import mybir
from contextlib import ExitStack


def mamba_moe_attention_moe_kernel(nc: bass.Bass, A: dict, out: bass.AP):
    f32 = mybir.dt.float32
    bf16 = mybir.dt.bfloat16
    ALU = mybir.AluOpType
    ACT = mybir.ActivationFunctionType
    AX = mybir.AxisListType

    P = 128
    NB, L, D = A["L0_attn_x"].shape
    TPB = L // P
    NT = NB * TPB
    NTOK = NB * L
    DI = A["L0_attn_D_param"].shape[0]
    NG = DI // P
    TAPS = A["L0_attn_conv_w"].shape[1]
    PAD = TAPS - 1
    NS = A["L0_attn_A_log"].shape[1]
    RANK = A["L0_attn_dt_proj_w"].shape[0]
    BC = 2 * NS
    E0 = A["L0_ffn_router_w"].shape[1]
    E0S = A["L0_ffn_w1_s"].shape[0]
    E1 = A["L1_ffn_gate_w"].shape[0]
    HID = A["L0_ffn_w1"].shape[2]
    NH = HID // P
    KD = A["L1_attn_w_q"].shape[1]
    GW = 16
    LN_EPS = 1e-5
    RMS_EPS = 1.1920929e-07
    TOPK0_EPS = 1e-9
    TOPK1_EPS = 1e-5
    NEG = -1e30

    ctx = ExitStack()
    with ctx:
        def sb(name, shape, dt=f32):
            return ctx.enter_context(nc.sbuf_tensor(name, shape, dt))

        def sem(name):
            return ctx.enter_context(nc.semaphore(name))

        x = sb("x", [P, NT, D])
        xT = sb("xT", [P, NB, PAD + L])
        big1 = sb("big1", [P, NG, NTOK])
        big2 = sb("big2", [P, NG, NTOK])
        big3 = sb("big3", [P, NG, NTOK])
        dt, u, xm = big1, big2, big3
        xnt = sb("xnt", [P, 2, TPB, D])
        bc = sb("bc", [3 * BC, NTOK + L], bf16)
        sel = sb("sel", [3 * BC, BC, P], bf16)
        selg = sb("selg", [3 * GW, GW, P], bf16)
        ident = sb("ident", [P, P])
        cmask = sb("cmask", [P, P])
        Wk = sb("Wk", [P, TAPS, DI])
        cwb = sb("cwb", [P, DI, TAPS])
        inw = sb("inw", [P, 2 * DI])
        xpw = sb("xpw", [P, NG, 3 * BC + RANK])
        dtw = sb("dtw", [3 * BC + RANK, DI])
        opw = sb("opw", [P, NG, D])
        cols = sb("cols", [P, 16])
        Aneg = sb("Aneg", [P, NG, NS])
        ring = sb("ring", [P, 16, L])
        stats = sb("stats", [P, NT, 6])
        sm = sb("sm", [P, 16, NT])
        gl = big3[:, 0, 0:8 * NT * GW].rearrange("p (q t e) -> p q t e", t=NT, e=GW)
        iot = sb("iot", [P, NT, GW])
        wr = sb("wr", [P, E0])
        gwT = sb("gwT", [P, E1])
        gwr = sb("gwr", [E1, P])
        vrows = sb("vrows", [10, P])
        rs_sb = sb("rs_sb", [P, 1])
        lnbr = sb("lnbr", [P, P])
        gconst = sb("gconst", [P, E1])
        rmsT = sb("rmsT", [P, E0 + E0S])
        rmsr = sb("rmsr", [E0 + E0S, P])
        wqk = sb("wqk", [P, 3, KD])
        wv2 = sb("wv2", [KD, D])
        ps = [ctx.enter_context(nc.psum_tensor(f"ps{i}", [P, 2, L], f32)) for i in range(4)]

        lnw, lnb = cols[:, 0:1], cols[:, 1:2]
        convb = cols[:, 2:2 + NG]
        dtb = cols[:, 4:4 + NG]
        Dp = cols[:, 6:6 + NG]
        lnsb = cols[:, 8:10]
        rs = rs_sb[:, :]
        NV = 10

        mu, var, r1, r2, t0, t1, t2, t3, gain, shift = (sm[:, k, :] for k in range(10))
        root = sm[:, 10, :]
        rl = sm[:, 11, :]

        loaded = sem("loaded")
        ident_ready = sem("ident_ready")
        carried = sem("carried")
        vec_done = sem("vec_done")
        x_in = sem("x_in")
        w_in = [sem(f"w_in{k}") for k in range(2)]
        stored = sem("stored")
        step = sem("step")
        step_act = sem("step_act")
        step_pool = sem("step_pool")
        phase_done = sem("phase_done")
        rs_in = sem("rs_in")
        rs_out = sem("rs_out")

        def sems(prefix, names):
            return {n: sem(f"{prefix}_{n}") for n in names.split()}

        ln = [sems(f"ln{k}", "norm tr xT") for k in range(4)]
        pre = sems("pre", "conv xm xp dtr split dtp absd soft dt u")
        sc = sems("sc", "bb cb cs da dbx scan hc ns y")
        po = sems("po", "z sz gated o oc tr add")
        gt = [sems(f"gt{k}", "wt wc lt lc tm tk logit stage tr copied") for k in range(2)]
        mo = [sems(f"mo{k}", "g h sil um gb gm mm2 acc tr add") for k in range(2)]
        at = sems("at", "qkv qkvs v vs s mx p pt pts o add")

        DEPTH = (4, 3)
        block = ctx.enter_context(nc.Block())

        x_d = A["L0_attn_x"].rearrange("b (k p) d -> p (b k) d", p=P)
        out_d = out.rearrange("b (k p) d -> p (b k) d", p=P)

        moe0_w1 = big1[:, 0, :].rearrange("p (e h) -> p e h", h=HID)
        moe0_w2 = big1[:, 1, :].rearrange("p (e b d) -> p e b d", b=NH, d=D)
        NE1 = E1 + 1
        b2 = big2[:, :, :].rearrange("p g t -> p (g t)")
        moe1_wg = b2[:, 0:NE1 * HID].rearrange("p (e h) -> p e h", h=HID)
        moe1_wu = b2[:, NE1 * HID:2 * NE1 * HID].rearrange("p (e h) -> p e h", h=HID)
        moe1_wd = b2[:, 2 * NE1 * HID:3 * NE1 * HID].rearrange("p (e b d) -> p e b d", b=NH, d=D)

        smalls = []

        def vec(name):
            return A[name].rearrange("(g p) -> g p", p=P)

        smalls += [(vrows[0:1, :], vec("L0_attn_ln_w")), (vrows[1:2, :], vec("L0_attn_ln_b")),
                   (vrows[2:2 + NG, :], vec("L0_attn_conv_b")), (vrows[4:4 + NG, :], vec("L0_attn_dt_proj_b")),
                   (vrows[6:6 + NG, :], vec("L0_attn_D_param")),
                   (vrows[8:9, :], vec("L1_ffn_ln_scale")), (vrows[9:10, :], vec("L1_ffn_ln_bias")),
                   (rs, A["L0_attn_res_scale"].rearrange("(a o) -> a o", a=1).to_broadcast([P, 1])),
                   (inw[:, :], A["L0_attn_in_proj_w"]),
                   (cwb[:, :, :].rearrange("p c k -> p (c k)"),
                    A["L0_attn_conv_w"].rearrange("(a c) k -> a (c k)", a=1).to_broadcast([P, DI * TAPS])),
                   (Aneg[:, :, :], A["L0_attn_A_log"].rearrange("(g p) n -> p g n", p=P)),
                   (opw[:, :, :], A["L0_attn_out_proj_w"].rearrange("(g p) n -> p g n", p=P)),
                   (dtw[3 * BC:3 * BC + RANK, :], A["L0_attn_dt_proj_w"]),
                   (wr[:, :], A["L0_ffn_router_w"]),
                   (gwr[:, :], A["L1_ffn_gate_w"]),
                   (rmsr[0:E0, :], A["L0_ffn_rms_w"]), (rmsr[E0:E0 + E0S, :], A["L0_ffn_rms_w_s"]),
                   (wqk[:, 0, :], A["L1_attn_w_q"]), (wqk[:, 1, :], A["L1_attn_w_k"]),
                   (wqk[:, 2, :], A["L1_attn_w_v1"]), (wv2[:, :], A["L1_attn_w_v2"])]
        xpw_d = A["L0_attn_x_proj_w"].rearrange("(g p) n -> p g n", p=P)
        smalls += [(xpw[:, :, k * BC:(k + 1) * BC], xpw_d[:, :, RANK:RANK + BC]) for k in range(3)]
        smalls += [(xpw[:, :, 3 * BC:], xpw_d[:, :, 0:RANK])]

        def barrier(eng, n):
            eng.drain().then_inc(phase_done, 1)
            eng.wait_ge(phase_done, 4 * n)

        def carry(eng):
            eng.sem_inc(carried, 1)

        @block.sync
        def _(sp):
            sp.dma_start(x[:, :, :], x_d).then_inc(x_in, 16)
            for dst, src in smalls:
                sp.dma_start(dst, src).then_inc(loaded, 16)
            sp.wait_ge(phase_done, 4 * 4)
            for dst, src in ((moe0_w1[:, 0:E0, :], A["L0_ffn_w1"].rearrange("e d h -> d e h")),
                             (moe0_w1[:, E0:, :], A["L0_ffn_w1_s"].rearrange("e d h -> d e h"))):
                sp.dma_start(dst, src).then_inc(w_in[0], 16)
            for dst, src in ((moe0_w2[:, 0:E0, :, :], A["L0_ffn_w2"].rearrange("e (b p) d -> p e b d", p=P)),
                             (moe0_w2[:, E0:, :, :], A["L0_ffn_w2_s"].rearrange("e (b p) d -> p e b d", p=P))):
                for e in range(dst.shape[1]):
                    sp.dma_start(dst[:, e, :, :], src[:, e, :, :]).then_inc(w_in[0], 16)
            for w, a, s in ((moe1_wg, "L1_ffn_Wg", "L1_ffn_sWg"), (moe1_wu, "L1_ffn_Wu", "L1_ffn_sWu")):
                sp.dma_start(w[:, 0:E1, :], A[a].rearrange("e d h -> d e h")).then_inc(w_in[1], 16)
                sp.dma_start(w[:, E1, :], A[s]).then_inc(w_in[1], 16)
            wd = A["L1_ffn_Wd"].rearrange("e (b p) d -> p e b d", p=P)
            for e in range(E1):
                sp.dma_start(moe1_wd[:, e, :, :], wd[:, e, :, :]).then_inc(w_in[1], 16)
            sp.dma_start(moe1_wd[:, E1, :, :], A["L1_ffn_sWd"].rearrange("(b p) d -> p b d", p=P)).then_inc(w_in[1], 16)
            sp.wait_ge(phase_done, 4 * 11)
            sp.dma_start(out_d, x[:, :, :]).then_inc(stored, 16)
            sp.wait_ge(stored, 16)

        W_MOE0 = 16 * (2 + E0 + E0S)
        W_MOE1 = 16 * (4 + E1 + 1)
        N_SMALL = 16 * len(smalls)

        @block.gpsimd
        def _(pool):
            n = [0]

            def link(ins):
                n[0] += 1
                ins.then_inc(step_pool, 1)
                pool.wait_ge(step_pool, n[0])

            link(nc.gpsimd.memset(ident[:, :], 0.0))
            link(nc.gpsimd.affine_select(out=ident[:, :], in_=ident[:, :], compare_op=ALU.not_equal, fill=1.0,
                                         base=0, pattern=[[-1, P]], channel_multiplier=1))
            pool.sem_inc(ident_ready, 1)
            link(nc.gpsimd.memset(cmask[:, :], 0.0))
            link(nc.gpsimd.affine_select(out=cmask[:, :], in_=cmask[:, :], compare_op=ALU.is_ge, fill=NEG,
                                         base=0, pattern=[[-1, P]], channel_multiplier=1))
            link(nc.gpsimd.memset(xT[:, :, 0:PAD], 0.0))
            link(nc.gpsimd.memset(sel[:, :, :], 0.0))
            link(nc.gpsimd.memset(selg[:, :, :], 0.0))
            link(nc.gpsimd.memset(bc[:, NTOK:], 0.0))
            for k in range(3):
                link(nc.gpsimd.affine_select(out=sel[:, :, :], in_=sel[:, :, :], compare_op=ALU.not_equal, fill=1.0,
                                             base=-k * BC, pattern=[[-1, BC], [0, P]], channel_multiplier=1))
                link(nc.gpsimd.affine_select(out=selg[:, :, :], in_=selg[:, :, :], compare_op=ALU.not_equal,
                                             fill=1.0, base=-k * GW, pattern=[[-1, GW], [0, P]],
                                             channel_multiplier=1))
            link(nc.gpsimd.iota(iot[:, :, :], pattern=[[0, NT], [-1, GW]], base=GW, channel_multiplier=0,
                                allow_small_or_imprecise_dtypes=True))
            barrier(pool, 1)

            barrier(pool, 2)

            with pool.Fori(0, NB) as b:
                pool.wait_ge(pre["dt"], b + 1 + 2)
                w = bass.ds(b * L, L)
                nc.gpsimd.tensor_tensor(u[:, :, w], dt[:, :, w], xm[:, :, w], ALU.mult)
            barrier(pool, 3)

            h, hc, cs = ring[:, 2:6, :], ring[:, 6:10, :], ring[:, 10:12, :]
            pool.sem_inc(sc["hc"], 4)
            with pool.Fori(0, NB) as b:
                for n_ in range(NS):
                    for g in range(NG):
                        m = n_ * NG + g
                        M = b * (NS * NG) + m
                        pool.wait_ge(sc["scan"], M + 1 + 2)
                        if g == 0:
                            pool.wait_ge(sc["cs"], b * NS + n_ + 1 + 2)
                        pool.wait_ge(sc["ns"], M + 1)
                        nc.gpsimd.tensor_tensor(hc[:, m % 4, :], h[:, m % 4, :], cs[:, n_ % 2, :],
                                                ALU.mult).then_inc(sc["hc"], 1)
            for k in range(4, 12):
                barrier(pool, k)

        @block.scalar
        def _(act):
            n = [0]

            def link(ins):
                n[0] += 1
                ins.then_inc(step_act, 1)
                act.wait_ge(step_act, n[0])

            roots = [0]

            def inverse_root():
                roots[0] += 1
                act.wait_ge(rs_in, roots[0])
                link(nc.scalar.activation(rl, t0, ACT.Ln))
                nc.scalar.activation(root, rl, ACT.Exp, scale=-0.5).then_inc(rs_out, 1)

            def evacuate(k, phase, scale=None, bias=None, after=None):
                s = ln[k]
                act.sem_inc(s["xT"], 2)
                with act.Fori(0, NB // 2) as i:
                    for j in range(2):
                        b = i * 2 + j
                        act.wait_ge(s["tr"], b + 1 + 2)
                        carry(act)
                        dst = xT[:, bass.ds(b, 1), PAD:].rearrange("p o t -> p (o t)")
                        if scale is None:
                            nc.scalar.activation(dst, ps[0][:, j, :], ACT.Copy).then_inc(s["xT"], 1)
                        else:
                            nc.scalar.activation(dst, ps[0][:, j, :], ACT.Identity, scale=scale,
                                                 bias=bias).then_inc(s["xT"], 1)
                        if after:
                            after(b, j)

            act.wait_ge(loaded, N_SMALL)
            link(nc.scalar.activation(Aneg[:, :, :], Aneg[:, :, :], ACT.Exp))
            link(nc.scalar.mul(Aneg[:, :, :], Aneg[:, :, :], -1.0))
            inverse_root()
            inverse_root()
            barrier(act, 1)

            act.sem_inc(pre["xm"], 2)

            def silu_conv(b, j):
                act.wait_ge(pre["conv"], b + 1)
                carry(act)
                for g in range(NG):
                    last = nc.scalar.activation(xm[:, g, bass.ds(b * L, L)], ps[1 + j][:, g, :], ACT.Silu,
                                                bias=convb[:, g:g + 1])
                last.then_inc(pre["xm"], 1)

            evacuate(0, 2, lnw, lnb, silu_conv)
            barrier(act, 2)

            dtr = ring[:, 0:2, :]
            av = ring[:, 2:4, :]
            lt = ring[:, 4:8, :]
            with act.Fori(0, NB // 2) as i:
                for j in range(2):
                    b = i * 2 + j
                    act.wait_ge(pre["xp"], b + 1)
                    nc.scalar.activation(dtr[3 * BC:3 * BC + RANK, j, :], ps[0][3 * BC:3 * BC + RANK, j, :],
                                         ACT.Copy).then_inc(pre["dtr"], 1)
                    act.wait_ge(pre["dtp"], b + 1)
                    for g in range(NG):
                        last = nc.scalar.activation(av[:, g, :], ps[1 + j][:, g, :], ACT.Abs, bias=dtb[:, g:g + 1])
                    last.then_inc(pre["absd"], 1)
                    act.wait_ge(pre["absd"], b * 2 + 1)
                    nc.scalar.activation(av[:, :, :], av[:, :, :], ACT.Exp, scale=-1.0).then_inc(pre["absd"], 1)
                    act.wait_ge(pre["absd"], b * 2 + 2)
                    act.wait_ge(pre["dt"], b + 1 - 2 + 2)
                    nc.scalar.activation(lt[:, 2 * j:2 * j + 2, :], av[:, :, :], ACT.Ln, bias=1.0)\
                        .then_inc(pre["soft"], 1)
            barrier(act, 3)

            act.sem_inc(sc["cs"], 2)
            cs = ring[:, 10:12, :]
            with act.Fori(0, NB) as b:
                for n_ in range(NS):
                    N = b * NS + n_
                    for g in range(NG):
                        M = b * (NS * NG) + n_ * NG + g
                        act.wait_ge(sc["scan"], M + 1)
                        carry(act)
                        nc.scalar.activation(ps[2][:, g, :], dt[:, g, bass.ds(b * L, L)], ACT.Exp,
                                             scale=Aneg[:, g, n_:n_ + 1]).then_inc(sc["da"], 1)
                        if g == 0:
                            act.wait_ge(sc["cb"], N + 1)
                            act.wait_ge(sc["hc"], N * 2 + 2)
                            nc.scalar.activation(cs[:, n_ % 2, :], ps[1][:, n_ % 2, :], ACT.Copy)\
                                .then_inc(sc["cs"], 1)
            barrier(act, 4)

            sz = ring[:, 0:4, :]
            act.sem_inc(po["sz"], 2)
            act.sem_inc(po["oc"], 2)
            with act.Fori(0, NB // 2) as i:
                for j in range(2):
                    b = i * 2 + j
                    act.wait_ge(po["z"], b + 1)
                    act.wait_ge(po["gated"], b + 1)
                    nc.scalar.activation(sz[:, 2 * j:2 * j + 2, :], ps[j][:, :, :], ACT.Silu).then_inc(po["sz"], 1)
                    act.wait_ge(po["o"], b + 1)
                    act.wait_ge(po["tr"], b + 1)
                    nc.scalar.activation(ring[:, 4 + j, :], ps[2][:, j, :], ACT.Copy).then_inc(po["oc"], 1)
            barrier(act, 5)

            def gates(k, E):
                s = gt[k]
                act.sem_inc(s["lc"], 2)
                with act.Fori(0, NB // 2) as i:
                    for j in range(2):
                        b = i * 2 + j
                        act.wait_ge(s["lt"], b + 1)
                        act.wait_ge(s["tm"], b + 1)
                        nc.scalar.activation(ring[0:E, j, :], ps[1][0:E, j, :], ACT.Copy).then_inc(s["lc"], 1)
                act.wait_ge(s["logit"], 1)
                nc.scalar.activation(gl[:, 1, :, 0:E], gl[:, 0, :, 0:E], ACT.Exp).then_inc(s["logit"], 1)

            def moe(k, units):
                s = mo[k]
                depth = DEPTH[k]
                hs = ring[:, 0:4, :]
                ya = ring[:, 10, :]
                act.sem_inc(s["sil"], 2)
                act.sem_inc(s["acc"], 1)
                with act.Fori(0, NB) as c:
                    for q in range(units):
                        K = c * units + q
                        act.wait_ge(s["g"] if k else s["h"], K + 1)
                        act.wait_ge(s["um"] if k else s["gm"], K + 1)
                        nc.scalar.activation(hs[:, q % depth, :], ps[0][:, q % 2, :], ACT.Silu).then_inc(s["sil"], 1)
                    act.wait_ge(s["mm2"], (c + 1) * units + depth)
                    nc.scalar.activation(ya, ps[3][:, 0, :], ACT.Copy).then_inc(s["acc"], 1)

            inverse_root()
            inverse_root()
            evacuate(1, 6)
            barrier(act, 6)
            gates(0, E0)
            barrier(act, 7)
            moe(0, (E0 + E0S) * NH)
            barrier(act, 8)

            inverse_root()
            evacuate(2, 9)
            qkv = ring[:, 0:3, :]
            vs = ring[:, 3, :]
            pr = ring[:, 4:8, :]
            pt = ring[:, 8:10, :]
            act.sem_inc(at["pts"], 1)
            with act.Fori(0, NB) as b:
                act.wait_ge(at["qkv"], b + 1)
                nc.scalar.activation(qkv[0:KD, 0, :], ps[2][0:KD, 0, :], ACT.Copy, scale=float(KD) ** -0.5)
                nc.scalar.activation(qkv[0:KD, 1, :], ps[2][0:KD, 1, :], ACT.Copy)
                nc.scalar.activation(qkv[0:KD, 2, :], ps[3][0:KD, 0, :], ACT.Copy).then_inc(at["qkvs"], 1)
                act.wait_ge(at["v"], b + 1)
                nc.scalar.activation(vs, ps[3][:, 1, :], ACT.Copy).then_inc(at["vs"], 1)
                for i in range(TPB):
                    act.wait_ge(at["mx"], b * TPB + i + 1)
                    W = (i + 1) * P
                    nc.scalar.activation(pr[:, i, 0:W], ps[i // 2][:, i % 2, 0:W], ACT.Exp,
                                         bias=sm[:, 12, i:i + 1], accum_out=sm[:, 13, i:i + 1])\
                        .then_inc(at["p"], 1)
                    act.wait_ge(at["pt"], b * TPB + i + 1)
                    nc.scalar.activation(pt[:, i % 2, 0:W], ps[2][:, i % 2, 0:W], ACT.Copy).then_inc(at["pts"], 1)
            barrier(act, 9)

            inverse_root()
            inverse_root()
            evacuate(3, 10)
            gates(1, E1)
            barrier(act, 10)
            moe(1, NE1 * NH)
            barrier(act, 11)

        @block.vector
        def _(dve):
            n = [0]

            def link(ins):
                n[0] += 1
                ins.then_inc(step, 1)
                dve.wait_ge(step, n[0])

            roots = [0]

            def inverse_root(dst, z):
                link(nc.vector.tensor_copy(t0, z))
                roots[0] += 1
                dve.sem_inc(rs_in, 1)
                dve.wait_ge(rs_out, roots[0])
                link(nc.vector.tensor_tensor(t1, root, root, ALU.mult))
                link(nc.vector.tensor_tensor(t1, t1, t0, ALU.mult))
                link(nc.vector.tensor_scalar(t1, t1, -0.5, 1.5, ALU.mult, ALU.add))
                link(nc.vector.tensor_tensor(dst, root, t1, ALU.mult))

            def moments():
                with dve.Fori(0, NB) as b:
                    for k in range(TPB):
                        t = b * TPB + k
                        last = nc.vector.bn_stats(stats[:, bass.ds(t, 1), :].rearrange("p o s -> p (o s)"),
                                                  x[:, bass.ds(t, 1), :].rearrange("p o d -> p (o d)"))
                dve.drain()
                me, ve, mo_, vo = stats[:, :, 1], stats[:, :, 2], stats[:, :, 4], stats[:, :, 5]
                link(nc.vector.tensor_tensor(t0, me, mo_, ALU.add))
                link(nc.vector.tensor_scalar(mu, t0, 0.5, None, ALU.mult))
                link(nc.vector.tensor_tensor(t1, me, mo_, ALU.subtract))
                link(nc.vector.tensor_tensor(t1, t1, t1, ALU.mult))
                link(nc.vector.tensor_tensor(t2, ve, vo, ALU.add))
                link(nc.vector.scalar_tensor_tensor(out=var, in0=t1, scalar=D / 4.0, in1=t2, op0=ALU.mult,
                                                    op1=ALU.add))
                link(nc.vector.tensor_scalar(var, var, 1.0 / D, None, ALU.mult))
                link(nc.vector.tensor_scalar(t3, var, LN_EPS, None, ALU.add))
                inverse_root(r1, t3)

            def second_root(eps):
                link(nc.vector.tensor_tensor(t3, r1, r1, ALU.mult))
                link(nc.vector.tensor_tensor(t3, t3, var, ALU.mult))
                link(nc.vector.tensor_scalar(t3, t3, eps, None, ALU.add))
                inverse_root(r2, t3)

            def normalise(k, scale):
                s = ln[k]
                with dve.Fori(0, NB // 2) as i:
                    for j in range(2):
                        b = i * 2 + j
                        dve.wait_ge(s["tr"], b + 1)
                        for q in range(TPB):
                            t = b * TPB + q
                            last = nc.vector.tensor_scalar(
                                xnt[:, j, q, :], x[:, bass.ds(t, 1), :].rearrange("p o d -> p (o d)"),
                                mu[:, bass.ds(t, 1)], scale[:, bass.ds(t, 1)], ALU.subtract, ALU.mult)
                        last.then_inc(s["norm"], 1)
                        if k == 0:
                            for q in range(TPB):
                                t = b * TPB + q
                                xt = x[:, bass.ds(t, 1), :].rearrange("p o d -> p (o d)")
                                nc.vector.tensor_scalar(xt, xt, gain[:, bass.ds(t, 1)], shift[:, bass.ds(t, 1)],
                                                        ALU.mult, ALU.add)

            dve.wait_ge(vec_done, 1)
            nc.vector.tensor_copy(cols[:, 0:NV], ps[1][:, 0, 0:NV])
            dve.wait_ge(loaded, N_SMALL)
            for k in range(TAPS):
                link(nc.vector.tensor_tensor(Wk[:, k, :], inw[:, 0:DI], cwb[:, :, k], ALU.mult))
            dve.wait_ge(x_in, 16)
            moments()
            second_root(LN_EPS)
            link(nc.vector.tensor_tensor(r2, r1, r2, ALU.mult))
            link(nc.vector.tensor_scalar(gain, r1, 1.0, None, ALU.add))
            link(nc.vector.scalar_tensor_tensor(out=shift, in0=mu, scalar=-1.0, in1=r1, op0=ALU.mult, op1=ALU.mult))
            barrier(dve, 1)

            normalise(0, r2)
            barrier(dve, 2)

            part = ring[:, 8, :]
            lt = ring[:, 4:8, :]
            dve.sem_inc(pre["split"], 2)
            dve.sem_inc(pre["dt"], 2)
            with dve.Fori(0, NB // 2) as i:
                for j in range(2):
                    b = i * 2 + j
                    w = bass.ds(b * L, L)
                    B3, B2 = 3 * BC, 2 * BC
                    dve.wait_ge(pre["xp"], b + 1)
                    carry(dve)
                    nc.vector.tensor_copy(bc[0:B3, w], ps[0][0:B3, j, :]).then_inc(step, 1)
                    dve.wait_ge(step, n[0] + b * 5 + 1)
                    nc.vector.tensor_tensor(part[0:B3, :], ps[0][0:B3, j, :], bc[0:B3, w], ALU.subtract)\
                        .then_inc(step, 1)
                    dve.wait_ge(step, n[0] + b * 5 + 2)
                    carry(dve)
                    nc.vector.tensor_copy(bc[BC:B2, w], part[BC:B2, :])
                    nc.vector.tensor_copy(bc[B2:B3, w], part[B2:B3, :]).then_inc(step, 1)
                    dve.wait_ge(step, n[0] + b * 5 + 3)
                    nc.vector.tensor_tensor(part[B2:B3, :], part[B2:B3, :], bc[B2:B3, w], ALU.subtract)\
                        .then_inc(step, 1)
                    dve.wait_ge(step, n[0] + b * 5 + 4)
                    carry(dve)
                    nc.vector.tensor_copy(bc[B2:B3, w], part[B2:B3, :]).then_inc(pre["split"], 1)
                    dve.wait_ge(pre["soft"], b + 1)
                    for g in range(NG):
                        last = nc.vector.scalar_tensor_tensor(out=dt[:, g, w], in0=ps[1 + j][:, g, :],
                                                              scalar=dtb[:, g:g + 1], in1=lt[:, 2 * j + g, :],
                                                              op0=ALU.add, op1=ALU.add)
                    last.then_inc(step, 1)
                    dve.wait_ge(step, n[0] + b * 5 + 5)
                    nc.vector.tensor_tensor(dt[:, :, w], dt[:, :, w], lt[:, 2 * j:2 * j + 2, :], ALU.max)\
                        .then_inc(pre["dt"], 1)
            n[0] += 5 * NB
            barrier(dve, 3)

            dbx, h = ring[:, 12:16, :], ring[:, 2:6, :]
            dve.sem_inc(sc["dbx"], 4)
            dve.sem_inc(sc["scan"], 2)
            dve.sem_inc(sc["y"], 1)

            def add_skip(b):
                dve.wait_ge(sc["ns"], (b + 1) * (NS * NG) + 4)
                for g in range(NG):
                    w = bass.ds(b * L, L)
                    last = nc.vector.scalar_tensor_tensor(out=xm[:, g, w], in0=xm[:, g, w], scalar=Dp[:, g:g + 1],
                                                          in1=ps[3][:, g, :], op0=ALU.mult, op1=ALU.add)
                last.then_inc(sc["y"], 1)

            def scan_batch(b, first):
                def input_term(m):
                    n_, g = m // NG, m % NG
                    if g == 0:
                        dve.wait_ge(sc["bb"], b * NS + n_ + 1)
                    if not first or m:
                        dve.wait_ge(sc["scan"], b * (NS * NG) + m)
                    nc.vector.tensor_tensor(dbx[:, m % 4, :], u[:, g, bass.ds(b * L, L)], ps[0][:, n_ % 2, :],
                                            ALU.mult).then_inc(sc["dbx"], 1)

                input_term(0)
                for m in range(NS * NG):
                    M = b * (NS * NG) + m
                    if m == 3 and not first:
                        add_skip(b - 1)
                    if m + 1 < NS * NG:
                        input_term(m + 1)
                    dve.wait_ge(sc["dbx"], M + 1 + 4)
                    dve.wait_ge(sc["da"], M + 1)
                    dve.wait_ge(sc["hc"], M + 1)
                    nc.vector.tensor_tensor_scan(h[:, m % 4, :], ps[2][:, m % NG, :], dbx[:, m % 4, :], 0.0,
                                                 ALU.mult, ALU.add).then_inc(sc["scan"], 1)

            scan_batch(0, True)
            with dve.Fori(1, NB) as b:
                scan_batch(b, False)
            add_skip(NB - 1)
            barrier(dve, 4)

            sz = ring[:, 0:4, :]
            dve.sem_inc(po["gated"], 2)
            dve.sem_inc(po["add"], 2)
            with dve.Fori(0, NB // 2) as i:
                for j in range(2):
                    b = i * 2 + j
                    w = bass.ds(b * L, L)
                    dve.wait_ge(po["sz"], b + 1 + 2)
                    nc.vector.tensor_tensor(xm[:, :, w], xm[:, :, w], sz[:, 2 * j:2 * j + 2, :], ALU.mult)\
                        .then_inc(po["gated"], 1)
                    dve.wait_ge(po["tr"], b + 1 + 2)
                    xb = x[:, bass.ds(b * TPB, TPB), :].rearrange("p t d -> p (t d)")
                    nc.vector.scalar_tensor_tensor(out=xb, in0=ps[3][:, j, :], scalar=rs, in1=xb,
                                                   op0=ALU.mult, op1=ALU.add).then_inc(po["add"], 1)
            barrier(dve, 5)

            def top2(k, E, eps):
                s = gt[k]
                W = [gl[:, q, :, 0:E] for q in range(8)]
                tk = [sm[:, q, :] for q in (12, 13, 14)]

                def row(v):
                    return v.unsqueeze(2).to_broadcast([P, NT, E])

                def by_row(out_, a, v, op):
                    link(nc.vector.tensor_tensor(out_, a, row(v), op))

                link(nc.vector.tensor_reduce(tk[0], W[0], op=ALU.max, axis=AX.X))
                by_row(W[0], W[0], tk[0], ALU.subtract)
                dve.sem_inc(s["logit"], 1)
                dve.wait_ge(s["logit"], 2)
                link(nc.vector.tensor_reduce(tk[0], W[1], op=ALU.add, axis=AX.X))
                link(nc.vector.reciprocal(tk[0], tk[0]))
                by_row(W[1], W[1], tk[0], ALU.mult)
                iv = iot[:, :, 0:E]
                link(nc.vector.tensor_copy(W[2], W[1]))
                for q in range(2):
                    link(nc.vector.tensor_reduce(tk[q], W[2], op=ALU.max, axis=AX.X))
                    by_row(W[3], W[2], tk[q], ALU.is_equal)
                    link(nc.vector.tensor_tensor(W[3], W[3], iv, ALU.mult))
                    link(nc.vector.tensor_reduce(tk[2], W[3], op=ALU.max, axis=AX.X))
                    by_row(W[4 + q], W[3], tk[2], ALU.is_equal)
                    if q == 0:
                        link(nc.vector.scalar_tensor_tensor(out=W[2], in0=W[4], scalar=-2.0, in1=W[2],
                                                            op0=ALU.mult, op1=ALU.add))
                link(nc.vector.tensor_tensor(W[4], W[4], W[5], ALU.add))
                link(nc.vector.tensor_tensor(W[4], W[4], W[1], ALU.mult))
                link(nc.vector.tensor_tensor(tk[0], tk[0], tk[1], ALU.add))
                link(nc.vector.tensor_scalar(tk[0], tk[0], eps, None, ALU.add))
                link(nc.vector.reciprocal(tk[0], tk[0]))
                full = gl[:, 7, :, :]
                link(nc.vector.memset(full, 1.0))
                by_row(full[:, :, 0:E], W[4], tk[0], ALU.mult)
                hi, mid, low = (gl[:, q, :, :] for q in (1, 2, 3))
                tmp = gl[:, 4:5, :, :].rearrange("p o t e -> p (o t e)").bitcast(bf16)
                b16 = tmp[:, 0:NT * GW].rearrange("p (t e) -> p t e", e=GW)
                rest = gl[:, 5, :, :]
                link(nc.vector.tensor_copy(b16, full))
                link(nc.vector.tensor_copy(hi, b16))
                link(nc.vector.tensor_tensor(rest, full, hi, ALU.subtract))
                link(nc.vector.tensor_copy(b16, rest))
                link(nc.vector.tensor_copy(mid, b16))
                link(nc.vector.tensor_tensor(rest, rest, mid, ALU.subtract))
                link(nc.vector.tensor_copy(b16, rest))
                link(nc.vector.tensor_copy(low, b16))
                dve.sem_inc(s["copied"], 2)
                with dve.Fori(0, NB // 2) as i:
                    for j in range(2):
                        b = i * 2 + j
                        dve.wait_ge(s["tr"], b + 1)
                        carry(dve)
                        for q, v in enumerate((hi, mid, low)):
                            last = nc.vector.tensor_copy(xnt[:, j, :, q * GW:(q + 1) * GW],
                                                         v[:, bass.ds(b * TPB, TPB), :])
                        last.then_inc(s["stage"], 1)
                        dve.wait_ge(s["tr"], b + 1 + 2)
                        carry(dve)
                        nc.vector.tensor_copy(bc[0:3 * GW, bass.ds(b * L, L)], ps[3][0:3 * GW, j, :])\
                            .then_inc(s["copied"], 1)

            def take_logits(k, E):
                s = gt[k]
                dve.sem_inc(s["tk"], 2)
                with dve.Fori(0, NB // 2) as i:
                    for j in range(2):
                        b = i * 2 + j
                        dve.wait_ge(s["tm"], b + 1 + 2)
                        carry(dve)
                        src = ps[2][:, j, 0:TPB * GW].rearrange("p (t e) -> p t e", e=GW)
                        nc.vector.tensor_copy(gl[:, 0, bass.ds(b * TPB, TPB), 0:E], src[:, :, 0:E])\
                            .then_inc(s["tk"], 1)
                dve.wait_ge(s["tk"], NB + 2)

            def moe(k, units):
                s = mo[k]
                depth = DEPTH[k]
                hs, t_, hg = ring[:, 0:4, :], ring[:, 4:6, :], ring[:, 6:10, :]
                dve.sem_inc(s["gm"], 4)
                if k:
                    dve.sem_inc(s["um"], depth)
                dve.sem_inc(s["add"], 1)
                with dve.Fori(0, NB) as c:
                    for q in range(units):
                        K = c * units + q
                        dve.wait_ge(s["sil"], K + 1 + 2)
                        src = hs[:, q % depth, :]
                        if k:
                            dve.wait_ge(s["h"], K + 1)
                            nc.vector.tensor_tensor(t_[:, q % 2, :], src, ps[1][:, q % 2, :], ALU.mult)\
                                .then_inc(s["um"], 1)
                            dve.wait_ge(s["um"], K + 1 + depth)
                            src = t_[:, q % 2, :]
                        dve.wait_ge(s["gb"], c * (units // NH) + q // NH + 1)
                        dve.wait_ge(s["mm2"], K + 1)
                        nc.vector.tensor_tensor(hg[:, q % depth, :], src, ps[2][:, (q // NH) % 2, :], ALU.mult)\
                            .then_inc(s["gm"], 1)
                    dve.wait_ge(s["tr"], c + 1)
                    xb = x[:, bass.ds(c * TPB, TPB), :].rearrange("p t d -> p (t d)")
                    nc.vector.tensor_tensor(xb, xb, ps[3][:, 1, :], ALU.add).then_inc(s["add"], 1)

            moments()
            second_root(RMS_EPS)
            link(nc.vector.reciprocal(gain, r2))
            link(nc.vector.tensor_tensor(r2, r1, r2, ALU.mult))
            normalise(1, r2)
            dve.wait_ge(gt[0]["wt"], 1)
            link(nc.vector.tensor_copy(rmsT[:, :], ps[1][:, 0, 0:E0 + E0S]))
            dve.wait_ge(w_in[0], W_MOE0)
            for e in range(E0 + E0S):
                last = nc.vector.tensor_scalar(moe0_w1[:, e, :], moe0_w1[:, e, :], rmsT[:, e:e + 1], None, ALU.mult)
            barrier(dve, 6)

            take_logits(0, E0)
            link(nc.vector.tensor_tensor(gl[:, 0, :, 0:E0], gl[:, 0, :, 0:E0],
                                         gain.unsqueeze(2).to_broadcast([P, NT, E0]), ALU.mult))
            top2(0, E0, TOPK0_EPS)
            barrier(dve, 7)
            moe(0, (E0 + E0S) * NH)
            barrier(dve, 8)

            moments()
            normalise(2, r1)
            dve.sem_inc(at["add"], 1)
            with dve.Fori(0, NB) as b:
                for i in range(TPB):
                    dve.wait_ge(at["s"], b * TPB + i + 1)
                    S_ = ps[i // 2][:, i % 2, :]
                    nc.vector.tensor_tensor(S_[:, i * P:(i + 1) * P], S_[:, i * P:(i + 1) * P], cmask[:, :],
                                            ALU.add).then_inc(step, 1)
                    dve.wait_ge(step, n[0] + b * 2 * TPB + i + 1)
                    nc.vector.tensor_reduce(sm[:, 12, i:i + 1], S_[:, 0:(i + 1) * P], op=ALU.max, axis=AX.X,
                                            negate=True).then_inc(at["mx"], 1)
                for i in range(TPB):
                    dve.wait_ge(at["p"], b * TPB + i + 1)
                    nc.vector.reciprocal(sm[:, 14, i:i + 1], sm[:, 13, i:i + 1]).then_inc(step, 1)
                    dve.wait_ge(step, n[0] + b * 2 * TPB + TPB + i + 1)
                    if i == 0:
                        dve.wait_ge(at["o"], (b + 1) * TPB)
                    xb = x[:, bass.ds(b * TPB + i, 1), :].rearrange("p t d -> p (t d)")
                    nc.vector.scalar_tensor_tensor(out=xb, in0=ps[3][:, 0, i * P:(i + 1) * P],
                                                   scalar=sm[:, 14, i:i + 1], in1=xb, op0=ALU.mult,
                                                   op1=ALU.add).then_inc(at["add"], 1)
            n[0] += NB * 2 * TPB
            barrier(dve, 9)

            moments()
            second_root(LN_EPS)
            normalise(3, r1)
            dve.wait_ge(gt[1]["wt"], 1)
            link(nc.vector.tensor_copy(gwT[:, :], ps[1][:, 0, 0:E1]))
            link(nc.vector.tensor_copy(lnbr[:, :], lnsb[:, 1:2].to_broadcast([P, P])))
            dve.sem_inc(gt[1]["wc"], 1)
            dve.wait_ge(gt[1]["wt"], 2)
            link(nc.vector.tensor_copy(gconst[:, :], ps[1][:, 0, 0:E1]))
            link(nc.vector.tensor_scalar(gwT[:, :], gwT[:, :], lnsb[:, 0:1], None, ALU.mult))
            dve.sem_inc(gt[1]["wc"], 1)
            take_logits(1, E1)
            link(nc.vector.tensor_tensor(gl[:, 0, :, 0:E1], gl[:, 0, :, 0:E1],
                                         r2.unsqueeze(2).to_broadcast([P, NT, E1]), ALU.mult))
            link(nc.vector.tensor_tensor(gl[:, 0, :, 0:E1], gl[:, 0, :, 0:E1],
                                         gconst[:, :].unsqueeze(1).to_broadcast([P, NT, E1]), ALU.add))
            top2(1, E1, TOPK1_EPS)
            barrier(dve, 10)
            moe(1, NE1 * NH)
            barrier(dve, 11)

        @block.tensor
        def _(pe):
            def transposes(k, after=None):
                s = ln[k]
                pe.sem_inc(s["tr"], 2)
                with pe.Fori(0, NB // 2) as i:
                    for j in range(2):
                        b = i * 2 + j
                        pe.wait_ge(s["norm"], b + 1)
                        pe.wait_ge(s["xT"], b + 1)
                        for q in range(TPB):
                            last = nc.tensor.transpose(ps[0][:, j, q * P:(q + 1) * P], xnt[:, j, q, :], ident[:, :])
                        last.then_inc(s["tr"], 1)
                        if after:
                            after(b, j)

            def rows(b):
                return xT[:, bass.ds(b, 1), PAD:].rearrange("p o t -> p (o t)")

            pe.wait_ge(loaded, N_SMALL)
            pe.wait_ge(ident_ready, 1)
            nc.tensor.transpose(ps[1][:, 0, 0:NV], vrows[:, :], ident[0:NV, 0:NV]).then_inc(vec_done, 1)
            barrier(pe, 1)

            def conv(b, j):
                pe.wait_ge(ln[0]["xT"], b + 1 + 2)
                pe.wait_ge(pre["xm"], b + 1)
                for g in range(NG):
                    for k in range(TAPS):
                        last = nc.tensor.matmul(ps[1 + j][:, g, :], Wk[:, k, g * P:(g + 1) * P],
                                                xT[:, bass.ds(b, 1), k:k + L].rearrange("p o t -> p (o t)"),
                                                start=k == 0, stop=k == TAPS - 1)
                last.then_inc(pre["conv"], 1)

            transposes(0, conv)
            barrier(pe, 2)

            R0, R1 = 3 * BC, 3 * BC + RANK
            dtr = ring[:, 0:2, :]
            with pe.Fori(0, NB // 2) as i:
                for j in range(2):
                    b = i * 2 + j
                    pe.wait_ge(pre["split"], b + 1)
                    for g in range(NG):
                        last = nc.tensor.matmul(ps[0][0:R1, j, :], xpw[:, g, :], xm[:, g, bass.ds(b * L, L)],
                                                start=g == 0, stop=g == NG - 1)
                    last.then_inc(pre["xp"], 1)
                    pe.wait_ge(pre["dtr"], b + 1)
                    pe.wait_ge(pre["dt"], b + 1)
                    for g in range(NG):
                        last = nc.tensor.matmul(ps[1 + j][:, g, :], dtw[R0:R1, g * P:(g + 1) * P],
                                                dtr[R0:R1, j, :], start=True, stop=True)
                    last.then_inc(pre["dtp"], 1)
            barrier(pe, 3)

            hc = ring[:, 6:10, :]
            pe.sem_inc(sc["ns"], 4)

            def spread(b, n_, N):
                w = bass.ds(b * L, L)
                pe.wait_ge(sc["dbx"], N * 2 + 2)
                nc.tensor.matmul(ps[0][:, n_ % 2, :], sel[:, n_, :], bc[:, w], start=True, stop=True)\
                    .then_inc(sc["bb"], 1)
                pe.wait_ge(sc["cs"], N + 1)
                nc.tensor.matmul(ps[1][:, n_ % 2, :], sel[:, NS + n_, :], bc[:, w], start=True, stop=True)\
                    .then_inc(sc["cb"], 1)

            spread(0, 0, 0)
            with pe.Fori(0, NB) as b:
                for n_ in range(NS):
                    if n_ + 1 < NS:
                        spread(b, n_ + 1, b * NS + n_ + 1)
                    else:
                        spread(b + 1, 0, (b + 1) * NS)
                    for g in range(NG):
                        m = n_ * NG + g
                        if m == 0:
                            pe.wait_ge(sc["y"], b + 1)
                        pe.wait_ge(sc["hc"], b * (NS * NG) + m + 1 + 4)
                        nc.tensor.matmul(ps[3][:, g, :], ident[:, :], hc[:, m % 4, :], start=n_ == 0,
                                         stop=n_ == NS - 1, skip_group_check=True).then_inc(sc["ns"], 1)
            barrier(pe, 4)

            pe.sem_inc(po["tr"], 2)
            with pe.Fori(0, NB // 2) as i:
                for j in range(2):
                    b = i * 2 + j
                    pe.wait_ge(po["sz"], b + 1)
                    for g in range(NG):
                        last = nc.tensor.matmul(ps[j][:, g, :], inw[:, DI + g * P:DI + (g + 1) * P], rows(b),
                                                start=True, stop=True)
                    last.then_inc(po["z"], 1)
                    pe.wait_ge(po["gated"], b + 1 + 2)
                    pe.wait_ge(po["oc"], b + 1)
                    for g in range(NG):
                        last = nc.tensor.matmul(ps[2][:, j, :], opw[:, g, :], xm[:, g, bass.ds(b * L, L)],
                                                start=g == 0, stop=g == NG - 1)
                    last.then_inc(po["o"], 1)
                    pe.wait_ge(po["oc"], b + 1 + 2)
                    pe.wait_ge(po["add"], b + 1)
                    for q in range(TPB):
                        last = nc.tensor.transpose(ps[3][:, j, q * P:(q + 1) * P],
                                                   ring[:, 4 + j, q * P:(q + 1) * P], ident[:, :])
                    last.then_inc(po["tr"], 1)
            barrier(pe, 5)

            def router(k, w, E):
                s = gt[k]
                pe.sem_inc(s["tm"], 2)
                pe.sem_inc(s["tr"], 2)
                with pe.Fori(0, NB // 2) as i:
                    for j in range(2):
                        b = i * 2 + j
                        pe.wait_ge(s["lc"], b + 1)
                        nc.tensor.matmul(ps[1][0:E, j, :], w, rows(b), start=True, stop=True).then_inc(s["lt"], 1)
                        pe.wait_ge(s["lc"], b + 1 + 2)
                        pe.wait_ge(s["tk"], b + 1)
                        carry(pe)
                        for q in range(TPB):
                            last = nc.tensor.transpose(ps[2][:, j, q * GW:q * GW + E],
                                                       ring[0:E, j, q * P:(q + 1) * P], ident[0:E, 0:E])
                        last.then_inc(s["tm"], 1)
                with pe.Fori(0, NB // 2) as i:
                    for j in range(2):
                        b = i * 2 + j
                        pe.wait_ge(s["stage"], b + 1)
                        pe.wait_ge(s["copied"], b + 1)
                        carry(pe)
                        for q in range(TPB):
                            last = nc.tensor.transpose(ps[3][0:3 * GW, j, q * P:(q + 1) * P],
                                                       xnt[:, j, q, 0:3 * GW], ident[:, :])
                        last.then_inc(s["tr"], 1)

            def moe(k, nexp, first, second, down):
                s = mo[k]
                units = nexp * NH
                depth = DEPTH[k]
                hg = ring[:, 6:10, :]
                ya = ring[:, 10, :]
                pe.sem_inc(s["mm2"], depth)

                def hidden(c, q):
                    e, hb = q // NH, q % NH
                    K = c * units + q
                    pe.wait_ge(s["sil"], K + 1)
                    last = nc.tensor.matmul(ps[0][:, q % 2, :], first[:, e, hb * P:(hb + 1) * P], rows(c),
                                            start=True, stop=True)
                    if second is not None:
                        pe.wait_ge(s["um"], K - 1 + depth)
                        last.then_inc(s["g"], 1)
                        last = nc.tensor.matmul(ps[1][:, q % 2, :], second[:, e, hb * P:(hb + 1) * P], rows(c),
                                                start=True, stop=True)
                    last.then_inc(s["h"], 1)
                    if hb == 0:
                        E = c * nexp + e
                        pe.wait_ge(s["gm"], E * 2 + (4 if e == 0 and nexp % 2 else 2))
                        carry(pe)
                        nc.tensor.matmul(ps[2][:, e % 2, :], selg[:, e, :], bc[0:3 * GW, bass.ds(c * L, L)],
                                         start=True, stop=True).then_inc(s["gb"], 1)

                with pe.Fori(0, NB) as c:
                    hidden(c, 0)
                    hidden(c, 1)
                    for q in range(units):
                        if q + 2 < units:
                            hidden(c, q + 2)
                        if q == 0:
                            pe.wait_ge(s["acc"], c + 1)
                        pe.wait_ge(s["gm"], c * units + q + 1 + 4)
                        nc.tensor.matmul(ps[3][:, 0, :], down[:, q // NH, q % NH, :], hg[:, q % depth, :],
                                         start=q == 0, stop=q == units - 1).then_inc(s["mm2"], 1)
                    pe.wait_ge(s["acc"], c + 1 + 1)
                    pe.wait_ge(s["add"], c + 1)
                    for q in range(TPB):
                        last = nc.tensor.transpose(ps[3][:, 1, q * P:(q + 1) * P], ya[:, q * P:(q + 1) * P],
                                                   ident[:, :])
                    last.then_inc(s["tr"], 1)

            nc.tensor.transpose(ps[1][:, 0, 0:E0 + E0S], rmsr[:, :], ident[0:E0 + E0S, 0:E0 + E0S])\
                .then_inc(gt[0]["wt"], 1)
            transposes(1)
            barrier(pe, 6)
            router(0, wr[:, :], E0)
            barrier(pe, 7)
            pe.wait_ge(w_in[0], W_MOE0)
            moe(0, E0 + E0S, moe0_w1, None, moe0_w2)
            barrier(pe, 8)

            transposes(2)
            qkv = ring[:, 0:3, :]
            vs = ring[:, 3, :]
            pr = ring[:, 4:8, :]
            pt = ring[:, 8:10, :]
            pe.wait_ge(ln[2]["xT"], NB + 2)
            with pe.Fori(0, NB) as b:
                pe.wait_ge(at["pts"], b * TPB + 1)
                pe.wait_ge(at["add"], b * TPB + 1)
                for k, bank in enumerate((ps[2][0:KD, 0, :], ps[2][0:KD, 1, :], ps[3][0:KD, 0, :])):
                    last = nc.tensor.matmul(bank, wqk[:, k, :], rows(b), start=True, stop=True)
                last.then_inc(at["qkv"], 1)
                pe.wait_ge(at["qkvs"], b + 1)
                for i in range(TPB):
                    nc.tensor.matmul(ps[i // 2][:, i % 2, 0:(i + 1) * P], qkv[0:KD, 0, i * P:(i + 1) * P],
                                     qkv[0:KD, 1, 0:(i + 1) * P], start=True, stop=True).then_inc(at["s"], 1)
                for i in range(TPB):
                    last = nc.tensor.matmul(ps[3][:, 1, i * P:(i + 1) * P], qkv[0:KD, 2, i * P:(i + 1) * P],
                                            wv2[:, :], start=True, stop=True)
                last.then_inc(at["v"], 1)
                for i in range(TPB):
                    pe.wait_ge(at["p"], b * TPB + i + 1)
                    if i >= 2:
                        pe.wait_ge(at["pts"], b * TPB + i - 1 + 1)
                    for k in range(i + 1):
                        last = nc.tensor.transpose(ps[2][:, i % 2, k * P:(k + 1) * P],
                                                   pr[:, i, k * P:(k + 1) * P], ident[:, :])
                    last.then_inc(at["pt"], 1)
                    pe.wait_ge(at["pts"], b * TPB + i + 1 + 1)
                    if i == 0:
                        pe.wait_ge(at["vs"], b + 1)
                    for k in range(i + 1):
                        last = nc.tensor.matmul(ps[3][:, 0, i * P:(i + 1) * P], pt[:, i % 2, k * P:(k + 1) * P],
                                                vs[:, k * P:(k + 1) * P], start=k == 0, stop=k == i)
                    last.then_inc(at["o"], 1)
            barrier(pe, 9)

            nc.tensor.transpose(ps[1][:, 0, 0:E1], gwr[:, :], ident[0:E1, 0:E1]).then_inc(gt[1]["wt"], 1)
            transposes(3)
            pe.wait_ge(gt[1]["wc"], 1)
            nc.tensor.matmul(ps[1][:, 0, 0:E1], lnbr[:, :], gwT[:, :], start=True, stop=True)\
                .then_inc(gt[1]["wt"], 1)
            pe.wait_ge(gt[1]["wc"], 2)
            pe.wait_ge(ln[3]["xT"], NB + 2)
            router(1, gwT[:, :], E1)
            barrier(pe, 10)
            pe.wait_ge(w_in[1], W_MOE1)
            moe(1, NE1, moe1_wg, moe1_wu, moe1_wd)
            barrier(pe, 11)


_IN_ORDER = ['L0_attn_x', 'L0_attn_ln_w', 'L0_attn_ln_b', 'L0_attn_in_proj_w', 'L0_attn_conv_w', 'L0_attn_conv_b',
             'L0_attn_x_proj_w', 'L0_attn_dt_proj_w', 'L0_attn_dt_proj_b', 'L0_attn_A_log', 'L0_attn_D_param',
             'L0_attn_out_proj_w', 'L0_attn_res_scale', 'L0_ffn_router_w', 'L0_ffn_rms_w', 'L0_ffn_w1', 'L0_ffn_w2',
             'L0_ffn_rms_w_s', 'L0_ffn_w1_s', 'L0_ffn_w2_s', 'L1_attn_w_q', 'L1_attn_w_k', 'L1_attn_w_v1',
             'L1_attn_w_v2', 'L1_ffn_ln_scale', 'L1_ffn_ln_bias', 'L1_ffn_gate_w', 'L1_ffn_Wg', 'L1_ffn_Wu',
             'L1_ffn_Wd', 'L1_ffn_sWg', 'L1_ffn_sWu', 'L1_ffn_sWd']


def kernel(**inputs):
    import numpy as np
    import concourse.bacc as bacc
    from concourse.bass_utils import run_bass_kernel_spmd

    nc = bacc.Bacc("TRN2", target_bir_lowering=False, num_devices=1)
    arrays, args = {}, {}
    for name in _IN_ORDER:
        a = np.ascontiguousarray(inputs[name])
        arrays[f"in_{name}"] = a
        args[name] = nc.dram_tensor(f"in_{name}", a.shape, mybir.dt.from_np(a.dtype), kind="ExternalInput").ap()
    shape = arrays["in_L0_attn_x"].shape
    out = nc.dram_tensor("out_x", shape, mybir.dt.float32, kind="ExternalOutput").ap()
    mamba_moe_attention_moe_kernel(nc, args, out)
    r = run_bass_kernel_spmd(nc, [arrays], core_ids=[0])
    return r.results[0]["out_x"]
```

```python
import concourse.bass as bass
from concourse import mybir
from contextlib import ExitStack


def mamba_moe_attention_moe_kernel(nc: bass.Bass, A: dict, out: bass.AP):
    f32 = mybir.dt.float32
    bf16 = mybir.dt.bfloat16
    ALU = mybir.AluOpType
    ACT = mybir.ActivationFunctionType
    AX = mybir.AxisListType

    P = 128
    NB, L, D = A["L0_attn_x"].shape
    TPB = L // P
    NT = NB * TPB
    NTOK = NB * L
    DI = A["L0_attn_D_param"].shape[0]
    NG = DI // P
    TAPS = A["L0_attn_conv_w"].shape[1]
    PAD = TAPS - 1
    NS = A["L0_attn_A_log"].shape[1]
    RANK = A["L0_attn_dt_proj_w"].shape[0]
    BC = 2 * NS
    E0 = A["L0_ffn_router_w"].shape[1]
    E0S = A["L0_ffn_w1_s"].shape[0]
    E1 = A["L1_ffn_gate_w"].shape[0]
    HID = A["L0_ffn_w1"].shape[2]
    NH = HID // P
    KD = A["L1_attn_w_q"].shape[1]
    GW = 16
    LN_EPS = 1e-5
    RMS_EPS = 1.1920929e-07
    TOPK0_EPS = 1e-9
    TOPK1_EPS = 1e-5
    NEG = -1e30

    ctx = ExitStack()
    with ctx:
        def sb(name, shape, dt=f32):
            return ctx.enter_context(nc.sbuf_tensor(name, shape, dt))

        def sem(name):
            return ctx.enter_context(nc.semaphore(name))

        x = sb("x", [P, NT, D])
        xT = sb("xT", [P, NB, PAD + L])
        big1 = sb("big1", [P, NG, NTOK])
        big2 = sb("big2", [P, NG, NTOK])
        big3 = sb("big3", [P, NG, NTOK])
        dt, u, xm = big1, big2, big3
        bc = sb("bc", [3 * BC, NTOK + L], bf16)
        sel = sb("sel", [3 * BC, BC, P], bf16)
        selg = sb("selg", [3 * GW, GW, P], bf16)
        ident = sb("ident", [P, P])
        cmask = sb("cmask", [P, P])
        Wk = sb("Wk", [P, TAPS, DI])
        inw = sb("inw", [P, 2 * DI])
        xpw = sb("xpw", [P, NG, 3 * BC + RANK])
        dtw = sb("dtw", [3 * BC + RANK, DI])
        opw = sb("opw", [P, NG, D])
        cols = sb("cols", [P, 16])
        Aneg = sb("Aneg", [P, NG, NS])
        ring = sb("ring", [P, 20, L])
        cwb = ring[:, 0:DI * TAPS // L, :].rearrange("p r t -> p (r t)").rearrange("p (c k) -> p c k", k=TAPS)
        xnt = ring[:, 18:20, :].rearrange("p j (q d) -> p j q d", d=D)
        stats = sb("stats", [P, NT, 6])
        sm = sb("sm", [P, 16, NT])
        gl = big3[:, 0, 0:8 * NT * GW].rearrange("p (q t e) -> p q t e", t=NT, e=GW)
        iot = sb("iot", [P, NT, GW])
        wr = sb("wr", [P, E0])
        gwT = sb("gwT", [P, E1])
        gwr = sb("gwr", [E1, P])
        vrows = sb("vrows", [10, P])
        rs_sb = sb("rs_sb", [P, 1])
        lnbr = sb("lnbr", [P, P])
        gconst = sb("gconst", [P, E1])
        rmsT = sb("rmsT", [P, E0 + E0S])
        rmsr = sb("rmsr", [E0 + E0S, P])
        wqk = sb("wqk", [P, 3, KD])
        wv2 = sb("wv2", [KD, D])
        ps = [ctx.enter_context(nc.psum_tensor(f"ps{i}", [P, 2, L], f32)) for i in range(4)]

        lnw, lnb = cols[:, 0:1], cols[:, 1:2]
        convb = cols[:, 2:2 + NG]
        dtb = cols[:, 4:4 + NG]
        Dp = cols[:, 6:6 + NG]
        lnsb = cols[:, 8:10]
        rs = rs_sb[:, :]
        NV = 10

        mu, var, r1, r2, t0, t1, t2, t3, gain, shift = (sm[:, k, :] for k in range(10))
        root = sm[:, 10, :]
        rl = sm[:, 11, :]

        loaded = sem("loaded")
        ident_ready = sem("ident_ready")
        consts_ready = sem("consts_ready")
        carried = sem("carried")
        vec_done = sem("vec_done")
        x_in = sem("x_in")
        w_in = [sem(f"w_in{k}") for k in range(2)]
        stored = sem("stored")
        step = sem("step")
        step_act = sem("step_act")
        step_pool = sem("step_pool")
        phase_done = sem("phase_done")
        rs_in = sem("rs_in")
        rs_out = sem("rs_out")

        def sems(prefix, names):
            return {n: sem(f"{prefix}_{n}") for n in names.split()}

        ln = [sems(f"ln{k}", "norm tr xT") for k in range(4)]
        pre = sems("pre", "conv xm xp dtr parts split dtp absd soft dsum dt u")
        sc = sems("sc", "bb cb cs da dbx scan hc ns y")
        po = sems("po", "z sz gated o oc tr add")
        gt = [sems(f"gt{k}", "wt wc lt lc tm tk logit stage tr copied") for k in range(2)]
        mo = [sems(f"mo{k}", "g h sil um gb gm mm2 acc tr add") for k in range(2)]
        at = sems("at", "even odd even_out odd_out s masked mx p pt pts rd o add")

        DEPTH = (4, 3)
        block = ctx.enter_context(nc.Block())

        x_d = A["L0_attn_x"].rearrange("b (k p) d -> p (b k) d", p=P)
        out_d = out.rearrange("b (k p) d -> p (b k) d", p=P)

        moe0_w1 = big1[:, 0, :].rearrange("p (e h) -> p e h", h=HID)
        moe0_w2 = big1[:, 1, :].rearrange("p (e b d) -> p e b d", b=NH, d=D)
        NE1 = E1 + 1
        b2 = big2[:, :, :].rearrange("p g t -> p (g t)")
        moe1_wg = b2[:, 0:NE1 * HID].rearrange("p (e h) -> p e h", h=HID)
        moe1_wu = b2[:, NE1 * HID:2 * NE1 * HID].rearrange("p (e h) -> p e h", h=HID)
        moe1_wd = b2[:, 2 * NE1 * HID:3 * NE1 * HID].rearrange("p (e b d) -> p e b d", b=NH, d=D)

        smalls = []

        def vec(name):
            return A[name].rearrange("(g p) -> g p", p=P)

        smalls += [(vrows[0:1, :], vec("L0_attn_ln_w")), (vrows[1:2, :], vec("L0_attn_ln_b")),
                   (vrows[2:2 + NG, :], vec("L0_attn_conv_b")), (vrows[4:4 + NG, :], vec("L0_attn_dt_proj_b")),
                   (vrows[6:6 + NG, :], vec("L0_attn_D_param")),
                   (vrows[8:9, :], vec("L1_ffn_ln_scale")), (vrows[9:10, :], vec("L1_ffn_ln_bias")),
                   (rs, A["L0_attn_res_scale"].rearrange("(a o) -> a o", a=1).to_broadcast([P, 1])),
                   (inw[:, :], A["L0_attn_in_proj_w"]),
                   (cwb[:, :, :].rearrange("p c k -> p (c k)"),
                    A["L0_attn_conv_w"].rearrange("(a c) k -> a (c k)", a=1).to_broadcast([P, DI * TAPS])),
                   (Aneg[:, :, :], A["L0_attn_A_log"].rearrange("(g p) n -> p g n", p=P)),
                   (opw[:, :, :], A["L0_attn_out_proj_w"].rearrange("(g p) n -> p g n", p=P)),
                   (dtw[3 * BC:3 * BC + RANK, :], A["L0_attn_dt_proj_w"]),
                   (wr[:, :], A["L0_ffn_router_w"]),
                   (gwr[:, :], A["L1_ffn_gate_w"]),
                   (rmsr[0:E0, :], A["L0_ffn_rms_w"]), (rmsr[E0:E0 + E0S, :], A["L0_ffn_rms_w_s"]),
                   (wqk[:, 0, :], A["L1_attn_w_q"]), (wqk[:, 1, :], A["L1_attn_w_k"]),
                   (wqk[:, 2, :], A["L1_attn_w_v1"]), (wv2[:, :], A["L1_attn_w_v2"])]
        xpw_d = A["L0_attn_x_proj_w"].rearrange("(g p) n -> p g n", p=P)
        smalls += [(xpw[:, :, k * BC:(k + 1) * BC], xpw_d[:, :, RANK:RANK + BC]) for k in range(3)]
        smalls += [(xpw[:, :, 3 * BC:], xpw_d[:, :, 0:RANK])]

        def barrier(eng, n):
            eng.drain().then_inc(phase_done, 1)
            eng.wait_ge(phase_done, 3 * n)

        def skewed(eng, ahead, behind):
            ahead(0, 0)
            with eng.Fori(0, NB // 2 - 1) as i:
                for j in range(2):
                    b = i * 2 + j
                    ahead(b + 1, 1 - j)
                    behind(b, j)
            ahead(NB - 1, 1)
            behind(NB - 2, 0)
            behind(NB - 1, 1)

        def carry(eng):
            eng.sem_inc(carried, 1)

        qkv = [ring[:, 3 * j:3 * j + 3, :] for j in range(2)]
        vs = [ring[:, 6 + j, :] for j in range(2)]
        pr = [ring[:, 8 + 4 * j:12 + 4 * j, :] for j in range(2)]
        pt = ring[:, 16:18, :]

        @block.sync
        def _(sp):
            sp.dma_start(x[:, :, :], x_d).then_inc(x_in, 16)
            for dst, src in smalls:
                sp.dma_start(dst, src).then_inc(loaded, 16)
            sp.wait_ge(phase_done, 3 * 4)
            for dst, src in ((moe0_w1[:, 0:E0, :], A["L0_ffn_w1"].rearrange("e d h -> d e h")),
                             (moe0_w1[:, E0:, :], A["L0_ffn_w1_s"].rearrange("e d h -> d e h"))):
                sp.dma_start(dst, src).then_inc(w_in[0], 16)
            for dst, src in ((moe0_w2[:, 0:E0, :, :], A["L0_ffn_w2"].rearrange("e (b p) d -> p e b d", p=P)),
                             (moe0_w2[:, E0:, :, :], A["L0_ffn_w2_s"].rearrange("e (b p) d -> p e b d", p=P))):
                for e in range(dst.shape[1]):
                    sp.dma_start(dst[:, e, :, :], src[:, e, :, :]).then_inc(w_in[0], 16)
            for w, a, s in ((moe1_wg, "L1_ffn_Wg", "L1_ffn_sWg"), (moe1_wu, "L1_ffn_Wu", "L1_ffn_sWu")):
                sp.dma_start(w[:, 0:E1, :], A[a].rearrange("e d h -> d e h")).then_inc(w_in[1], 16)
                sp.dma_start(w[:, E1, :], A[s]).then_inc(w_in[1], 16)
            wd = A["L1_ffn_Wd"].rearrange("e (b p) d -> p e b d", p=P)
            for e in range(E1):
                sp.dma_start(moe1_wd[:, e, :, :], wd[:, e, :, :]).then_inc(w_in[1], 16)
            sp.dma_start(moe1_wd[:, E1, :, :], A["L1_ffn_sWd"].rearrange("(b p) d -> p b d", p=P)).then_inc(w_in[1], 16)
            sp.wait_ge(phase_done, 3 * 11)
            sp.dma_start(out_d, x[:, :, :]).then_inc(stored, 16)
            sp.wait_ge(stored, 16)

        W_MOE0 = 16 * (2 + E0 + E0S)
        W_MOE1 = 16 * (4 + E1 + 1)
        N_SMALL = 16 * len(smalls)

        @block.gpsimd
        def _(pool):
            n = [0]

            def link(ins):
                n[0] += 1
                ins.then_inc(step_pool, 1)
                pool.wait_ge(step_pool, n[0])

            link(nc.gpsimd.memset(ident[:, :], 0.0))
            link(nc.gpsimd.affine_select(out=ident[:, :], in_=ident[:, :], compare_op=ALU.not_equal, fill=1.0,
                                         base=0, pattern=[[-1, P]], channel_multiplier=1))
            link(nc.gpsimd.memset(xT[:, :, 0:PAD], 0.0))
            pool.sem_inc(ident_ready, 1)
            link(nc.gpsimd.memset(bc[:, NTOK:], 0.0))
            link(nc.gpsimd.memset(sel[:, :, :], 0.0))
            for k in range(3):
                link(nc.gpsimd.affine_select(out=sel[:, :, :], in_=sel[:, :, :], compare_op=ALU.not_equal, fill=1.0,
                                             base=-k * BC, pattern=[[-1, BC], [0, P]], channel_multiplier=1))
            link(nc.gpsimd.memset(selg[:, :, :], 0.0))
            for k in range(3):
                link(nc.gpsimd.affine_select(out=selg[:, :, :], in_=selg[:, :, :], compare_op=ALU.not_equal,
                                             fill=1.0, base=-k * GW, pattern=[[-1, GW], [0, P]],
                                             channel_multiplier=1))
            link(nc.gpsimd.memset(cmask[:, :], 0.0))
            link(nc.gpsimd.affine_select(out=cmask[:, :], in_=cmask[:, :], compare_op=ALU.is_ge, fill=NEG,
                                         base=0, pattern=[[-1, P]], channel_multiplier=1))
            link(nc.gpsimd.iota(iot[:, :, :], pattern=[[0, NT], [-1, GW]], base=GW, channel_multiplier=0,
                                allow_small_or_imprecise_dtypes=True))
            pool.sem_inc(consts_ready, 1)

            with pool.Fori(0, NB) as b:
                pool.wait_ge(pre["dt"], b + 1 + 2)
                w = bass.ds(b * L, L)
                nc.gpsimd.tensor_tensor(u[:, :, w], dt[:, :, w], xm[:, :, w], ALU.mult).then_inc(pre["u"], 1)

            h, hc, cs = ring[:, 0:4, :], ring[:, 4:12, :], ring[:, 12:16, :]
            pool.sem_inc(sc["hc"], 8)
            with pool.Fori(0, NB) as b:
                for n_ in range(NS):
                    for g in range(NG):
                        m = n_ * NG + g
                        M = b * (NS * NG) + m
                        pool.wait_ge(sc["scan"], M + 1 + 2)
                        if g == 0:
                            pool.wait_ge(sc["cs"], b * NS + n_ + 1 + 1)
                        pool.wait_ge(sc["ns"], M + 1)
                        nc.gpsimd.tensor_tensor(hc[:, m % 8, :], h[:, m % 4, :], cs[:, n_ % 4, :],
                                                ALU.mult).then_inc(sc["hc"], 1)

        @block.scalar
        def _(act):
            n = [0]

            def link(ins):
                n[0] += 1
                ins.then_inc(step_act, 1)
                act.wait_ge(step_act, n[0])

            roots = [0]

            def inverse_root():
                roots[0] += 1
                act.wait_ge(rs_in, roots[0])
                link(nc.scalar.activation(rl, t0, ACT.Ln))
                nc.scalar.activation(root, rl, ACT.Exp, scale=-0.5).then_inc(rs_out, 1)

            def evacuate(k, scale=None, bias=None):
                s = ln[k]
                act.sem_inc(s["xT"], 2)

                def one(b, j):
                    act.wait_ge(s["tr"], b + 1 + 2)
                    carry(act)
                    dst = xT[:, bass.ds(b, 1), PAD:].rearrange("p o t -> p (o t)")
                    if scale is None:
                        nc.scalar.activation(dst, ps[0][:, j, :], ACT.Copy).then_inc(s["xT"], 1)
                    else:
                        nc.scalar.activation(dst, ps[0][:, j, :], ACT.Identity, scale=scale,
                                             bias=bias).then_inc(s["xT"], 1)

                return one

            def pairs(one):
                with act.Fori(0, NB // 2) as i:
                    for j in range(2):
                        one(i * 2 + j, j)

            nc.scalar.preload_act_table_set("natural_log_exp_and_others")
            act.wait_ge(loaded, N_SMALL)
            link(nc.scalar.activation(Aneg[:, :, :], Aneg[:, :, :], ACT.Exp))
            link(nc.scalar.mul(Aneg[:, :, :], Aneg[:, :, :], -1.0))
            inverse_root()
            inverse_root()
            barrier(act, 1)

            nc.scalar.preload_act_table(ACT.Silu)
            act.sem_inc(pre["xm"], 2)

            def silu_conv(b, j):
                act.wait_ge(pre["conv"], b + 1)
                carry(act)
                for g in range(NG):
                    last = nc.scalar.activation(xm[:, g, bass.ds(b * L, L)], ps[1 + j][:, g, :], ACT.Silu,
                                                bias=convb[:, g:g + 1])
                last.then_inc(pre["xm"], 1)

            skewed(act, evacuate(0, lnw, lnb), silu_conv)
            barrier(act, 2)

            dtr = ring[:, 0:2, :]
            av = ring[:, 10:14, :]
            lt = ring[:, 4:8, :]
            nc.scalar.preload_act_table_set("natural_log_exp_and_others")

            def copy_dt(b, j):
                act.wait_ge(pre["xp"], b + 1)
                nc.scalar.activation(dtr[3 * BC:3 * BC + RANK, j, :], ps[0][3 * BC:3 * BC + RANK, j, :],
                                     ACT.Copy).then_inc(pre["dtr"], 1)

            def softplus(b, j):
                act.wait_ge(pre["dtp"], b + 1)
                act.wait_ge(pre["dt"], b + 1)
                a = av[:, 2 * j:2 * j + 2, :]
                for g in range(NG):
                    last = nc.scalar.activation(a[:, g, :], ps[1 + j][:, g, :], ACT.Abs, bias=dtb[:, g:g + 1])
                last.then_inc(pre["absd"], 1)
                act.wait_ge(pre["absd"], b * 2 + 1)
                nc.scalar.activation(a, a, ACT.Exp, scale=-1.0).then_inc(pre["absd"], 1)
                act.wait_ge(pre["absd"], b * 2 + 2)
                nc.scalar.activation(lt[:, 2 * j:2 * j + 2, :], a, ACT.Ln, bias=1.0)\
                    .then_inc(pre["soft"], 1)

            skewed(act, copy_dt, softplus)
            barrier(act, 3)

            act.sem_inc(sc["cs"], 1)
            cs = ring[:, 12:16, :]
            with act.Fori(0, NB) as b:
                for n_ in range(NS):
                    N = b * NS + n_
                    act.wait_ge(sc["cb"], N + 1)
                    act.wait_ge(sc["hc"], N * 2 + 2)
                    nc.scalar.activation(cs[:, n_ % 4, :], ps[1][:, 0, :], ACT.Copy).then_inc(sc["cs"], 1)
                    for g in range(NG):
                        M = b * (NS * NG) + n_ * NG + g
                        act.wait_ge(sc["scan"], M + 1)
                        carry(act)
                        nc.scalar.activation(ps[2][:, g, :], dt[:, g, bass.ds(b * L, L)], ACT.Exp,
                                             scale=Aneg[:, g, n_:n_ + 1]).then_inc(sc["da"], 1)
            barrier(act, 4)

            sz = ring[:, 0:4, :]
            act.sem_inc(po["sz"], 2)
            act.sem_inc(po["oc"], 2)
            nc.scalar.preload_act_table(ACT.Silu)

            def silu_z(b, j):
                act.wait_ge(po["z"], b + 1)
                act.wait_ge(po["gated"], b + 1)
                nc.scalar.activation(sz[:, 2 * j:2 * j + 2, :], ps[j][:, :, :], ACT.Silu).then_inc(po["sz"], 1)

            def copy_o(b, j):
                act.wait_ge(po["o"], b + 1)
                act.wait_ge(po["tr"], b + 1)
                nc.scalar.activation(ring[:, 4 + j, :], ps[2][:, j, :], ACT.Copy).then_inc(po["oc"], 1)

            skewed(act, silu_z, copy_o)
            barrier(act, 5)

            def gates(k, E):
                s = gt[k]
                act.sem_inc(s["lc"], 2)
                with act.Fori(0, NB // 2) as i:
                    for j in range(2):
                        b = i * 2 + j
                        act.wait_ge(s["lt"], b + 1)
                        act.wait_ge(s["tm"], b + 1)
                        nc.scalar.activation(ring[0:E, j, :], ps[1][0:E, j, :], ACT.Copy).then_inc(s["lc"], 1)
                act.wait_ge(s["logit"], 1)
                nc.scalar.activation(gl[:, 1, :, 0:E], gl[:, 0, :, 0:E], ACT.Exp).then_inc(s["logit"], 1)

            def moe(k, units):
                s = mo[k]
                depth = DEPTH[k]
                hs = ring[:, 0:4, :]
                ya = ring[:, 10, :]
                nc.scalar.preload_act_table(ACT.Silu)
                act.sem_inc(s["sil"], 2)
                act.sem_inc(s["acc"], 1)
                with act.Fori(0, NB) as c:
                    for q in range(units):
                        K = c * units + q
                        act.wait_ge(s["g"] if k else s["h"], K + 1)
                        act.wait_ge(s["um"] if k else s["gm"], K + 1)
                        nc.scalar.activation(hs[:, q % depth, :], ps[0][:, q % 2, :], ACT.Silu).then_inc(s["sil"], 1)
                    act.wait_ge(s["mm2"], (c + 1) * units + depth)
                    nc.scalar.activation(ya, ps[3][:, 0, :], ACT.Copy).then_inc(s["acc"], 1)

            nc.scalar.preload_act_table_set("natural_log_exp_and_others")
            inverse_root()
            inverse_root()
            pairs(evacuate(1))
            barrier(act, 6)
            gates(0, E0)
            barrier(act, 7)
            moe(0, (E0 + E0S) * NH)
            barrier(act, 8)

            nc.scalar.preload_act_table_set("natural_log_exp_and_others")
            inverse_root()
            pairs(evacuate(2))
            act.sem_inc(at["even_out"], 1)
            act.sem_inc(at["pts"], 1)

            def evac_even(b, j, r):
                act.wait_ge(at["even"], b * 2 + r + 1)
                nc.scalar.activation(qkv[j][0:KD, 2 * r, :], ps[3][0:KD, 0, :], ACT.Copy,
                                     scale=1.0 if r else float(KD) ** -0.5).then_inc(at["even_out"], 1)

            def exps(b, j, i):
                act.wait_ge(at["mx"], b * TPB + i + 1)
                W = (i + 1) * P
                q = j * TPB + i
                nc.scalar.activation(pr[j][:, i, 0:W], ps[i // 2][:, i % 2, 0:W], ACT.Exp,
                                     bias=sm[:, 12, q:q + 1], accum_out=sm[:, 13, q:q + 1]).then_inc(at["p"], 1)

            def copy_pt(b, i):
                act.wait_ge(at["pt"], b * TPB + i + 1)
                W = (i + 1) * P
                nc.scalar.activation(pt[:, i % 2, 0:W], ps[2][:, 0, 0:W], ACT.Copy).then_inc(at["pts"], 1)

            def attend(b, j, scores, loads):
                for i in range(TPB):
                    copy_pt(b, i)
                    if loads and i == 0:
                        evac_even(b + 2, j, 0)
                    if loads and i == 2:
                        evac_even(b + 2, j, 1)
                    if scores:
                        exps(b + 1, 1 - j, i)

            for b in range(2):
                evac_even(b, b, 0)
                evac_even(b, b, 1)
            for i in range(TPB):
                exps(0, 0, i)
            with act.Fori(0, NB // 2 - 1) as h_:
                for j in range(2):
                    attend(h_ * 2 + j, j, True, True)
            attend(NB - 2, 0, True, False)
            attend(NB - 1, 1, False, False)
            barrier(act, 9)

            inverse_root()
            inverse_root()
            pairs(evacuate(3))
            gates(1, E1)
            barrier(act, 10)
            moe(1, NE1 * NH)
            barrier(act, 11)

        @block.vector
        def _(dve):
            n = [0]

            def link(ins):
                n[0] += 1
                ins.then_inc(step, 1)
                dve.wait_ge(step, n[0])

            roots = [0]

            def inverse_root(dst, z):
                link(nc.vector.tensor_copy(t0, z))
                roots[0] += 1
                dve.sem_inc(rs_in, 1)
                dve.wait_ge(rs_out, roots[0])
                link(nc.vector.tensor_tensor(t1, root, root, ALU.mult))
                link(nc.vector.tensor_tensor(t1, t1, t0, ALU.mult))
                link(nc.vector.tensor_scalar(t1, t1, -0.5, 1.5, ALU.mult, ALU.add))
                link(nc.vector.tensor_tensor(dst, root, t1, ALU.mult))

            def batch_stats(b):
                for k in range(TPB):
                    t = b * TPB + k
                    nc.vector.bn_stats(stats[:, bass.ds(t, 1), :].rearrange("p o s -> p (o s)"),
                                       x[:, bass.ds(t, 1), :].rearrange("p o d -> p (o d)"))

            def moments():
                me, ve, mo_, vo = stats[:, :, 1], stats[:, :, 2], stats[:, :, 4], stats[:, :, 5]
                link(nc.vector.tensor_tensor(t0, me, mo_, ALU.add))
                link(nc.vector.tensor_scalar(mu, t0, 0.5, None, ALU.mult))
                link(nc.vector.tensor_tensor(t1, me, mo_, ALU.subtract))
                link(nc.vector.tensor_tensor(t1, t1, t1, ALU.mult))
                link(nc.vector.tensor_tensor(t2, ve, vo, ALU.add))
                link(nc.vector.scalar_tensor_tensor(out=var, in0=t1, scalar=D / 4.0, in1=t2, op0=ALU.mult,
                                                    op1=ALU.add))
                link(nc.vector.tensor_scalar(var, var, 1.0 / D, None, ALU.mult))
                link(nc.vector.tensor_scalar(t3, var, LN_EPS, None, ALU.add))
                inverse_root(r1, t3)

            def second_root(eps):
                link(nc.vector.tensor_tensor(t3, r1, r1, ALU.mult))
                link(nc.vector.tensor_tensor(t3, t3, var, ALU.mult))
                link(nc.vector.tensor_scalar(t3, t3, eps, None, ALU.add))
                inverse_root(r2, t3)

            def normalise(k, scale):
                s = ln[k]
                with dve.Fori(0, NB // 2) as i:
                    for j in range(2):
                        b = i * 2 + j
                        dve.wait_ge(s["tr"], b + 1)
                        for q in range(TPB):
                            t = b * TPB + q
                            last = nc.vector.tensor_scalar(
                                xnt[:, j, q, :], x[:, bass.ds(t, 1), :].rearrange("p o d -> p (o d)"),
                                mu[:, bass.ds(t, 1)], scale[:, bass.ds(t, 1)], ALU.subtract, ALU.mult)
                        last.then_inc(s["norm"], 1)
                        if k == 0:
                            for q in range(TPB):
                                t = b * TPB + q
                                xt = x[:, bass.ds(t, 1), :].rearrange("p o d -> p (o d)")
                                nc.vector.tensor_scalar(xt, xt, gain[:, bass.ds(t, 1)], shift[:, bass.ds(t, 1)],
                                                        ALU.mult, ALU.add)

            dve.wait_ge(x_in, 16)
            with dve.Fori(0, NB) as b:
                batch_stats(b)
            dve.wait_ge(vec_done, 1)
            nc.vector.tensor_copy(cols[:, 0:NV], ps[1][:, 0, 0:NV])
            dve.wait_ge(loaded, N_SMALL)
            for k in range(TAPS):
                link(nc.vector.tensor_tensor(Wk[:, k, :], inw[:, 0:DI], cwb[:, :, k], ALU.mult))
            dve.drain()
            moments()
            second_root(LN_EPS)
            link(nc.vector.tensor_tensor(r2, r1, r2, ALU.mult))
            link(nc.vector.tensor_scalar(gain, r1, 1.0, None, ALU.add))
            link(nc.vector.scalar_tensor_tensor(out=shift, in0=mu, scalar=-1.0, in1=r1, op0=ALU.mult, op1=ALU.mult))
            barrier(dve, 1)

            normalise(0, r2)
            barrier(dve, 2)

            part = ring[:, 8, :]
            lt = ring[:, 4:8, :]
            dve.sem_inc(pre["split"], 2)
            dve.sem_inc(pre["dt"], 2)
            B3, B2 = 3 * BC, 2 * BC

            def split(b, j):
                w = bass.ds(b * L, L)
                dve.wait_ge(pre["xp"], b + 1)
                carry(dve)
                nc.vector.tensor_copy(bc[0:B3, w], ps[0][0:B3, j, :]).then_inc(pre["parts"], 1)
                dve.wait_ge(pre["parts"], b * 4 + 1)
                nc.vector.tensor_tensor(part[0:B3, :], ps[0][0:B3, j, :], bc[0:B3, w], ALU.subtract)\
                    .then_inc(pre["parts"], 1)
                dve.wait_ge(pre["parts"], b * 4 + 2)
                carry(dve)
                nc.vector.tensor_copy(bc[BC:B2, w], part[BC:B2, :])
                nc.vector.tensor_copy(bc[B2:B3, w], part[B2:B3, :]).then_inc(pre["parts"], 1)
                dve.wait_ge(pre["parts"], b * 4 + 3)
                nc.vector.tensor_tensor(part[B2:B3, :], part[B2:B3, :], bc[B2:B3, w], ALU.subtract)\
                    .then_inc(pre["parts"], 1)
                dve.wait_ge(pre["parts"], b * 4 + 4)
                carry(dve)
                nc.vector.tensor_copy(bc[B2:B3, w], part[B2:B3, :]).then_inc(pre["split"], 1)

            def soft_dt(b, j):
                w = bass.ds(b * L, L)
                dve.wait_ge(pre["soft"], b + 1)
                for g in range(NG):
                    last = nc.vector.scalar_tensor_tensor(out=dt[:, g, w], in0=ps[1 + j][:, g, :],
                                                          scalar=dtb[:, g:g + 1], in1=lt[:, 2 * j + g, :],
                                                          op0=ALU.add, op1=ALU.add)
                last.then_inc(pre["dsum"], 1)
                dve.wait_ge(pre["dsum"], b + 1)
                nc.vector.tensor_tensor(dt[:, :, w], dt[:, :, w], lt[:, 2 * j:2 * j + 2, :], ALU.max)\
                    .then_inc(pre["dt"], 1)

            skewed(dve, split, soft_dt)
            barrier(dve, 3)

            dbx, h = ring[:, 16:20, :], ring[:, 0:4, :]
            dve.wait_ge(pre["u"], NB)
            dve.sem_inc(sc["dbx"], 4)
            dve.sem_inc(sc["scan"], 2)
            dve.sem_inc(sc["y"], 1)

            def add_skip(b):
                dve.wait_ge(sc["ns"], (b + 1) * (NS * NG) + 8)
                for g in range(NG):
                    w = bass.ds(b * L, L)
                    last = nc.vector.scalar_tensor_tensor(out=xm[:, g, w], in0=xm[:, g, w], scalar=Dp[:, g:g + 1],
                                                          in1=ps[3][:, g, :], op0=ALU.mult, op1=ALU.add)
                last.then_inc(sc["y"], 1)

            def scan_batch(b, first):
                def input_term(m):
                    n_, g = m // NG, m % NG
                    if g == 0:
                        dve.wait_ge(sc["bb"], b * NS + n_ + 1)
                    if not first or m:
                        dve.wait_ge(sc["scan"], b * (NS * NG) + m)
                    nc.vector.tensor_tensor(dbx[:, m % 4, :], u[:, g, bass.ds(b * L, L)], ps[0][:, n_ % 2, :],
                                            ALU.mult).then_inc(sc["dbx"], 1)

                input_term(0)
                for m in range(NS * NG):
                    M = b * (NS * NG) + m
                    if m == 3 and not first:
                        add_skip(b - 1)
                    if m + 1 < NS * NG:
                        input_term(m + 1)
                    dve.wait_ge(sc["dbx"], M + 1 + 4)
                    dve.wait_ge(sc["da"], M + 1)
                    dve.wait_ge(sc["hc"], M + 1 + 4)
                    nc.vector.tensor_tensor_scan(h[:, m % 4, :], ps[2][:, m % NG, :], dbx[:, m % 4, :], 0.0,
                                                 ALU.mult, ALU.add).then_inc(sc["scan"], 1)

            scan_batch(0, True)
            with dve.Fori(1, NB) as b:
                scan_batch(b, False)
            add_skip(NB - 1)
            barrier(dve, 4)

            sz = ring[:, 0:4, :]
            dve.sem_inc(po["gated"], 2)
            dve.sem_inc(po["add"], 2)

            def gate_y(b, j):
                w = bass.ds(b * L, L)
                dve.wait_ge(po["sz"], b + 1 + 2)
                nc.vector.tensor_tensor(xm[:, :, w], xm[:, :, w], sz[:, 2 * j:2 * j + 2, :], ALU.mult)\
                    .then_inc(po["gated"], 1)

            def add_o(b, j):
                dve.wait_ge(po["tr"], b + 1 + 2)
                xb = x[:, bass.ds(b * TPB, TPB), :].rearrange("p t d -> p (t d)")
                nc.vector.scalar_tensor_tensor(out=xb, in0=ps[3][:, j, :], scalar=rs, in1=xb,
                                               op0=ALU.mult, op1=ALU.add).then_inc(po["add"], 1)
                dve.wait_ge(po["add"], b + 1 + 2)
                batch_stats(b)

            skewed(dve, gate_y, add_o)
            barrier(dve, 5)

            def top2(k, E, eps):
                s = gt[k]
                W = [gl[:, q, :, 0:E] for q in range(8)]
                tk = [sm[:, q, :] for q in (12, 13, 14)]

                def row(v):
                    return v.unsqueeze(2).to_broadcast([P, NT, E])

                def by_row(out_, a, v, op):
                    link(nc.vector.tensor_tensor(out_, a, row(v), op))

                link(nc.vector.tensor_reduce(tk[0], W[0], op=ALU.max, axis=AX.X))
                by_row(W[0], W[0], tk[0], ALU.subtract)
                dve.sem_inc(s["logit"], 1)
                dve.wait_ge(s["logit"], 2)
                link(nc.vector.tensor_reduce(tk[0], W[1], op=ALU.add, axis=AX.X))
                link(nc.vector.reciprocal(tk[0], tk[0]))
                by_row(W[1], W[1], tk[0], ALU.mult)
                iv = iot[:, :, 0:E]
                link(nc.vector.tensor_copy(W[2], W[1]))
                for q in range(2):
                    link(nc.vector.tensor_reduce(tk[q], W[2], op=ALU.max, axis=AX.X))
                    by_row(W[3], W[2], tk[q], ALU.is_equal)
                    link(nc.vector.tensor_tensor(W[3], W[3], iv, ALU.mult))
                    link(nc.vector.tensor_reduce(tk[2], W[3], op=ALU.max, axis=AX.X))
                    by_row(W[4 + q], W[3], tk[2], ALU.is_equal)
                    if q == 0:
                        link(nc.vector.scalar_tensor_tensor(out=W[2], in0=W[4], scalar=-2.0, in1=W[2],
                                                            op0=ALU.mult, op1=ALU.add))
                link(nc.vector.tensor_tensor(W[4], W[4], W[5], ALU.add))
                link(nc.vector.tensor_tensor(W[4], W[4], W[1], ALU.mult))
                link(nc.vector.tensor_tensor(tk[0], tk[0], tk[1], ALU.add))
                link(nc.vector.tensor_scalar(tk[0], tk[0], eps, None, ALU.add))
                link(nc.vector.reciprocal(tk[0], tk[0]))
                full = gl[:, 7, :, :]
                link(nc.vector.memset(full, 1.0))
                by_row(full[:, :, 0:E], W[4], tk[0], ALU.mult)
                hi, mid, low = (gl[:, q, :, :] for q in (1, 2, 3))
                tmp = gl[:, 4:5, :, :].rearrange("p o t e -> p (o t e)").bitcast(bf16)
                b16 = tmp[:, 0:NT * GW].rearrange("p (t e) -> p t e", e=GW)
                rest = gl[:, 5, :, :]
                link(nc.vector.tensor_copy(b16, full))
                link(nc.vector.tensor_copy(hi, b16))
                link(nc.vector.tensor_tensor(rest, full, hi, ALU.subtract))
                link(nc.vector.tensor_copy(b16, rest))
                link(nc.vector.tensor_copy(mid, b16))
                link(nc.vector.tensor_tensor(rest, rest, mid, ALU.subtract))
                link(nc.vector.tensor_copy(b16, rest))
                link(nc.vector.tensor_copy(low, b16))
                dve.sem_inc(s["copied"], 2)
                def stage(b, j):
                    dve.wait_ge(s["tr"], b + 1)
                    carry(dve)
                    for q, v in enumerate((hi, mid, low)):
                        last = nc.vector.tensor_copy(xnt[:, j, :, q * GW:(q + 1) * GW],
                                                     v[:, bass.ds(b * TPB, TPB), :])
                    last.then_inc(s["stage"], 1)

                def fetch(b, j):
                    dve.wait_ge(s["tr"], b + 1 + 2)
                    carry(dve)
                    nc.vector.tensor_copy(bc[0:3 * GW, bass.ds(b * L, L)], ps[3][0:3 * GW, j, :])\
                        .then_inc(s["copied"], 1)

                skewed(dve, stage, fetch)

            def take_logits(k, E):
                s = gt[k]
                dve.sem_inc(s["tk"], 2)
                with dve.Fori(0, NB // 2) as i:
                    for j in range(2):
                        b = i * 2 + j
                        dve.wait_ge(s["tm"], b + 1 + 2)
                        carry(dve)
                        src = ps[2][:, j, 0:TPB * GW].rearrange("p (t e) -> p t e", e=GW)
                        nc.vector.tensor_copy(gl[:, 0, bass.ds(b * TPB, TPB), 0:E], src[:, :, 0:E])\
                            .then_inc(s["tk"], 1)
                dve.wait_ge(s["tk"], NB + 2)

            def moe(k, units):
                s = mo[k]
                depth = DEPTH[k]
                hs, t_, hg = ring[:, 0:4, :], ring[:, 4:6, :], ring[:, 6:10, :]
                dve.sem_inc(s["gm"], 4)
                if k:
                    dve.sem_inc(s["um"], depth)
                dve.sem_inc(s["add"], 1)
                with dve.Fori(0, NB) as c:
                    for q in range(units):
                        K = c * units + q
                        dve.wait_ge(s["sil"], K + 1 + 2)
                        src = hs[:, q % depth, :]
                        if k:
                            dve.wait_ge(s["h"], K + 1)
                            nc.vector.tensor_tensor(t_[:, q % 2, :], src, ps[1][:, q % 2, :], ALU.mult)\
                                .then_inc(s["um"], 1)
                            dve.wait_ge(s["um"], K + 1 + depth)
                            src = t_[:, q % 2, :]
                        dve.wait_ge(s["gb"], c * (units // NH) + q // NH + 1)
                        dve.wait_ge(s["mm2"], K + 1)
                        nc.vector.tensor_tensor(hg[:, q % depth, :], src, ps[2][:, (q // NH) % 2, :], ALU.mult)\
                            .then_inc(s["gm"], 1)
                    dve.wait_ge(s["tr"], c + 1)
                    xb = x[:, bass.ds(c * TPB, TPB), :].rearrange("p t d -> p (t d)")
                    nc.vector.tensor_tensor(xb, xb, ps[3][:, 1, :], ALU.add).then_inc(s["add"], 1)
                    if k == 0:
                        dve.wait_ge(s["add"], c + 1 + 1)
                        batch_stats(c)

            moments()
            second_root(RMS_EPS)
            link(nc.vector.reciprocal(gain, r2))
            link(nc.vector.tensor_tensor(r2, r1, r2, ALU.mult))
            normalise(1, r2)
            dve.wait_ge(gt[0]["wt"], 1)
            link(nc.vector.tensor_copy(rmsT[:, :], ps[1][:, 0, 0:E0 + E0S]))
            dve.wait_ge(w_in[0], W_MOE0)
            for e in range(E0 + E0S):
                last = nc.vector.tensor_scalar(moe0_w1[:, e, :], moe0_w1[:, e, :], rmsT[:, e:e + 1], None, ALU.mult)
            barrier(dve, 6)

            take_logits(0, E0)
            link(nc.vector.tensor_tensor(gl[:, 0, :, 0:E0], gl[:, 0, :, 0:E0],
                                         gain.unsqueeze(2).to_broadcast([P, NT, E0]), ALU.mult))
            top2(0, E0, TOPK0_EPS)
            barrier(dve, 7)
            moe(0, (E0 + E0S) * NH)
            barrier(dve, 8)

            moments()
            normalise(2, r1)
            dve.sem_inc(at["add"], 1)
            dve.sem_inc(at["odd_out"], 1)

            def evac_odd(b, j, r):
                dve.wait_ge(at["odd"], b * 2 + r + 1)
                if r == 0:
                    nc.vector.tensor_copy(qkv[j][0:KD, 1, :], ps[3][0:KD, 1, :]).then_inc(at["odd_out"], 1)
                else:
                    nc.vector.tensor_copy(vs[j], ps[3][:, 1, :]).then_inc(at["odd_out"], 1)

            def mask_max(b, j, i):
                dve.wait_ge(at["s"], b * TPB + i + 1)
                S_ = ps[i // 2][:, i % 2, :]
                q = j * TPB + i
                nc.vector.tensor_tensor(S_[:, i * P:(i + 1) * P], S_[:, i * P:(i + 1) * P], cmask[:, :],
                                        ALU.add).then_inc(at["masked"], 1)
                dve.wait_ge(at["masked"], b * TPB + i + 1)
                nc.vector.tensor_reduce(sm[:, 12, q:q + 1], S_[:, 0:(i + 1) * P], op=ALU.max, axis=AX.X,
                                        negate=True).then_inc(at["mx"], 1)

            def attend(b, j, scores, loads):
                for i in range(TPB):
                    if loads and i == 1:
                        evac_odd(b + 2, j, 0)
                    if scores:
                        mask_max(b + 1, 1 - j, i)
                q = j * TPB
                dve.wait_ge(at["p"], (b + 1) * TPB)
                nc.vector.reciprocal(sm[:, 14, q:q + TPB], sm[:, 13, q:q + TPB]).then_inc(at["rd"], 1)
                if loads:
                    evac_odd(b + 2, j, 1)
                dve.wait_ge(at["rd"], b + 1)
                dve.wait_ge(at["o"], (b + 1) * TPB)
                for i in range(TPB):
                    xb = x[:, bass.ds(b * TPB + i, 1), :].rearrange("p t d -> p (t d)")
                    last = nc.vector.scalar_tensor_tensor(out=xb, in0=ps[2][:, 1, i * P:(i + 1) * P],
                                                          scalar=sm[:, 14, q + i:q + i + 1], in1=xb,
                                                          op0=ALU.mult, op1=ALU.add)
                last.then_inc(at["add"], 1)
                dve.wait_ge(at["add"], b + 1 + 1)
                batch_stats(b)

            for b in range(2):
                evac_odd(b, b, 0)
                evac_odd(b, b, 1)
            for i in range(TPB):
                mask_max(0, 0, i)
            with dve.Fori(0, NB // 2 - 1) as h_:
                for j in range(2):
                    attend(h_ * 2 + j, j, True, True)
            attend(NB - 2, 0, True, False)
            attend(NB - 1, 1, False, False)
            barrier(dve, 9)

            moments()
            second_root(LN_EPS)
            normalise(3, r1)
            dve.wait_ge(gt[1]["wt"], 1)
            link(nc.vector.tensor_copy(gwT[:, :], ps[1][:, 0, 0:E1]))
            link(nc.vector.tensor_copy(lnbr[:, :], lnsb[:, 1:2].to_broadcast([P, P])))
            dve.sem_inc(gt[1]["wc"], 1)
            dve.wait_ge(gt[1]["wt"], 2)
            link(nc.vector.tensor_copy(gconst[:, :], ps[1][:, 0, 0:E1]))
            link(nc.vector.tensor_scalar(gwT[:, :], gwT[:, :], lnsb[:, 0:1], None, ALU.mult))
            dve.sem_inc(gt[1]["wc"], 1)
            take_logits(1, E1)
            link(nc.vector.tensor_tensor(gl[:, 0, :, 0:E1], gl[:, 0, :, 0:E1],
                                         r2.unsqueeze(2).to_broadcast([P, NT, E1]), ALU.mult))
            link(nc.vector.tensor_tensor(gl[:, 0, :, 0:E1], gl[:, 0, :, 0:E1],
                                         gconst[:, :].unsqueeze(1).to_broadcast([P, NT, E1]), ALU.add))
            top2(1, E1, TOPK1_EPS)
            barrier(dve, 10)
            moe(1, NE1 * NH)
            barrier(dve, 11)

        @block.tensor
        def _(pe):
            def transposes(k):
                s = ln[k]
                pe.sem_inc(s["tr"], 2)

                def one(b, j):
                    pe.wait_ge(s["norm"], b + 1)
                    pe.wait_ge(s["xT"], b + 1)
                    for q in range(TPB):
                        last = nc.tensor.transpose(ps[0][:, j, q * P:(q + 1) * P], xnt[:, j, q, :], ident[:, :])
                    last.then_inc(s["tr"], 1)

                return one

            def pairs(one):
                with pe.Fori(0, NB // 2) as i:
                    for j in range(2):
                        one(i * 2 + j, j)

            def rows(b):
                return xT[:, bass.ds(b, 1), PAD:].rearrange("p o t -> p (o t)")

            pe.wait_ge(loaded, N_SMALL)
            pe.wait_ge(ident_ready, 1)
            nc.tensor.transpose(ps[1][:, 0, 0:NV], vrows[:, :], ident[0:NV, 0:NV]).then_inc(vec_done, 1)
            barrier(pe, 1)

            def conv(b, j):
                pe.wait_ge(ln[0]["xT"], b + 1 + 2)
                pe.wait_ge(pre["xm"], b + 1)
                for g in range(NG):
                    for k in range(TAPS):
                        last = nc.tensor.matmul(ps[1 + j][:, g, :], Wk[:, k, g * P:(g + 1) * P],
                                                xT[:, bass.ds(b, 1), k:k + L].rearrange("p o t -> p (o t)"),
                                                start=k == 0, stop=k == TAPS - 1)
                last.then_inc(pre["conv"], 1)

            skewed(pe, transposes(0), conv)
            barrier(pe, 2)

            R0, R1 = 3 * BC, 3 * BC + RANK
            dtr = ring[:, 0:2, :]

            def project_x(b, j):
                pe.wait_ge(pre["split"], b + 1)
                for g in range(NG):
                    last = nc.tensor.matmul(ps[0][0:R1, j, :], xpw[:, g, :], xm[:, g, bass.ds(b * L, L)],
                                            start=g == 0, stop=g == NG - 1)
                last.then_inc(pre["xp"], 1)

            def project_dt(b, j):
                pe.wait_ge(pre["dtr"], b + 1)
                pe.wait_ge(pre["dt"], b + 1)
                for g in range(NG):
                    last = nc.tensor.matmul(ps[1 + j][:, g, :], dtw[R0:R1, g * P:(g + 1) * P],
                                            dtr[R0:R1, j, :], start=True, stop=True)
                last.then_inc(pre["dtp"], 1)

            skewed(pe, project_x, project_dt)
            pe.wait_ge(consts_ready, 1)
            barrier(pe, 3)

            hc = ring[:, 4:12, :]
            pe.sem_inc(sc["ns"], 8)

            def spread(b, n_, N):
                w = bass.ds(b * L, L)
                pe.wait_ge(sc["dbx"], N * 2 + 2)
                nc.tensor.matmul(ps[0][:, n_ % 2, :], sel[:, n_, :], bc[:, w], start=True, stop=True)\
                    .then_inc(sc["bb"], 1)
                pe.wait_ge(sc["cs"], N + 1)
                nc.tensor.matmul(ps[1][:, 0, :], sel[:, NS + n_, :], bc[:, w], start=True, stop=True)\
                    .then_inc(sc["cb"], 1)

            def sum_state(b, n_):
                for g in range(NG):
                    m = n_ * NG + g
                    if m == 0:
                        pe.wait_ge(sc["y"], b + 1)
                    pe.wait_ge(sc["hc"], b * (NS * NG) + m + 1 + 8)
                    nc.tensor.matmul(ps[3][:, g, :], ident[:, :], hc[:, m % 8, :], start=n_ == 0,
                                     stop=n_ == NS - 1, skip_group_check=True).then_inc(sc["ns"], 1)

            spread(0, 0, 0)
            with pe.Fori(0, NB) as b:
                for n_ in range(NS):
                    if n_ + 1 < NS:
                        spread(b, n_ + 1, b * NS + n_ + 1)
                    else:
                        spread(b + 1, 0, (b + 1) * NS)
                    if n_:
                        sum_state(b, n_ - 1)
                sum_state(b, NS - 1)
            barrier(pe, 4)

            pe.sem_inc(po["tr"], 2)

            def project_z(b, j):
                pe.wait_ge(po["sz"], b + 1)
                for g in range(NG):
                    last = nc.tensor.matmul(ps[j][:, g, :], inw[:, DI + g * P:DI + (g + 1) * P], rows(b),
                                            start=True, stop=True)
                last.then_inc(po["z"], 1)

            def project_y(b, j):
                pe.wait_ge(po["gated"], b + 1 + 2)
                pe.wait_ge(po["oc"], b + 1)
                for g in range(NG):
                    last = nc.tensor.matmul(ps[2][:, j, :], opw[:, g, :], xm[:, g, bass.ds(b * L, L)],
                                            start=g == 0, stop=g == NG - 1)
                last.then_inc(po["o"], 1)
                pe.wait_ge(po["oc"], b + 1 + 2)
                pe.wait_ge(po["add"], b + 1)
                for q in range(TPB):
                    last = nc.tensor.transpose(ps[3][:, j, q * P:(q + 1) * P],
                                               ring[:, 4 + j, q * P:(q + 1) * P], ident[:, :])
                last.then_inc(po["tr"], 1)

            skewed(pe, project_z, project_y)
            barrier(pe, 5)

            def router(k, w, E):
                s = gt[k]
                pe.sem_inc(s["tm"], 2)
                pe.sem_inc(s["tr"], 2)

                def logits(b, j):
                    pe.wait_ge(s["lc"], b + 1)
                    nc.tensor.matmul(ps[1][0:E, j, :], w, rows(b), start=True, stop=True).then_inc(s["lt"], 1)

                def token_major(b, j):
                    pe.wait_ge(s["lc"], b + 1 + 2)
                    pe.wait_ge(s["tk"], b + 1)
                    carry(pe)
                    for q in range(TPB):
                        last = nc.tensor.transpose(ps[2][:, j, q * GW:q * GW + E],
                                                   ring[0:E, j, q * P:(q + 1) * P], ident[0:E, 0:E])
                    last.then_inc(s["tm"], 1)

                skewed(pe, logits, token_major)
                with pe.Fori(0, NB // 2) as i:
                    for j in range(2):
                        b = i * 2 + j
                        pe.wait_ge(s["stage"], b + 1)
                        pe.wait_ge(s["copied"], b + 1)
                        carry(pe)
                        for q in range(TPB):
                            last = nc.tensor.transpose(ps[3][0:3 * GW, j, q * P:(q + 1) * P],
                                                       xnt[:, j, q, 0:3 * GW], ident[:, :])
                        last.then_inc(s["tr"], 1)

            def moe(k, nexp, first, second, down):
                s = mo[k]
                units = nexp * NH
                depth = DEPTH[k]
                hg = ring[:, 6:10, :]
                ya = ring[:, 10, :]
                pe.sem_inc(s["mm2"], depth)

                def hidden(c, q):
                    e, hb = q // NH, q % NH
                    K = c * units + q
                    pe.wait_ge(s["sil"], K + 1)
                    last = nc.tensor.matmul(ps[0][:, q % 2, :], first[:, e, hb * P:(hb + 1) * P], rows(c),
                                            start=True, stop=True)
                    if second is not None:
                        pe.wait_ge(s["um"], K - 1 + depth)
                        last.then_inc(s["g"], 1)
                        last = nc.tensor.matmul(ps[1][:, q % 2, :], second[:, e, hb * P:(hb + 1) * P], rows(c),
                                                start=True, stop=True)
                    last.then_inc(s["h"], 1)
                    if hb == 0:
                        E = c * nexp + e
                        pe.wait_ge(s["gm"], E * 2 + (4 if e == 0 and nexp % 2 else 2))
                        carry(pe)
                        nc.tensor.matmul(ps[2][:, e % 2, :], selg[:, e, :], bc[0:3 * GW, bass.ds(c * L, L)],
                                         start=True, stop=True).then_inc(s["gb"], 1)

                with pe.Fori(0, NB) as c:
                    hidden(c, 0)
                    hidden(c, 1)
                    for q in range(units):
                        if q + 2 < units:
                            hidden(c, q + 2)
                        if q == 0:
                            pe.wait_ge(s["acc"], c + 1)
                        pe.wait_ge(s["gm"], c * units + q + 1 + 4)
                        nc.tensor.matmul(ps[3][:, 0, :], down[:, q // NH, q % NH, :], hg[:, q % depth, :],
                                         start=q == 0, stop=q == units - 1).then_inc(s["mm2"], 1)
                    pe.wait_ge(s["acc"], c + 1 + 1)
                    pe.wait_ge(s["add"], c + 1)
                    for q in range(TPB):
                        last = nc.tensor.transpose(ps[3][:, 1, q * P:(q + 1) * P], ya[:, q * P:(q + 1) * P],
                                                   ident[:, :])
                    last.then_inc(s["tr"], 1)

            nc.tensor.transpose(ps[1][:, 0, 0:E0 + E0S], rmsr[:, :], ident[0:E0 + E0S, 0:E0 + E0S])\
                .then_inc(gt[0]["wt"], 1)
            pairs(transposes(1))
            barrier(pe, 6)
            router(0, wr[:, :], E0)
            barrier(pe, 7)
            pe.wait_ge(w_in[0], W_MOE0)
            moe(0, E0 + E0S, moe0_w1, None, moe0_w2)
            barrier(pe, 8)

            pairs(transposes(2))
            pe.wait_ge(ln[2]["xT"], NB + 2)

            def load_qk(b, j):
                pe.wait_ge(at["even_out"], b * 2 + 1)
                carry(pe)
                nc.tensor.matmul(ps[3][0:KD, 0, :], wqk[:, 0, :], rows(b), start=True, stop=True)\
                    .then_inc(at["even"], 1)
                pe.wait_ge(at["odd_out"], b * 2 + 1)
                carry(pe)
                nc.tensor.matmul(ps[3][0:KD, 1, :], wqk[:, 1, :], rows(b), start=True, stop=True)\
                    .then_inc(at["odd"], 1)

            def load_v1(b, j):
                pe.wait_ge(at["even_out"], b * 2 + 2)
                carry(pe)
                nc.tensor.matmul(ps[3][0:KD, 0, :], wqk[:, 2, :], rows(b), start=True, stop=True)\
                    .then_inc(at["even"], 1)

            def load_v(b, j):
                pe.wait_ge(at["even_out"], b * 2 + 3)
                pe.wait_ge(at["odd_out"], b * 2 + 2)
                for i in range(TPB):
                    last = nc.tensor.matmul(ps[3][:, 1, i * P:(i + 1) * P], qkv[j][0:KD, 2, i * P:(i + 1) * P],
                                            wv2[:, :], start=True, stop=True)
                last.then_inc(at["odd"], 1)

            def scores_of(b, j, i):
                if i == 0:
                    pe.wait_ge(at["even_out"], b * 2 + 2)
                    pe.wait_ge(at["odd_out"], b * 2 + 2)
                nc.tensor.matmul(ps[i // 2][:, i % 2, 0:(i + 1) * P], qkv[j][0:KD, 0, i * P:(i + 1) * P],
                                 qkv[j][0:KD, 1, 0:(i + 1) * P], start=True, stop=True).then_inc(at["s"], 1)

            def attend(b, j, scores, loads):
                for i in range(TPB):
                    pe.wait_ge(at["p"], b * TPB + i + 1)
                    pe.wait_ge(at["pts"], b * TPB + i + 1)
                    for k in range(i + 1):
                        last = nc.tensor.transpose(ps[2][:, 0, k * P:(k + 1) * P],
                                                   pr[j][:, i, k * P:(k + 1) * P], ident[:, :])
                    last.then_inc(at["pt"], 1)
                    if loads and i == 0:
                        load_qk(b + 2, j)
                    if loads and i == 2:
                        load_v1(b + 2, j)
                    if scores:
                        scores_of(b + 1, 1 - j, i)
                    pe.wait_ge(at["pts"], b * TPB + i + 1 + 1)
                    if i == 0:
                        pe.wait_ge(at["odd_out"], b * 2 + 3)
                        pe.wait_ge(at["add"], b + 1)
                    for k in range(i + 1):
                        last = nc.tensor.matmul(ps[2][:, 1, i * P:(i + 1) * P], pt[:, i % 2, k * P:(k + 1) * P],
                                                vs[j][:, k * P:(k + 1) * P], start=k == 0, stop=k == i)
                    last.then_inc(at["o"], 1)
                if loads:
                    load_v(b + 2, j)

            for b in range(2):
                load_qk(b, b)
                load_v1(b, b)
                load_v(b, b)
            for i in range(TPB):
                scores_of(0, 0, i)
            with pe.Fori(0, NB // 2 - 1) as h_:
                for j in range(2):
                    attend(h_ * 2 + j, j, True, True)
            attend(NB - 2, 0, True, False)
            attend(NB - 1, 1, False, False)
            barrier(pe, 9)

            nc.tensor.transpose(ps[1][:, 0, 0:E1], gwr[:, :], ident[0:E1, 0:E1]).then_inc(gt[1]["wt"], 1)
            pairs(transposes(3))
            pe.wait_ge(gt[1]["wc"], 1)
            nc.tensor.matmul(ps[1][:, 0, 0:E1], lnbr[:, :], gwT[:, :], start=True, stop=True)\
                .then_inc(gt[1]["wt"], 1)
            pe.wait_ge(gt[1]["wc"], 2)
            pe.wait_ge(ln[3]["xT"], NB + 2)
            router(1, gwT[:, :], E1)
            barrier(pe, 10)
            pe.wait_ge(w_in[1], W_MOE1)
            moe(1, NE1, moe1_wg, moe1_wu, moe1_wd)
            barrier(pe, 11)


_IN_ORDER = ['L0_attn_x', 'L0_attn_ln_w', 'L0_attn_ln_b', 'L0_attn_in_proj_w', 'L0_attn_conv_w', 'L0_attn_conv_b',
             'L0_attn_x_proj_w', 'L0_attn_dt_proj_w', 'L0_attn_dt_proj_b', 'L0_attn_A_log', 'L0_attn_D_param',
             'L0_attn_out_proj_w', 'L0_attn_res_scale', 'L0_ffn_router_w', 'L0_ffn_rms_w', 'L0_ffn_w1', 'L0_ffn_w2',
             'L0_ffn_rms_w_s', 'L0_ffn_w1_s', 'L0_ffn_w2_s', 'L1_attn_w_q', 'L1_attn_w_k', 'L1_attn_w_v1',
             'L1_attn_w_v2', 'L1_ffn_ln_scale', 'L1_ffn_ln_bias', 'L1_ffn_gate_w', 'L1_ffn_Wg', 'L1_ffn_Wu',
             'L1_ffn_Wd', 'L1_ffn_sWg', 'L1_ffn_sWu', 'L1_ffn_sWd']


def kernel(**inputs):
    import numpy as np
    import concourse.bacc as bacc
    from concourse.bass_utils import run_bass_kernel_spmd

    nc = bacc.Bacc("TRN2", target_bir_lowering=False, num_devices=1)
    arrays, args = {}, {}
    for name in _IN_ORDER:
        a = np.ascontiguousarray(inputs[name])
        arrays[f"in_{name}"] = a
        args[name] = nc.dram_tensor(f"in_{name}", a.shape, mybir.dt.from_np(a.dtype), kind="ExternalInput").ap()
    shape = arrays["in_L0_attn_x"].shape
    out = nc.dram_tensor("out_x", shape, mybir.dt.float32, kind="ExternalOutput").ap()
    mamba_moe_attention_moe_kernel(nc, args, out)
    r = run_bass_kernel_spmd(nc, [arrays], core_ids=[0])
    return r.results[0]["out_x"]
```

```python
import concourse.bass as bass
from concourse import mybir
from contextlib import ExitStack


def mamba_moe_attention_moe_kernel(nc: bass.Bass, A: dict, out: bass.AP):
    f32 = mybir.dt.float32
    bf16 = mybir.dt.bfloat16
    f32r = mybir.dt.float32r
    i32 = mybir.dt.int32
    ALU = mybir.AluOpType
    ACT = mybir.ActivationFunctionType
    AX = mybir.AxisListType

    P = 128
    NB, L, D = A["L0_attn_x"].shape
    TPB = L // P
    NT = NB * TPB
    NTOK = NB * L
    DI = A["L0_attn_D_param"].shape[0]
    NG = DI // P
    TAPS = A["L0_attn_conv_w"].shape[1]
    PAD = TAPS - 1
    NS = A["L0_attn_A_log"].shape[1]
    RANK = A["L0_attn_dt_proj_w"].shape[0]
    BC = 2 * NS
    E0 = A["L0_ffn_router_w"].shape[1]
    E0S = A["L0_ffn_w1_s"].shape[0]
    E1 = A["L1_ffn_gate_w"].shape[0]
    HID = A["L0_ffn_w1"].shape[2]
    NH = HID // P
    KD = A["L1_attn_w_q"].shape[1]
    GW = 16
    LN_EPS = 1e-5
    RMS_EPS = 1.1920929e-07
    TOPK0_EPS = 1e-9
    TOPK1_EPS = 1e-5
    NEG = -1e30

    ctx = ExitStack()
    with ctx:
        def sb(name, shape, dt=f32):
            return ctx.enter_context(nc.sbuf_tensor(name, shape, dt))

        def sem(name):
            return ctx.enter_context(nc.semaphore(name))

        x = sb("x", [P, NT, D])
        xT = sb("xT", [P, NB, PAD + L])
        big3 = sb("big3", [P, NG, NTOK])
        xm = big3
        bc = sb("bc", [3 * BC, NTOK + L], bf16)
        sel = sb("sel", [3 * BC, BC, P], bf16)
        selg = sb("selg", [3 * GW, GW, P], bf16)
        ident = sb("ident", [P, P])
        cmask = sb("cmask", [P, P])
        Wk = sb("Wk", [P, TAPS, DI])
        inw = sb("inw", [P, 2 * DI])
        xpw = sb("xpw", [P, NG, 3 * BC + RANK])
        dtw = sb("dtw", [RANK, DI])
        opw = sb("opw", [P, NG, D])
        cols = sb("cols", [P, 16])
        Aneg = sb("Aneg", [P, NG, NS])
        wqk = sb("wqk", [P, 3, KD])
        wv2 = sb("wv2", [KD, D])
        stats = sb("stats", [P, NT, 6])
        sm = sb("sm", [P, 16, NT])
        iot = sb("iot", [P, NT, GW])
        wr = sb("wr", [P, E0])
        gwT = sb("gwT", [P, E1])
        gwr = sb("gwr", [E1, P])
        vrows = sb("vrows", [10, P])
        rs_sb = sb("rs_sb", [P, 1])
        lnbr = sb("lnbr", [P, P])
        gconst = sb("gconst", [P, E1])
        rmsT = sb("rmsT", [P, E0 + E0S])
        rmsr = sb("rmsr", [E0 + E0S, P])
        with ExitStack() as early:
            dt = early.enter_context(nc.sbuf_tensor("softplus_dt", [P, NG, NTOK], f32))
            u = early.enter_context(nc.sbuf_tensor("dt_x_main", [P, NG, NTOK], f32))
            ring = early.enter_context(nc.sbuf_tensor("ring", [P, 20, L], f32))
        w_hi = sb("w_hi", [P, NG * NTOK], f32r)
        w_lo = sb("w_lo", [P, NG * NTOK], f32r)
        mrows = sb("mrows", [P, 6, L])
        hg_hi = sb("hg_hi", [P, 4, L], f32r)
        hg_lo = sb("hg_lo", [P, 4, L], f32r)
        x_hi = sb("x_hi", [P, 2, L], f32r)
        x_lo = sb("x_lo", [P, 2, L], f32r)
        cwb = ring[:, 0:DI * TAPS // L, :].rearrange("p r t -> p (r t)").rearrange("p (c k) -> p c k", k=TAPS)
        xnt = ring[:, 18:20, :].rearrange("p j (q d) -> p j q d", d=D)
        gates_flat = big3[:, :, :].rearrange("p g t -> p (g t)")
        gl = gates_flat[:, 0:8 * NT * GW].rearrange("p (q t e) -> p q t e", t=NT, e=GW)
        gate_parts = gates_flat[:, 8 * NT * GW:(8 + 3) * NT * GW].rearrange("p (t m) -> p t m", m=3 * GW)
        ps = [ctx.enter_context(nc.psum_tensor(f"ps{i}", [P, 2, L], f32)) for i in range(4)]

        lnw, lnb = cols[:, 0:1], cols[:, 1:2]
        convb = cols[:, 2:2 + NG]
        dtb = cols[:, 4:4 + NG]
        Dp = cols[:, 6:6 + NG]
        lnsb = cols[:, 8:10]
        rs = rs_sb[:, :]
        XW = NB * (PAD + L)
        xT_hi, xT_lo = (t[:, 0:XW].rearrange("p (b t) -> p b t", t=PAD + L) for t in (w_hi, w_lo))
        Wk_hi, Wk_lo = (t[:, XW:XW + TAPS * DI].rearrange("p (k c) -> p k c", c=DI) for t in (w_hi, w_lo))
        R0, R1 = 3 * BC, 3 * BC + RANK
        av, lt, dtr, part = ring[:, 0:4, :], ring[:, 4:8, :], ring[:, 8:8 + NB, :], ring[:, 8 + NB, :]
        TRB = [[ps[0][:, j, :] for j in range(2)], [ps[0][:, j, :] for j in range(2)], [ps[1][:, 1, :]] * 2,
               [ps[3][:, 0, :]] * 2]
        ACC = [[ps[3][:, j, :] for j in range(2)], [ps[3][:, 0, :]] * 2]
        NACC = [2, 1]
        GATE_BANK = [ps[1][:, 1, :], ps[3][:, 1, :]]
        TRS = [ps[1][:, 0, :], ps[3][:, 1, :]]
        NV = 10

        mu, var, r1, r2, t0, t1, t2, t3, gain, shift = (sm[:, k, :] for k in range(10))

        loaded = sem("loaded")
        ident_ready = sem("ident_ready")
        consts_ready = sem("consts_ready")
        carried = sem("carried")
        vec_done = sem("vec_done")
        x_in = [sem(f"x_in{k}") for k in range(2)]
        taps_in = sem("taps_in")
        w_in = [sem(f"w_in{k}") for k in range(5)]
        w_split = [sem(f"w_split{k}") for k in range(2)]
        rms_ready = sem("rms_ready")
        w_scaled = sem("w_scaled")
        w_high = sem("w_high")
        stored = sem("stored")
        step = sem("step")
        step_act = sem("step_act")
        step_pool = sem("step_pool")
        phase_done = sem("phase_done")

        def sems(prefix, names):
            return {n: sem(f"{prefix}_{n}") for n in names.split()}

        ln = [sems(f"ln{k}", "num norm tr xT") for k in range(4)]
        pre = sems("pre", "wk wk_hi wk_lo x_lo conv xm xp dtr parts split dtp absd soft dsum dt u")
        sc = sems("sc", "bb cb cs da dbx scan hc ns y")
        po = sems("po", "z sz gated o oc tr add")
        gt = [sems(f"gt{k}", "wt wc lt lc tm tk logit stage tr copied") for k in range(2)]
        mo = [sems(f"mo{k}", "xh xl g h sil um gb gm hi lo mm2 acc tr add") for k in range(2)]
        at = sems("at", "even odd even_out odd_out s masked mx p pt pts rd o add")

        GB = (2, 4)
        GATE_UNITS = [{u: GB[k] + i for i, u in enumerate(us)} for k, us in enumerate(((2, 4, 6, 8, 10, 12),
                                                                                       (5, 8, 11, 13)))]
        LAG = 4
        DEPTH = 4
        AHEAD = 3
        block = ctx.enter_context(nc.Block())

        x_d = A["L0_attn_x"].rearrange("b (k p) d -> p (b k) d", p=P)
        out_d = out.rearrange("b (k p) d -> p (b k) d", p=P)

        NE0, NE1 = E0 + E0S, E1 + 1

        def up_weights(t, at_, n):
            return t[:, at_:at_ + n * HID].rearrange("p (e h) -> p e h", h=HID)

        def down_weights(t, at_, n):
            return t[:, at_:at_ + n * HID].rearrange("p (e b d) -> p e b d", b=NH, d=D)

        both = (w_hi, w_lo)
        moe0_w1 = [up_weights(t, 0, NE0) for t in both]
        moe0_w2 = [down_weights(t, NE0 * HID, NE0) for t in both]
        moe1_wg = [up_weights(t, 0, NE1) for t in both]
        moe1_wu = [up_weights(t, NE1 * HID, NE1) for t in both]
        moe1_wd = [down_weights(t, 2 * NE1 * HID, NE1) for t in both]
        HE = NE0 // 2
        PIECE = HE * HID
        piece_buf = [ring[:, 6 + 4 * k:10 + 4 * k, :].rearrange("p r t -> p (r t)") for k in range(3)]
        piece_at = [NE0 * HID, NE0 * HID + PIECE, 0, PIECE]
        raw1 = big3[:, :, :].rearrange("p g t -> p (g t)")
        raw_wg, raw_wu = up_weights(raw1, 0, NE1), up_weights(raw1, NE1 * HID, NE1)
        raw_wd = down_weights(raw1, 2 * NE1 * HID, NE1)

        smalls = []

        def vec(name):
            return A[name].rearrange("(g p) -> g p", p=P)

        smalls += [(vrows[0:1, :], vec("L0_attn_ln_w")), (vrows[1:2, :], vec("L0_attn_ln_b")),
                   (vrows[2:2 + NG, :], vec("L0_attn_conv_b")), (vrows[4:4 + NG, :], vec("L0_attn_dt_proj_b")),
                   (vrows[6:6 + NG, :], vec("L0_attn_D_param")),
                   (vrows[8:9, :], vec("L1_ffn_ln_scale")), (vrows[9:10, :], vec("L1_ffn_ln_bias")),
                   (rs, A["L0_attn_res_scale"].rearrange("(a o) -> a o", a=1).to_broadcast([P, 1])),
                   (Aneg[:, :, :], A["L0_attn_A_log"].rearrange("(g p) n -> p g n", p=P)),
                   (opw[:, :, :], A["L0_attn_out_proj_w"].rearrange("(g p) n -> p g n", p=P)),
                   (dtw[:, :], A["L0_attn_dt_proj_w"]),
                   (wr[:, :], A["L0_ffn_router_w"]),
                   (gwr[:, :], A["L1_ffn_gate_w"]),
                   (rmsr[0:E0, :], A["L0_ffn_rms_w"]), (rmsr[E0:E0 + E0S, :], A["L0_ffn_rms_w_s"]),
                   (wqk[:, 0, :], A["L1_attn_w_q"]), (wqk[:, 1, :], A["L1_attn_w_k"]),
                   (wqk[:, 2, :], A["L1_attn_w_v1"]), (wv2[:, :], A["L1_attn_w_v2"])]
        xpw_d = A["L0_attn_x_proj_w"].rearrange("(g p) n -> p g n", p=P)
        smalls += [(xpw[:, :, k * BC:(k + 1) * BC], xpw_d[:, :, RANK:RANK + BC]) for k in range(3)]
        smalls += [(xpw[:, :, 3 * BC:], xpw_d[:, :, 0:RANK])]

        BARRIERS = (1, 3, 4, 5, 6, 7, 8, 9, 10, 11)

        def ended(n):
            return 3 * (1 + BARRIERS.index(n))

        def barrier(eng, n):
            eng.drain().then_inc(phase_done, 1)
            eng.wait_ge(phase_done, ended(n))

        def skewed(eng, ahead, behind):
            ahead(0, 0)
            with eng.Fori(0, NB // 2 - 1) as i:
                for j in range(2):
                    b = i * 2 + j
                    ahead(b + 1, 1 - j)
                    behind(b, j)
            ahead(NB - 1, 1)
            behind(NB - 2, 0)
            behind(NB - 1, 1)

        def chunks(eng, chunk):
            chunk(0, 0, 0, False)
            chunk(1, 1, 1, False)
            with eng.Fori(0, NB // 2 - 2) as i:
                for j in range(2):
                    chunk(i * 2 + 2 + j, j, 2, False)
            chunk(NB - 2, 0, 2, False)
            chunk(NB - 1, 1, 2, True)

        def pairs(eng, one):
            with eng.Fori(0, NB // 2) as i:
                for j in range(2):
                    one(i * 2 + j, j)

        def fours(eng, one):
            with eng.Fori(0, NB // 4) as i:
                for j in range(4):
                    one(i * 4 + j, j)

        def thrice_skewed(eng, first, second, third):
            first(0, 0)
            first(1, 1)
            second(0, 0)
            with eng.Fori(0, NB // 2 - 1) as i:
                for j in range(2):
                    b = i * 2 + j
                    first(b + 2, j)
                    second(b + 1, 1 - j)
                    third(b, j)
            second(NB - 1, 1)
            third(NB - 2, 0)
            third(NB - 1, 1)

        def batches(eng, attend):
            attend(0, 0, 0, True, True)
            attend(1, 1, 1, True, True)
            with eng.Fori(0, NB // 2 - 2) as i:
                for j in range(2):
                    attend(i * 2 + 2 + j, j, 2, True, True)
            attend(NB - 2, 0, 2, True, False)
            attend(NB - 1, 1, 2, False, False)

        def carry(eng):
            eng.sem_inc(carried, 1)

        qkv = [ring[:, 3 * j:3 * j + 3, :] for j in range(2)]
        vs = [ring[:, 6 + j, :] for j in range(2)]
        pr = [ring[:, 8 + 4 * j:12 + 4 * j, :] for j in range(2)]
        pt = ring[:, 16:18, :]

        @block.sync
        def _(sp):
            sp.dma_start(inw[:, :], A["L0_attn_in_proj_w"]).then_inc(taps_in, 16)
            sp.dma_start(cwb[:, :, :].rearrange("p c k -> p (c k)"),
                         A["L0_attn_conv_w"].rearrange("(a c) k -> a (c k)", a=1).to_broadcast([P, DI * TAPS]))\
                .then_inc(taps_in, 16)
            for h_ in range(2):
                w = slice(h_ * NT // 2, (h_ + 1) * NT // 2)
                sp.dma_start(x[:, w, :], x_d[:, w, :]).then_inc(x_in[h_], 16)
            for dst, src in smalls[1::2]:
                sp.dma_start(dst, src).then_inc(loaded, 16)
            sp.wait_ge(phase_done, ended(4))
            w1_d = A["L0_ffn_w1"].rearrange("e d h -> d e h")
            w2_d = A["L0_ffn_w2"].rearrange("e (b p) d -> p e b d", p=P)
            w2s_d = A["L0_ffn_w2_s"].rearrange("e (b p) d -> p e b d", p=P)
            for k in range(4):
                dst = piece_buf[k % 3]
                if k < 2:
                    d2 = down_weights(dst, 0, HE)
                    for e in range(HE):
                        E = k * HE + e
                        sp.dma_start(d2[:, e, :, :], w2_d[:, E, :, :] if E < E0 else w2s_d[:, E - E0, :, :])\
                            .then_inc(w_in[k], 16)
                else:
                    d1 = up_weights(dst, 0, HE)
                    if k == 3:
                        sp.wait_ge(w_split[0], 1)
                        sp.dma_start(d1[:, 0:E0 - HE, :], w1_d[:, HE:E0, :]).then_inc(w_in[k], 16)
                        sp.dma_start(d1[:, E0 - HE:, :], A["L0_ffn_w1_s"].rearrange("e d h -> d e h"))\
                            .then_inc(w_in[k], 16)
                    else:
                        sp.dma_start(d1, w1_d[:, 0:HE, :]).then_inc(w_in[k], 16)
            sp.wait_ge(gt[0]["copied"], NB)
            for w, a, s in ((raw_wg, "L1_ffn_Wg", "L1_ffn_sWg"), (raw_wu, "L1_ffn_Wu", "L1_ffn_sWu")):
                sp.dma_start(w[:, 0:E1, :], A[a].rearrange("e d h -> d e h")).then_inc(w_in[4], 16)
                sp.dma_start(w[:, E1, :], A[s]).then_inc(w_in[4], 16)
            wd = A["L1_ffn_Wd"].rearrange("e (b p) d -> p e b d", p=P)
            for e in range(E1):
                sp.dma_start(raw_wd[:, e, :, :], wd[:, e, :, :]).then_inc(w_in[4], 16)
            sp.dma_start(raw_wd[:, E1, :, :], A["L1_ffn_sWd"].rearrange("(b p) d -> p b d", p=P))\
                .then_inc(w_in[4], 16)
            for c in range(NB):
                sp.wait_ge(mo[1]["add"], c + 1 + 1)
                w = slice(c * TPB, (c + 1) * TPB)
                sp.dma_start(out_d[:, w, :], x[:, w, :]).then_inc(stored, 16)
            sp.wait_ge(stored, 16 * NB)

        W_IN = [16 * HE, 16 * HE, 16, 16 * 2, 16 * (4 + E1 + 1)]
        N_SMALL = 16 * len(smalls)

        @block.gpsimd
        def _(pool):
            n = [0]

            def link(ins):
                n[0] += 1
                ins.then_inc(step_pool, 1)
                pool.wait_ge(step_pool, n[0])

            link(nc.gpsimd.memset(ident[:, :], 0.0))
            link(nc.gpsimd.affine_select(out=ident[:, :], in_=ident[:, :], compare_op=ALU.not_equal, fill=1.0,
                                         base=0, pattern=[[-1, P]], channel_multiplier=1))
            link(nc.gpsimd.memset(xT[:, :, 0:PAD], 0.0))
            link(nc.gpsimd.tensor_copy(xT_hi[:, :, 0:PAD], xT[:, :, 0:PAD]))
            link(nc.gpsimd.tensor_copy(xT_lo[:, :, 0:PAD], xT[:, :, 0:PAD]))
            pool.sem_inc(ident_ready, 1)

            with pool.Fori(0, NB) as b:
                pool.wait_ge(ln[0]["xT"], b + 1 + 2)
                w = bass.ds(b, 1)
                nc.gpsimd.tensor_tensor(xT_lo[:, w, PAD:], xT[:, w, PAD:], xT_hi[:, w, PAD:], ALU.subtract)\
                    .then_inc(pre["x_lo"], 1)

            link(nc.gpsimd.memset(bc[:, NTOK:], 0.0))
            link(nc.gpsimd.memset(sel[:, :, :], 0.0))
            for k in range(3):
                link(nc.gpsimd.affine_select(out=sel[:, :, :], in_=sel[:, :, :], compare_op=ALU.not_equal, fill=1.0,
                                             base=-k * BC, pattern=[[-1, BC], [0, P]], channel_multiplier=1))
            link(nc.gpsimd.memset(selg[:, :, :], 0.0))
            for k in range(3):
                link(nc.gpsimd.affine_select(out=selg[:, :, :], in_=selg[:, :, :], compare_op=ALU.not_equal,
                                             fill=1.0, base=-k * GW, pattern=[[-1, GW], [0, P]],
                                             channel_multiplier=1))
            link(nc.gpsimd.memset(cmask[:, :], 0.0))
            link(nc.gpsimd.affine_select(out=cmask[:, :], in_=cmask[:, :], compare_op=ALU.is_ge, fill=NEG,
                                         base=0, pattern=[[-1, P]], channel_multiplier=1))
            link(nc.gpsimd.iota(iot[:, :, :], pattern=[[0, NT], [-1, GW]], base=GW, channel_multiplier=0,
                                allow_small_or_imprecise_dtypes=True))
            pool.sem_inc(consts_ready, 1)

            with pool.Fori(0, NB) as b:
                pool.wait_ge(pre["dt"], b + 1 + 4)
                w = bass.ds(b * L, L)
                nc.gpsimd.tensor_tensor(u[:, :, w], dt[:, :, w], xm[:, :, w], ALU.mult).then_inc(pre["u"], 1)

            h, hc, cs = ring[:, 0:4, :], ring[:, 4:12, :], ring[:, 12:16, :]
            pool.sem_inc(sc["hc"], 8)
            with pool.Fori(0, NB) as b:
                for n_ in range(NS):
                    for g in range(NG):
                        m = n_ * NG + g
                        M = b * (NS * NG) + m
                        pool.wait_ge(sc["scan"], M + 1 + 2)
                        if g == 0:
                            pool.wait_ge(sc["cs"], b * NS + n_ + 1 + 1)
                        pool.wait_ge(sc["ns"], M + 1)
                        nc.gpsimd.tensor_tensor(hc[:, m % 8, :], h[:, m % 4, :], cs[:, n_ % 4, :],
                                                ALU.mult).then_inc(sc["hc"], 1)

            def split_weights(k, src, at_, n_):
                link(nc.gpsimd.tensor_copy(w_hi[:, at_:at_ + n_], src))
                nc.gpsimd.tensor_tensor(w_lo[:, at_:at_ + n_], src, w_hi[:, at_:at_ + n_], ALU.subtract)\
                    .then_inc(w_split[k], 1)

            def moe(k, nexp):
                s = mo[k]
                units = nexp * NH
                v = mrows[:, 2:4, :]
                pool.sem_inc(s["lo"], 2)

                def chunk(c, j, before, last):
                    for q in range(units):
                        K, m = c * units + q, j * units + q
                        pool.wait_ge(s["hi"], K + 1)
                        nc.gpsimd.tensor_tensor(hg_lo[:, m % DEPTH, :], v[:, m % 2, :], hg_hi[:, m % DEPTH, :],
                                                ALU.subtract).then_inc(s["lo"], 1)

                chunks(pool, chunk)

            for k in range(4):
                pool.wait_ge(w_in[k], W_IN[k])
                src = piece_buf[k % 3]
                if k == 2:
                    pool.wait_ge(rms_ready, 1)
                if k >= 2:
                    e0 = (k - 2) * HE
                    w1 = up_weights(src, 0, HE)
                    nc.gpsimd.tensor_tensor(w1, w1, rmsT[:, e0:e0 + HE].unsqueeze(2).to_broadcast([P, HE, HID]),
                                            ALU.mult).then_inc(w_scaled, 1)
                else:
                    split_weights(0, src, piece_at[k], PIECE)
            for k in range(2, 4):
                pool.wait_ge(w_high, k - 1)
                nc.gpsimd.tensor_tensor(w_lo[:, piece_at[k]:piece_at[k] + PIECE], piece_buf[k % 3],
                                        w_hi[:, piece_at[k]:piece_at[k] + PIECE], ALU.subtract)\
                    .then_inc(w_split[0], 1)
            moe(0, NE0)
            pool.wait_ge(w_in[4], W_IN[4])
            pool.wait_ge(phase_done, ended(8))
            for k in range(3):
                split_weights(1, raw1[:, k * NE1 * HID:(k + 1) * NE1 * HID], k * NE1 * HID, NE1 * HID)
            moe(1, NE1)

        @block.scalar
        def _(act):
            n = [0]

            def link(ins):
                n[0] += 1
                ins.then_inc(step_act, 1)
                act.wait_ge(step_act, n[0])

            def evacuate(k, banks, scale=None, bias=None):
                s = ln[k]
                act.sem_inc(s["xT"], 2)

                def one(b, j):
                    act.wait_ge(s["tr"], b + 1 + 2)
                    carry(act)
                    dst = xT[:, bass.ds(b, 1), PAD:].rearrange("p o t -> p (o t)")
                    if scale is None:
                        nc.scalar.activation(dst, banks[j], ACT.Copy).then_inc(s["xT"], 1)
                    else:
                        high = xT_hi[:, bass.ds(b, 1), PAD:].rearrange("p o t -> p (o t)")
                        nc.scalar.activation(dst, banks[j], ACT.Identity, scale=scale, bias=bias)
                        nc.scalar.activation(high, banks[j], ACT.Identity, scale=scale,
                                             bias=bias).then_inc(s["xT"], 1)

                return one

            for dst, src in smalls[0::2]:
                act.dma_start(dst, src).then_inc(loaded, 16)
            nc.scalar.preload_act_table(ACT.Silu)
            act.wait_ge(pre["wk"], 1)
            nc.scalar.activation(Wk_hi, Wk[:, :, :], ACT.Copy).then_inc(pre["wk_hi"], 1)
            barrier(act, 1)

            act.sem_inc(pre["xm"], 2)

            def silu_conv(b, j):
                act.wait_ge(pre["conv"], b + 1)
                carry(act)
                for g in range(NG):
                    last = nc.scalar.activation(xm[:, g, bass.ds(b * L, L)], ps[1 + j][:, g, :], ACT.Silu,
                                                bias=convb[:, g:g + 1])
                last.then_inc(pre["xm"], 1)

            act.sem_inc(pre["dtr"], 2)

            def copy_dt(b, j):
                act.wait_ge(pre["xp"], b + 1)
                carry(act)
                nc.scalar.activation(dtr[0:RANK, bass.ds(b, 1), :].rearrange("p o t -> p (o t)"), ps[3][R0:R1, j, :],
                                     ACT.Copy).then_inc(pre["dtr"], 1)

            thrice_skewed(act, evacuate(0, TRB[0], lnw, lnb), silu_conv, copy_dt)

            nc.scalar.preload_act_table_set("natural_log_exp_and_others")
            act.wait_ge(loaded, N_SMALL)
            link(nc.scalar.activation(Aneg[:, :, :], Aneg[:, :, :], ACT.Exp))
            link(nc.scalar.mul(Aneg[:, :, :], Aneg[:, :, :], -1.0))

            def softplus(b, j):
                act.wait_ge(pre["dtp"], b + 1)
                act.wait_ge(pre["dt"], b + 1 + 2)
                a, own = (t[:, 2 * (j % 2):2 * (j % 2) + 2, :] for t in (av, lt))
                for g in range(NG):
                    last = nc.scalar.activation(a[:, g, :], ps[j][:, g, :], ACT.Abs, bias=dtb[:, g:g + 1])
                last.then_inc(pre["absd"], 1)
                act.wait_ge(pre["absd"], b * 2 + 1)
                nc.scalar.activation(a, a, ACT.Exp, scale=-1.0).then_inc(pre["absd"], 1)
                act.wait_ge(pre["absd"], b * 2 + 2)
                nc.scalar.activation(own, a, ACT.Ln, bias=1.0)\
                    .then_inc(pre["soft"], 1)

            fours(act, softplus)
            barrier(act, 3)

            act.sem_inc(sc["cs"], 1)
            cs = ring[:, 12:16, :]
            with act.Fori(0, NB) as b:
                for n_ in range(NS):
                    N = b * NS + n_
                    act.wait_ge(sc["cb"], N + 1)
                    act.wait_ge(sc["hc"], N * 2 + 2)
                    nc.scalar.activation(cs[:, n_ % 4, :], ps[1][:, 0, :], ACT.Copy).then_inc(sc["cs"], 1)
                    for g in range(NG):
                        M = b * (NS * NG) + n_ * NG + g
                        act.wait_ge(sc["scan"], M + 1)
                        carry(act)
                        nc.scalar.activation(ps[2][:, g, :], dt[:, g, bass.ds(b * L, L)], ACT.Exp,
                                             scale=Aneg[:, g, n_:n_ + 1]).then_inc(sc["da"], 1)
            barrier(act, 4)

            sz = ring[:, 0:4, :]
            act.sem_inc(po["sz"], 2)
            act.sem_inc(po["oc"], 2)
            nc.scalar.preload_act_table(ACT.Silu)

            def silu_z(b, j):
                act.wait_ge(po["z"], b + 1)
                act.wait_ge(po["gated"], b + 1)
                nc.scalar.activation(sz[:, 2 * j:2 * j + 2, :], ps[j][:, :, :], ACT.Silu).then_inc(po["sz"], 1)

            def copy_o(b, j):
                act.wait_ge(po["o"], b + 1)
                act.wait_ge(po["tr"], b + 1)
                nc.scalar.activation(ring[:, 4 + j, :], ps[2][:, j, :], ACT.Copy).then_inc(po["oc"], 1)

            skewed(act, silu_z, copy_o)
            barrier(act, 5)

            def gates(k, E):
                s = gt[k]
                act.sem_inc(s["lc"], 2)
                with act.Fori(0, NB // 2) as i:
                    for j in range(2):
                        b = i * 2 + j
                        act.wait_ge(s["lt"], b + 1)
                        act.wait_ge(s["tm"], b + 1)
                        nc.scalar.activation(ring[0:E, j, :], ps[1][0:E, j, :], ACT.Copy).then_inc(s["lc"], 1)
                for i in range(2, 4):
                    if k == 0:
                        act.wait_ge(w_scaled, i - 1)
                        nc.scalar.activation(w_hi[:, piece_at[i]:piece_at[i] + PIECE], piece_buf[i % 3], ACT.Copy)\
                            .then_inc(w_high, 1)
                act.wait_ge(s["logit"], 1)
                nc.scalar.activation(gl[:, 1, :, 0:E], gl[:, 0, :, 0:E], ACT.Exp).then_inc(s["logit"], 1)

            def moe(k, nexp):
                s = mo[k]
                units = nexp * NH
                hs, v, ya = (mrows[:, r:r + 2, :] for r in (0, 2, 4))
                nc.scalar.preload_act_table(ACT.Silu)
                act.sem_inc(s["sil"], 2)
                act.sem_inc(s["acc"], NACC[k])

                def high(K, m):
                    act.wait_ge(s["gm"], K + 1 + 4)
                    act.wait_ge(s["mm2"], K + 1)
                    nc.scalar.activation(hg_hi[:, m % DEPTH, :], v[:, m % 2, :], ACT.Copy).then_inc(s["hi"], 1)

                def copy_sums(c, j):
                    act.wait_ge(s["mm2"], (c + 1) * units + DEPTH)
                    nc.scalar.activation(ya[:, j, :], ACC[k][j], ACT.Copy).then_inc(s["acc"], 1)

                def chunk(c, j, before, last):
                    for q in range(units):
                        K, m = c * units + q, j * units + q
                        act.wait_ge(s["g"] if k else s["h"], K + 1)
                        act.wait_ge(s["gm"], K + 3)
                        nc.scalar.activation(hs[:, m % 2, :], ps[0][:, m % 2, :], ACT.Silu).then_inc(s["sil"], 1)
                        if q or before:
                            high(K - 1, m - 1)
                        if q == (1 if k else 3) and before:
                            copy_sums(c - 1, 1 - j)
                        if q == 27 and before and not k:
                            evac(c - 1, 1 - j)
                    if last:
                        high(K, m)
                        copy_sums(c, j)
                        if not k:
                            evac(c, j)

                if not k:
                    evac = evacuate(2, TRB[2])
                chunks(act, chunk)

            nc.scalar.preload_act_table_set("natural_log_exp_and_others")
            pairs(act, evacuate(1, TRB[1]))
            barrier(act, 6)
            gates(0, E0)
            barrier(act, 7)
            moe(0, NE0)
            barrier(act, 8)

            nc.scalar.preload_act_table_set("natural_log_exp_and_others")
            evac = evacuate(3, TRB[3])
            act.sem_inc(at["even_out"], 1)
            act.sem_inc(at["pts"], 1)

            def evac_even(b, j, r):
                act.wait_ge(at["even"], b * 2 + r + 1)
                nc.scalar.activation(qkv[j][0:KD, 2 * r, :], ps[3][0:KD, 0, :], ACT.Copy,
                                     scale=1.0 if r else float(KD) ** -0.5).then_inc(at["even_out"], 1)

            def exps(b, j, i):
                act.wait_ge(at["mx"], b * TPB + i + 1)
                W = (i + 1) * P
                q = j * TPB + i
                nc.scalar.activation(pr[j][:, i, 0:W], ps[i // 2][:, i % 2, 0:W], ACT.Exp,
                                     bias=sm[:, 12, q:q + 1], accum_out=sm[:, 13, q:q + 1]).then_inc(at["p"], 1)

            def copy_pt(b, i):
                act.wait_ge(at["pt"], b * TPB + i + 1)
                W = (i + 1) * P
                nc.scalar.activation(pt[:, i % 2, 0:W], ps[2][:, 0, 0:W], ACT.Copy).then_inc(at["pts"], 1)

            def attend(b, j, before, scores, loads):
                for i in range(TPB):
                    copy_pt(b, i)
                    if loads and i == 0:
                        evac_even(b + 2, j, 0)
                    if loads and i == 2:
                        evac_even(b + 2, j, 1)
                    if scores:
                        exps(b + 1, 1 - j, i)
                    if before == 2 and i == 1:
                        evac(b - 2, j)

            for b in range(2):
                evac_even(b, b, 0)
                evac_even(b, b, 1)
            for i in range(TPB):
                exps(0, 0, i)
            batches(act, attend)
            evac(NB - 2, 0)
            evac(NB - 1, 1)
            barrier(act, 9)

            gates(1, E1)
            barrier(act, 10)
            moe(1, NE1)
            barrier(act, 11)

        @block.vector
        def _(dve):
            n = [0]

            def link(ins):
                n[0] += 1
                ins.then_inc(step, 1)
                dve.wait_ge(step, n[0])

            ALL = slice(0, NT)

            def counted(sm_, at_):
                k = [0]

                def link_(ins):
                    k[0] += 1
                    ins.then_inc(sm_, 1)
                    dve.wait_ge(sm_, at_ + k[0])

                return link_

            def root_step(i, y, z, t, link):
                if i == 0:
                    link(nc.vector.tensor_scalar(t.bitcast(i32), z.bitcast(i32), 1, None, ALU.logical_shift_right))
                elif i == 1:
                    link(nc.vector.tensor_scalar(y.bitcast(i32), t.bitcast(i32), -1.0, float(0x5f3759df),
                                                 ALU.mult, ALU.add))
                elif i % 3 == 2:
                    link(nc.vector.scalar_tensor_tensor(out=t, in0=z, scalar=-0.5, in1=y, op0=ALU.mult,
                                                        op1=ALU.mult))
                elif i % 3 == 0:
                    link(nc.vector.tensor_tensor(t, t, y, ALU.mult))
                else:
                    link(nc.vector.scalar_tensor_tensor(out=y, in0=t, scalar=1.5, in1=y, op0=ALU.add,
                                                        op1=ALU.mult))

            ROOT = 2 + 3 * 3

            def inverse_root(y, z, t, link):
                for i in range(ROOT):
                    root_step(i, y, z, t, link)

            def batch_stats(b, link=None, tiles=range(TPB)):
                for k in tiles:
                    t = b * TPB + k
                    last = nc.vector.bn_stats(stats[:, bass.ds(t, 1), :].rearrange("p o s -> p (o s)"),
                                              x[:, bass.ds(t, 1), :].rearrange("p o d -> p (o d)"))
                if link is not None and k == TPB - 1:
                    link(last)

            def moment_step(i, w, link):
                me, ve, mo_, vo = (stats[:, w, k] for k in (1, 2, 4, 5))
                a, b_, v = t0[:, w], t2[:, w], var[:, w]
                if i == 0:
                    link(nc.vector.tensor_tensor(a, me, mo_, ALU.add))
                elif i == 1:
                    link(nc.vector.tensor_scalar(mu[:, w], a, 0.5, None, ALU.mult))
                elif i == 2:
                    link(nc.vector.tensor_tensor(a, me, mo_, ALU.subtract))
                elif i == 3:
                    link(nc.vector.tensor_tensor(a, a, a, ALU.mult))
                elif i == 4:
                    link(nc.vector.tensor_tensor(b_, ve, vo, ALU.add))
                elif i == 5:
                    link(nc.vector.scalar_tensor_tensor(out=v, in0=a, scalar=D / 4.0, in1=b_, op0=ALU.mult,
                                                        op1=ALU.add))
                elif i == 6:
                    link(nc.vector.tensor_scalar(v, v, 1.0 / D, None, ALU.mult))
                elif i == 7:
                    link(nc.vector.tensor_scalar(t3[:, w], v, LN_EPS, None, ALU.add))
                else:
                    root_step(i - 8, r1[:, w], t3[:, w], t1[:, w], link)

            MOMENTS = 8 + ROOT

            def moments(w, link):
                for i in range(MOMENTS):
                    moment_step(i, w, link)

            def both_roots(eps):
                for i in range(8):
                    moment_step(i, ALL, link)
                link(nc.vector.tensor_copy(t2, t3))
                link(nc.vector.scalar_tensor_tensor(out=t3, in0=t2, scalar=eps, in1=var, op0=ALU.mult, op1=ALU.add))
                inverse_root(sm[:, 2:4, :], sm[:, 6:8, :], sm[:, 4:6, :], link)

            def second_root(eps, w, link):
                z = t3[:, w]
                link(nc.vector.tensor_tensor(z, r1[:, w], r1[:, w], ALU.mult))
                link(nc.vector.tensor_tensor(z, z, var[:, w], ALU.mult))
                link(nc.vector.tensor_scalar(z, z, eps, None, ALU.add))
                inverse_root(r2[:, w], z, t1[:, w], link)

            def normalise(k, scale, b, j, tiles=range(TPB)):
                s = ln[k]
                if 0 in tiles:
                    dve.wait_ge(s["tr"], b + 1)
                for q in tiles:
                    t = b * TPB + q
                    last = nc.vector.tensor_scalar(
                        xnt[:, j, q, :], x[:, bass.ds(t, 1), :].rearrange("p o d -> p (o d)"),
                        mu[:, bass.ds(t, 1)], scale[:, bass.ds(t, 1)], ALU.subtract, ALU.mult)
                if q == TPB - 1:
                    last.then_inc(s["norm"], 1)

            NORM_STEPS = 2 + (MOMENTS + 1) // 2 // 2 * 2 + 2

            def numbers(k, b):
                return counted(ln[k]["num"], b * (1 + MOMENTS))

            def batch_of(b):
                return bass.ds(b * TPB, TPB)

            dve.wait_ge(taps_in, 32)
            for k in range(TAPS):
                last = nc.vector.tensor_tensor(Wk[:, k, :], inw[:, 0:DI], cwb[:, :, k], ALU.mult)
            last.then_inc(pre["wk"], 1)
            for t in range(NT):
                if t % (NT // 2) == 0:
                    dve.wait_ge(x_in[t // (NT // 2)], 16)
                last = nc.vector.bn_stats(stats[:, t, :], x[:, t, :])
            link(last)
            dve.wait_ge(pre["wk_hi"], 1)
            nc.vector.tensor_tensor(Wk_lo, Wk[:, :, :], Wk_hi, ALU.subtract).then_inc(pre["wk_lo"], 1)
            both_roots(LN_EPS)
            link(nc.vector.tensor_scalar(gain, r1, 1.0, None, ALU.add))
            link(nc.vector.scalar_tensor_tensor(out=shift, in0=mu, scalar=-1.0, in1=r1, op0=ALU.mult, op1=ALU.mult))
            dve.wait_ge(vec_done, 1)
            link(nc.vector.tensor_copy(cols[:, 0:NV], ps[1][:, 0, 0:NV]))
            barrier(dve, 1)

            dve.sem_inc(pre["split"], 2)
            B3, B2 = 3 * BC, 2 * BC

            def norm_and_residual(b, j):
                normalise(0, r2, b, j)
                for q in range(TPB):
                    t = b * TPB + q
                    xt = x[:, bass.ds(t, 1), :].rearrange("p o d -> p (o d)")
                    nc.vector.tensor_scalar(xt, xt, gain[:, bass.ds(t, 1)], shift[:, bass.ds(t, 1)],
                                            ALU.mult, ALU.add)

            def split(b, j):
                w = bass.ds(b * L, L)
                dve.wait_ge(pre["xp"], b + 1)
                carry(dve)
                nc.vector.tensor_copy(bc[0:B3, w], ps[3][0:B3, j, :]).then_inc(pre["parts"], 1)
                dve.wait_ge(pre["parts"], b * 4 + 1)
                nc.vector.tensor_tensor(part[0:B3, :], ps[3][0:B3, j, :], bc[0:B3, w], ALU.subtract)\
                    .then_inc(pre["parts"], 1)
                dve.wait_ge(pre["parts"], b * 4 + 2)
                carry(dve)
                nc.vector.tensor_copy(bc[BC:B2, w], part[BC:B2, :])
                nc.vector.tensor_copy(bc[B2:B3, w], part[B2:B3, :]).then_inc(pre["parts"], 1)
                dve.wait_ge(pre["parts"], b * 4 + 3)
                nc.vector.tensor_tensor(part[B2:B3, :], part[B2:B3, :], bc[B2:B3, w], ALU.subtract)\
                    .then_inc(pre["parts"], 1)
                dve.wait_ge(pre["parts"], b * 4 + 4)
                carry(dve)
                nc.vector.tensor_copy(bc[B2:B3, w], part[B2:B3, :]).then_inc(pre["split"], 1)

            for b in range(3):
                norm_and_residual(b, b % 2)
            with dve.Fori(0, NB // 2 - 2) as i:
                for j in range(2):
                    norm_and_residual(i * 2 + j + 3, 1 - j)
                    split(i * 2 + j, j)
            norm_and_residual(NB - 1, 1)
            for b in range(NB - 4, NB):
                split(b, b % 2)

            dve.sem_inc(pre["dt"], 4)

            def soft_dt(b, j):
                w = bass.ds(b * L, L)
                dve.wait_ge(pre["soft"], b + 1)
                own = lt[:, 2 * (j % 2):2 * (j % 2) + 2, :]
                for g in range(NG):
                    last = nc.vector.scalar_tensor_tensor(out=dt[:, g, w], in0=ps[j][:, g, :],
                                                          scalar=dtb[:, g:g + 1], in1=own[:, g, :],
                                                          op0=ALU.add, op1=ALU.add)
                last.then_inc(pre["dsum"], 1)
                dve.wait_ge(pre["dsum"], b + 1)
                nc.vector.tensor_tensor(dt[:, :, w], dt[:, :, w], own, ALU.max)\
                    .then_inc(pre["dt"], 1)

            fours(dve, soft_dt)
            barrier(dve, 3)

            dbx, h = ring[:, 16:20, :], ring[:, 0:4, :]
            dve.sem_inc(sc["dbx"], 4)
            dve.sem_inc(sc["scan"], 2)
            dve.sem_inc(sc["y"], 1)

            def add_skip(b):
                dve.wait_ge(sc["ns"], (b + 1) * (NS * NG) + 8)
                for g in range(NG):
                    w = bass.ds(b * L, L)
                    last = nc.vector.scalar_tensor_tensor(out=xm[:, g, w], in0=xm[:, g, w], scalar=Dp[:, g:g + 1],
                                                          in1=ps[3][:, g, :], op0=ALU.mult, op1=ALU.add)
                last.then_inc(sc["y"], 1)

            def scan_batch(b, first):
                def input_term(m):
                    n_, g = m // NG, m % NG
                    if m == 0:
                        dve.wait_ge(pre["u"], b + 1)
                    if g == 0:
                        dve.wait_ge(sc["bb"], b * NS + n_ + 1)
                    if not first or m:
                        dve.wait_ge(sc["scan"], b * (NS * NG) + m)
                    nc.vector.tensor_tensor(dbx[:, m % 4, :], u[:, g, bass.ds(b * L, L)], ps[0][:, n_ % 2, :],
                                            ALU.mult).then_inc(sc["dbx"], 1)

                input_term(0)
                for m in range(NS * NG):
                    M = b * (NS * NG) + m
                    if m == 5 and not first:
                        add_skip(b - 1)
                    if m + 1 < NS * NG:
                        input_term(m + 1)
                    dve.wait_ge(sc["dbx"], M + 1 + 4)
                    dve.wait_ge(sc["da"], M + 1)
                    dve.wait_ge(sc["hc"], M + 1 + 4)
                    nc.vector.tensor_tensor_scan(h[:, m % 4, :], ps[2][:, m % NG, :], dbx[:, m % 4, :], 0.0,
                                                 ALU.mult, ALU.add).then_inc(sc["scan"], 1)

            scan_batch(0, True)
            with dve.Fori(1, NB) as b:
                scan_batch(b, False)
            add_skip(NB - 1)
            barrier(dve, 4)

            sz = ring[:, 0:4, :]
            dve.sem_inc(po["gated"], 2)
            dve.sem_inc(po["add"], 2)

            def gate_y(b, j):
                w = bass.ds(b * L, L)
                dve.wait_ge(po["sz"], b + 1 + 2)
                nc.vector.tensor_tensor(xm[:, :, w], xm[:, :, w], sz[:, 2 * j:2 * j + 2, :], ALU.mult)\
                    .then_inc(po["gated"], 1)

            def add_o(b, j):
                dve.wait_ge(po["tr"], b + 1 + 2)
                xb = x[:, bass.ds(b * TPB, TPB), :].rearrange("p t d -> p (t d)")
                nc.vector.scalar_tensor_tensor(out=xb, in0=ps[3][:, j, :], scalar=rs, in1=xb,
                                               op0=ALU.mult, op1=ALU.add).then_inc(po["add"], 1)
                dve.wait_ge(po["add"], b + 1 + 2)
                batch_stats(b)

            skewed(dve, gate_y, add_o)
            barrier(dve, 5)

            def exp_logits(k, E):
                s = gt[k]
                top = sm[:, 12, :]
                link(nc.vector.tensor_reduce(top, gl[:, 0, :, 0:E], op=ALU.max, axis=AX.X))
                link(nc.vector.tensor_tensor(gl[:, 0, :, 0:E], gl[:, 0, :, 0:E],
                                             top.unsqueeze(2).to_broadcast([P, NT, E]), ALU.subtract))
                dve.sem_inc(s["logit"], 1)
                link(nc.vector.memset(gl[:, 7, :, :], 1.0))
                dve.wait_ge(s["logit"], 2)

            def top2(k, E, eps, b0, b1):
                w = slice(b0 * TPB, b1 * TPB)
                T = (b1 - b0) * TPB
                W = [gl[:, q, w, 0:E] for q in range(7)]
                tk = [sm[:, q, w] for q in (12, 13, 14)]
                iv = iot[:, w, 0:E]

                def by_row(out_, a, v, op):
                    link(nc.vector.tensor_tensor(out_, a, v.unsqueeze(2).to_broadcast([P, T, E]), op))

                link(nc.vector.tensor_reduce(tk[0], W[1], op=ALU.add, axis=AX.X))
                yield
                link(nc.vector.reciprocal(tk[0], tk[0]))
                yield
                by_row(W[1], W[1], tk[0], ALU.mult)
                yield
                for q in range(2):
                    field = W[1 + q]
                    link(nc.vector.tensor_reduce(tk[q], field, op=ALU.max, axis=AX.X))
                    yield
                    by_row(W[3], field, tk[q], ALU.is_equal)
                    yield
                    link(nc.vector.tensor_tensor(W[3], W[3], iv, ALU.mult))
                    yield
                    link(nc.vector.tensor_reduce(tk[2], W[3], op=ALU.max, axis=AX.X))
                    yield
                    by_row(W[4 + q], W[3], tk[2], ALU.is_equal)
                    yield
                    if q == 0:
                        link(nc.vector.scalar_tensor_tensor(out=W[2], in0=W[4], scalar=-2.0, in1=W[1],
                                                            op0=ALU.mult, op1=ALU.add))
                        yield
                link(nc.vector.tensor_tensor(W[4], W[4], W[5], ALU.add))
                yield
                link(nc.vector.tensor_tensor(W[4], W[4], W[1], ALU.mult))
                yield
                link(nc.vector.tensor_tensor(tk[0], tk[0], tk[1], ALU.add))
                yield
                link(nc.vector.tensor_scalar(tk[0], tk[0], eps, None, ALU.add))
                yield
                link(nc.vector.reciprocal(tk[0], tk[0]))
                yield
                full = gl[:, 7, w, :]
                by_row(full[:, :, 0:E], W[4], tk[0], ALU.mult)
                yield
                hi, mid, low = (gate_parts[:, w, q * GW:(q + 1) * GW] for q in range(3))
                b16 = gl[:, 6, w, 0:GW // 2].bitcast(bf16)
                rest = gl[:, 5, w, :]
                link(nc.vector.tensor_copy(b16, full))
                yield
                link(nc.vector.tensor_copy(hi, b16))
                yield
                link(nc.vector.tensor_tensor(rest, full, hi, ALU.subtract))
                yield
                link(nc.vector.tensor_copy(b16, rest))
                yield
                link(nc.vector.tensor_copy(mid, b16))
                yield
                link(nc.vector.tensor_tensor(rest, rest, mid, ALU.subtract))
                yield
                link(nc.vector.tensor_copy(b16, rest))
                yield
                link(nc.vector.tensor_copy(low, b16))
                dve.sem_inc(gt[k]["stage"], 1)

            def take_gates(k, b, bank):
                s = gt[k]
                dve.wait_ge(s["tr"], b + 1)
                nc.vector.tensor_copy(bc[0:3 * GW, b * L:(b + 1) * L], bank[0:3 * GW, :]).then_inc(s["copied"], 1)

            def first_gates(k, E, eps):
                exp_logits(k, E)
                for _ in top2(k, E, eps, 0, GB[k]):
                    pass
                for b in range(GB[k]):
                    take_gates(k, b, ps[3 * (1 - b // 2)][:, b % 2, :])

            def take_logits(k, E):
                s = gt[k]
                dve.sem_inc(s["tk"], 2)
                with dve.Fori(0, NB // 2) as i:
                    for j in range(2):
                        b = i * 2 + j
                        dve.wait_ge(s["tm"], b + 1 + 2)
                        carry(dve)
                        src = ps[2][:, j, 0:TPB * GW].rearrange("p (t e) -> p t e", e=GW)
                        nc.vector.tensor_copy(gl[:, 0, bass.ds(b * TPB, TPB), 0:E], src[:, :, 0:E])\
                            .then_inc(s["tk"], 1)
                dve.wait_ge(s["tk"], NB + 2)

            def moe(k, nexp):
                rest = top2(k, (E0, E1)[k], (TOPK0_EPS, TOPK1_EPS)[k], GB[k], NB)
                s = mo[k]
                units = nexp * NH
                hs, v = mrows[:, 0:2, :], mrows[:, 2:4, :]
                dve.sem_inc(s["gm"], 4)
                if k:
                    dve.sem_inc(s["um"], 2)
                dve.sem_inc(s["add"], 1)

                def split_x(c, j):
                    carry(dve)
                    xc = xT[:, bass.ds(c, 1), PAD:].rearrange("p o t -> p (o t)")
                    nc.vector.tensor_copy(x_hi[:, j, :], xc).then_inc(s["xh"], 1)
                    dve.wait_ge(s["xh"], c + 1)
                    nc.vector.tensor_tensor(x_lo[:, j, :], xc, x_hi[:, j, :], ALU.subtract).then_inc(s["xl"], 1)

                def add_sums(c):
                    dve.wait_ge(s["tr"], c + 1)
                    xb = x[:, bass.ds(c * TPB, TPB), :].rearrange("p t d -> p (t d)")
                    nc.vector.tensor_tensor(xb, xb, TRS[k], ALU.add).then_inc(s["add"], 1)

                def norm_step(i, c, j, num):
                    half = range(i % 2 * TPB // 2, (i % 2 + 1) * TPB // 2)
                    if i < 2:
                        if i == 0:
                            dve.wait_ge(s["add"], c + 1 + 1)
                        batch_stats(c, num, half)
                    elif i < NORM_STEPS - 2:
                        for n_ in range(2 * (i - 2), min(2 * (i - 1), MOMENTS)):
                            moment_step(n_, batch_of(c), num)
                    elif i < NORM_STEPS:
                        normalise(2, r1, c, j, half)

                def chunk(c, j, before, last):
                    if not before:
                        split_x(c, j)
                    for q in range(units):
                        K, m = c * units + q, j * units + q
                        dve.wait_ge(s["sil"], K + 1 + 2)
                        if k:
                            dve.wait_ge(s["h"], K + 1)
                            nc.vector.tensor_tensor(hs[:, m % 2, :], hs[:, m % 2, :], ps[1][:, m % 2, :], ALU.mult)\
                                .then_inc(s["um"], 1)
                            dve.wait_ge(s["um"], K + 1 + 2)
                        dve.wait_ge(s["gb"], c * nexp + q // NH + 1)
                        dve.wait_ge(s["lo"], K + 1)
                        nc.vector.tensor_tensor(v[:, m % 2, :], hs[:, m % 2, :],
                                                ps[2][:, (m // NH) % 2, :], ALU.mult).then_inc(s["gm"], 1)
                        if q == units // 2 and not last:
                            if before:
                                dve.wait_ge(s["h"], c * units)
                            split_x(c + 1, 1 - j)
                        if before < 2 and not (k and before and q % 2):
                            next(rest, None)
                            if k and not before and q % 2 == 0:
                                next(rest, None)
                        b = GATE_UNITS[k].get(q - LAG)
                        if before == 1 and b is not None:
                            take_gates(k, b, GATE_BANK[k])
                        if q == 8 and before:
                            add_sums(c - 1)
                            num = numbers(2, c - 1)
                        if q > 8 and before and not k:
                            norm_step(q - 9, c - 1, 1 - j, num)
                    if last:
                        add_sums(c)
                        num = numbers(2, c)
                        for i in range(NORM_STEPS):
                            if not k:
                                norm_step(i, c, j, num)

                chunks(dve, chunk)

            dve.drain()
            both_roots(RMS_EPS)
            link(nc.vector.reciprocal(gain, r2))
            link(nc.vector.tensor_tensor(gain, gain, r1, ALU.mult))
            pairs(dve, lambda b, j: normalise(1, r2, b, j))
            dve.wait_ge(gt[0]["wt"], 1)
            link(nc.vector.tensor_copy(rmsT[:, :], ps[1][:, 0, 0:E0 + E0S]))
            dve.sem_inc(rms_ready, 1)
            barrier(dve, 6)

            take_logits(0, E0)
            link(nc.vector.tensor_tensor(gl[:, 0, :, 0:E0], gl[:, 0, :, 0:E0],
                                         gain.unsqueeze(2).to_broadcast([P, NT, E0]), ALU.mult))
            first_gates(0, E0, TOPK0_EPS)
            barrier(dve, 7)
            dve.wait_ge(w_split[0], 4)
            moe(0, NE0)
            barrier(dve, 8)

            dve.sem_inc(at["add"], 1)
            dve.sem_inc(at["odd_out"], 1)

            def evac_odd(b, j, r):
                dve.wait_ge(at["odd"], b * 2 + r + 1)
                if r == 0:
                    nc.vector.tensor_copy(qkv[j][0:KD, 1, :], ps[3][0:KD, 1, :]).then_inc(at["odd_out"], 1)
                else:
                    nc.vector.tensor_copy(vs[j], ps[3][:, 1, :]).then_inc(at["odd_out"], 1)

            def mask_max(b, j, i):
                dve.wait_ge(at["s"], b * TPB + i + 1)
                S_ = ps[i // 2][:, i % 2, :]
                q = j * TPB + i
                nc.vector.tensor_tensor(S_[:, i * P:(i + 1) * P], S_[:, i * P:(i + 1) * P], cmask[:, :],
                                        ALU.add).then_inc(at["masked"], 1)
                dve.wait_ge(at["masked"], b * TPB + i + 1)
                nc.vector.tensor_reduce(sm[:, 12, q:q + 1], S_[:, 0:(i + 1) * P], op=ALU.max, axis=AX.X,
                                        negate=True).then_inc(at["mx"], 1)

            def attend(b, j, before, scores, loads):
                for i in range(TPB):
                    if loads and i == 1:
                        evac_odd(b + 2, j, 0)
                    if scores:
                        mask_max(b + 1, 1 - j, i)
                    if before and i < TPB - 1:
                        norm_part(i, b - 1, 1 - j)
                q = j * TPB
                dve.wait_ge(at["p"], (b + 1) * TPB)
                nc.vector.reciprocal(sm[:, 14, q:q + TPB], sm[:, 13, q:q + TPB]).then_inc(at["rd"], 1)
                if loads:
                    evac_odd(b + 2, j, 1)
                dve.wait_ge(at["rd"], b + 1)
                dve.wait_ge(at["o"], (b + 1) * TPB)
                for i in range(TPB):
                    xb = x[:, bass.ds(b * TPB + i, 1), :].rearrange("p t d -> p (t d)")
                    last = nc.vector.scalar_tensor_tensor(out=xb, in0=ps[2][:, 1, i * P:(i + 1) * P],
                                                          scalar=sm[:, 14, q + i:q + i + 1], in1=xb,
                                                          op0=ALU.mult, op1=ALU.add)
                last.then_inc(at["add"], 1)
                if before:
                    norm_part(TPB - 1, b - 1, 1 - j)

            norm4 = {}
            STEPS4 = [range(0), range(0, 4), range(4, 12), range(12, MOMENTS)]

            def norm_part(i, b, j):
                if i == 1:
                    norm4["num"] = numbers(3, b)
                    dve.wait_ge(at["add"], b + 1 + 1)
                    batch_stats(b, norm4["num"])
                for n_ in range(MOMENTS):
                    if n_ in STEPS4[i]:
                        moment_step(n_, batch_of(b), norm4["num"])
                if i == TPB - 1:
                    normalise(3, r1, b, j)

            for b in range(2):
                evac_odd(b, b, 0)
                evac_odd(b, b, 1)
            for i in range(TPB):
                mask_max(0, 0, i)
            batches(dve, attend)
            for i in range(TPB):
                norm_part(i, NB - 1, 1)
            barrier(dve, 9)

            dve.wait_ge(w_split[1], 3)
            second_root(LN_EPS, ALL, link)
            dve.wait_ge(gt[1]["wt"], 1)
            link(nc.vector.tensor_copy(gwT[:, :], ps[1][:, 0, 0:E1]))
            link(nc.vector.tensor_copy(lnbr[:, :], lnsb[:, 1:2].to_broadcast([P, P])))
            dve.sem_inc(gt[1]["wc"], 1)
            dve.wait_ge(gt[1]["wt"], 2)
            link(nc.vector.tensor_copy(gconst[:, :], ps[1][:, 0, 0:E1]))
            link(nc.vector.tensor_scalar(gwT[:, :], gwT[:, :], lnsb[:, 0:1], None, ALU.mult))
            dve.sem_inc(gt[1]["wc"], 1)
            take_logits(1, E1)
            link(nc.vector.tensor_tensor(gl[:, 0, :, 0:E1], gl[:, 0, :, 0:E1],
                                         r2.unsqueeze(2).to_broadcast([P, NT, E1]), ALU.mult))
            link(nc.vector.tensor_tensor(gl[:, 0, :, 0:E1], gl[:, 0, :, 0:E1],
                                         gconst[:, :].unsqueeze(1).to_broadcast([P, NT, E1]), ALU.add))
            first_gates(1, E1, TOPK1_EPS)
            barrier(dve, 10)
            moe(1, NE1)
            barrier(dve, 11)

        @block.tensor
        def _(pe):
            def transposes(k):
                s = ln[k]
                pe.sem_inc(s["tr"], 2)

                def one(b, j):
                    pe.wait_ge(s["norm"], b + 1)
                    pe.wait_ge(s["xT"], b + 1 if k < 2 else b + 2)
                    for q in range(TPB):
                        last = nc.tensor.transpose(TRB[k][j][:, q * P:(q + 1) * P], xnt[:, j, q, :], ident[:, :])
                    last.then_inc(s["tr"], 1)

                return one

            def three(out_, w, hi, lo, start=True, stop=True):
                nc.tensor.matmul(out_, w[0], hi, start=start, stop=False)
                nc.tensor.matmul(out_, w[0], lo, start=False, stop=False)
                return nc.tensor.matmul(out_, w[1], hi, start=False, stop=stop)

            def rows(b):
                return xT[:, bass.ds(b, 1), PAD:].rearrange("p o t -> p (o t)")

            pe.wait_ge(loaded, N_SMALL)
            pe.wait_ge(ident_ready, 1)
            nc.tensor.transpose(ps[1][:, 0, 0:NV], vrows[:, :], ident[0:NV, 0:NV]).then_inc(vec_done, 1)
            barrier(pe, 1)

            pe.wait_ge(pre["wk_lo"], 1)
            def conv(b, j):
                pe.wait_ge(pre["x_lo"], b + 1)
                pe.wait_ge(pre["xm"], b + 1)
                for g in range(NG):
                    for k in range(TAPS):
                        xh, xl = (t[:, bass.ds(b, 1), k:k + L].rearrange("p o t -> p (o t)") for t in (xT_hi, xT_lo))
                        last = three(ps[1 + j][:, g, :], [t[:, k, g * P:(g + 1) * P] for t in (Wk_hi, Wk_lo)], xh, xl,
                                     k == 0, k == TAPS - 1)
                last.then_inc(pre["conv"], 1)

            def project_x(b, j):
                pe.wait_ge(pre["xm"], b + 1 + 2)
                pe.wait_ge(pre["split"], b + 1)
                pe.wait_ge(pre["dtr"], b + 1)
                for g in range(NG):
                    last = nc.tensor.matmul(ps[3][0:R1, j, :], xpw[:, g, :], xm[:, g, bass.ds(b * L, L)],
                                            start=g == 0, stop=g == NG - 1)
                last.then_inc(pre["xp"], 1)

            thrice_skewed(pe, transposes(0), conv, project_x)

            pe.wait_ge(ln[0]["xT"], NB + 2)
            pe.wait_ge(pre["xm"], NB + 2)
            pe.wait_ge(pre["dtr"], NB + 2)
            def project_dt(b, j):
                pe.wait_ge(pre["dt"], b + 1)
                if j == 3:
                    pe.wait_ge(pre["split"], NB + 2)
                carry(pe)
                for g in range(NG):
                    last = nc.tensor.matmul(ps[j][:, g, :], dtw[:, g * P:(g + 1) * P],
                                            dtr[0:RANK, bass.ds(b, 1), :].rearrange("p o t -> p (o t)"),
                                            start=True, stop=True)
                last.then_inc(pre["dtp"], 1)

            fours(pe, project_dt)
            pe.wait_ge(consts_ready, 1)
            barrier(pe, 3)

            hc = ring[:, 4:12, :]
            pe.sem_inc(sc["ns"], 8)

            def spread(b, n_, N):
                w = bass.ds(b * L, L)
                pe.wait_ge(sc["dbx"], N * 2 + 2)
                nc.tensor.matmul(ps[0][:, n_ % 2, :], sel[:, n_, :], bc[:, w], start=True, stop=True)\
                    .then_inc(sc["bb"], 1)
                pe.wait_ge(sc["cs"], N + 1)
                nc.tensor.matmul(ps[1][:, 0, :], sel[:, NS + n_, :], bc[:, w], start=True, stop=True)\
                    .then_inc(sc["cb"], 1)

            def sum_state(b, n_):
                for g in range(NG):
                    m = n_ * NG + g
                    if m == 0:
                        pe.wait_ge(sc["y"], b + 1)
                    pe.wait_ge(sc["hc"], b * (NS * NG) + m + 1 + 8)
                    nc.tensor.matmul(ps[3][:, g, :], ident[:, :], hc[:, m % 8, :], start=n_ == 0,
                                     stop=n_ == NS - 1, skip_group_check=True).then_inc(sc["ns"], 1)

            def spread_batch(b, first):
                for n_ in range(NS):
                    if n_ + 1 < NS:
                        spread(b, n_ + 1, b * NS + n_ + 1)
                    else:
                        spread(b + 1, 0, (b + 1) * NS)
                    if n_ >= BEHIND:
                        sum_state(b, n_ - BEHIND)
                    elif not first:
                        sum_state(b - 1, n_ - BEHIND + NS)

            BEHIND = 2
            spread(0, 0, 0)
            spread_batch(0, True)
            with pe.Fori(1, NB) as b:
                spread_batch(b, False)
            for n_ in range(NS - BEHIND, NS):
                sum_state(NB - 1, n_)
            barrier(pe, 4)

            pe.sem_inc(po["tr"], 2)

            def project_z(b, j):
                pe.wait_ge(po["sz"], b + 1)
                for g in range(NG):
                    last = nc.tensor.matmul(ps[j][:, g, :], inw[:, DI + g * P:DI + (g + 1) * P], rows(b),
                                            start=True, stop=True)
                last.then_inc(po["z"], 1)

            def project_y(b, j):
                pe.wait_ge(po["gated"], b + 1 + 2)
                pe.wait_ge(po["oc"], b + 1)
                for g in range(NG):
                    last = nc.tensor.matmul(ps[2][:, j, :], opw[:, g, :], xm[:, g, bass.ds(b * L, L)],
                                            start=g == 0, stop=g == NG - 1)
                last.then_inc(po["o"], 1)
                pe.wait_ge(po["oc"], b + 1 + 2)
                pe.wait_ge(po["add"], b + 1)
                for q in range(TPB):
                    last = nc.tensor.transpose(ps[3][:, j, q * P:(q + 1) * P],
                                               ring[:, 4 + j, q * P:(q + 1) * P], ident[:, :])
                last.then_inc(po["tr"], 1)

            skewed(pe, project_z, project_y)
            barrier(pe, 5)

            def gate_rows(k, b, bank):
                s = gt[k]
                pe.wait_ge(s["stage"], 1 if b < GB[k] else 2)
                if b > GB[k]:
                    pe.wait_ge(s["copied"], b)
                for q in range(TPB):
                    last = nc.tensor.transpose(bank[0:3 * GW, q * P:(q + 1) * P], gate_parts[:, b * TPB + q, :],
                                               ident[:, :])
                last.then_inc(s["tr"], 1)

            def router(k, w, E):
                s = gt[k]
                pe.sem_inc(s["tm"], 2)

                def logits(b, j):
                    pe.wait_ge(s["lc"], b + 1)
                    nc.tensor.matmul(ps[1][0:E, j, :], w, rows(b), start=True, stop=True).then_inc(s["lt"], 1)

                def token_major(b, j):
                    pe.wait_ge(s["lc"], b + 1 + 2)
                    pe.wait_ge(s["tk"], b + 1)
                    carry(pe)
                    for q in range(TPB):
                        last = nc.tensor.transpose(ps[2][:, j, q * GW:q * GW + E],
                                                   ring[0:E, j, q * P:(q + 1) * P], ident[0:E, 0:E])
                    last.then_inc(s["tm"], 1)

                skewed(pe, logits, token_major)
                for b in range(GB[k]):
                    gate_rows(k, b, ps[3 * (1 - b // 2)][:, b % 2, :])

            def moe(k, nexp, w_first, w_second, w_down):
                s = mo[k]
                units = nexp * NH
                ya = mrows[:, 4:6, :]
                pe.sem_inc(s["mm2"], DEPTH)

                def up(w, e, hb):
                    return [t[:, e, hb * P:(hb + 1) * P] for t in w]

                def hidden(c, j, q):
                    e, hb = q // NH, q % NH
                    K, m = c * units + q, j * units + q
                    if q == 0:
                        pe.wait_ge(s["xl"], c + 1)
                    pe.wait_ge(s["sil"], K + 1)
                    last = three(ps[0][:, m % 2, :], up(w_first, e, hb), x_hi[:, j, :], x_lo[:, j, :])
                    if w_second is not None:
                        last.then_inc(s["g"], 1)
                        pe.wait_ge(s["um"], K + 1)
                        last = three(ps[1][:, m % 2, :], up(w_second, e, hb), x_hi[:, j, :], x_lo[:, j, :])
                    last.then_inc(s["h"], 1)
                    if hb == 0:
                        if e == 0:
                            pe.wait_ge(gt[k]["copied"], c + 1)
                        pe.wait_ge(s["gm"], (c * nexp + e) * 2 + 2)
                        carry(pe)
                        nc.tensor.matmul(ps[2][:, (j * nexp + e) % 2, :], selg[:, e, :],
                                         bc[0:3 * GW, bass.ds(c * L, L)], start=True, stop=True)\
                            .then_inc(s["gb"], 1)

                def token_major(c, j):
                    pe.wait_ge(s["acc"], c + 1 + NACC[k])
                    pe.wait_ge(s["add"], c + 1)
                    for q in range(TPB):
                        last = nc.tensor.transpose(TRS[k][:, q * P:(q + 1) * P], ya[:, j, q * P:(q + 1) * P],
                                                   ident[:, :])
                    last.then_inc(s["tr"], 1)

                def chunk(c, j, before, last):
                    if not before:
                        for q in range(AHEAD):
                            hidden(c, j, q)
                    for q in range(units):
                        if q + AHEAD < units:
                            hidden(c, j, q + AHEAD)
                        elif not last:
                            hidden(c + 1, 1 - j, q + AHEAD - units)
                        K, m = c * units + q, j * units + q
                        if q == 0:
                            pe.wait_ge(s["acc"], c + 1)
                        pe.wait_ge(s["lo"], K + 1 + 2)
                        three(ACC[k][j], [t[:, q // NH, q % NH, :] for t in w_down], hg_hi[:, m % DEPTH, :],
                              hg_lo[:, m % DEPTH, :], q == 0, q == units - 1).then_inc(s["mm2"], 1)
                        b = GATE_UNITS[k].get(q)
                        if before == 1 and b is not None:
                            if k and b == GB[k]:
                                pe.wait_ge(s["add"], 1 + 1)
                            gate_rows(k, b, GATE_BANK[k])
                        if q == 3 and before:
                            token_major(c - 1, 1 - j)
                        if q == 22 and before and not k:
                            norm(c - 1, 1 - j)
                    if last:
                        token_major(c, j)
                        if not k:
                            norm(c, j)

                if not k:
                    norm = transposes(2)
                chunks(pe, chunk)

            nc.tensor.transpose(ps[1][:, 0, 0:E0 + E0S], rmsr[:, :], ident[0:E0 + E0S, 0:E0 + E0S])\
                .then_inc(gt[0]["wt"], 1)
            pairs(pe, transposes(1))
            barrier(pe, 6)
            router(0, wr[:, :], E0)
            barrier(pe, 7)
            pe.wait_ge(w_split[0], 4)
            moe(0, NE0, moe0_w1, None, moe0_w2)
            barrier(pe, 8)

            norm = transposes(3)
            pe.wait_ge(ln[2]["xT"], NB + 2)

            def load_qk(b, j):
                pe.wait_ge(at["even_out"], b * 2 + 1)
                carry(pe)
                nc.tensor.matmul(ps[3][0:KD, 0, :], wqk[:, 0, :], rows(b), start=True, stop=True)\
                    .then_inc(at["even"], 1)
                pe.wait_ge(at["odd_out"], b * 2 + 1)
                carry(pe)
                nc.tensor.matmul(ps[3][0:KD, 1, :], wqk[:, 1, :], rows(b), start=True, stop=True)\
                    .then_inc(at["odd"], 1)

            def load_v1(b, j):
                pe.wait_ge(at["even_out"], b * 2 + 2)
                carry(pe)
                nc.tensor.matmul(ps[3][0:KD, 0, :], wqk[:, 2, :], rows(b), start=True, stop=True)\
                    .then_inc(at["even"], 1)

            def load_v(b, j):
                pe.wait_ge(at["even_out"], b * 2 + 3)
                pe.wait_ge(at["odd_out"], b * 2 + 2)
                for i in range(TPB):
                    last = nc.tensor.matmul(ps[3][:, 1, i * P:(i + 1) * P], qkv[j][0:KD, 2, i * P:(i + 1) * P],
                                            wv2[:, :], start=True, stop=True)
                last.then_inc(at["odd"], 1)

            def scores_of(b, j, i):
                if i == 0:
                    pe.wait_ge(at["even_out"], b * 2 + 2)
                    pe.wait_ge(at["odd_out"], b * 2 + 2)
                nc.tensor.matmul(ps[i // 2][:, i % 2, 0:(i + 1) * P], qkv[j][0:KD, 0, i * P:(i + 1) * P],
                                 qkv[j][0:KD, 1, 0:(i + 1) * P], start=True, stop=True).then_inc(at["s"], 1)

            def attend(b, j, before, scores, loads):
                for i in range(TPB):
                    pe.wait_ge(at["p"], b * TPB + i + 1)
                    pe.wait_ge(at["pts"], b * TPB + i + 1)
                    for k in range(i + 1):
                        last = nc.tensor.transpose(ps[2][:, 0, k * P:(k + 1) * P],
                                                   pr[j][:, i, k * P:(k + 1) * P], ident[:, :])
                    last.then_inc(at["pt"], 1)
                    if loads and i == 0:
                        load_qk(b + 2, j)
                    if before == 2 and i == 1:
                        pe.wait_ge(at["even_out"], b * 2 + 6 if loads else NB * 2 + 1)
                        norm(b - 2, j)
                    if loads and i == 2:
                        if before == 2:
                            pe.wait_ge(ln[3]["xT"], b - 1 + 2)
                        load_v1(b + 2, j)
                    if scores:
                        scores_of(b + 1, 1 - j, i)
                    pe.wait_ge(at["pts"], b * TPB + i + 1 + 1)
                    if i == 0:
                        pe.wait_ge(at["odd_out"], b * 2 + 3)
                        pe.wait_ge(at["add"], b + 1)
                    for k in range(i + 1):
                        last = nc.tensor.matmul(ps[2][:, 1, i * P:(i + 1) * P], pt[:, i % 2, k * P:(k + 1) * P],
                                                vs[j][:, k * P:(k + 1) * P], start=k == 0, stop=k == i)
                    last.then_inc(at["o"], 1)
                if loads:
                    load_v(b + 2, j)

            for b in range(2):
                load_qk(b, b)
                load_v1(b, b)
                load_v(b, b)
            for i in range(TPB):
                scores_of(0, 0, i)
            batches(pe, attend)
            norm(NB - 2, 0)
            norm(NB - 1, 1)
            barrier(pe, 9)

            nc.tensor.transpose(ps[1][:, 0, 0:E1], gwr[:, :], ident[0:E1, 0:E1]).then_inc(gt[1]["wt"], 1)
            pe.wait_ge(gt[1]["wc"], 1)
            nc.tensor.matmul(ps[1][:, 0, 0:E1], lnbr[:, :], gwT[:, :], start=True, stop=True)\
                .then_inc(gt[1]["wt"], 1)
            pe.wait_ge(gt[1]["wc"], 2)
            pe.wait_ge(ln[3]["xT"], NB + 2)
            router(1, gwT[:, :], E1)
            barrier(pe, 10)
            pe.wait_ge(w_split[1], 3)
            moe(1, NE1, moe1_wg, moe1_wu, moe1_wd)
            barrier(pe, 11)


_IN_ORDER = ['L0_attn_x', 'L0_attn_ln_w', 'L0_attn_ln_b', 'L0_attn_in_proj_w', 'L0_attn_conv_w', 'L0_attn_conv_b',
             'L0_attn_x_proj_w', 'L0_attn_dt_proj_w', 'L0_attn_dt_proj_b', 'L0_attn_A_log', 'L0_attn_D_param',
             'L0_attn_out_proj_w', 'L0_attn_res_scale', 'L0_ffn_router_w', 'L0_ffn_rms_w', 'L0_ffn_w1', 'L0_ffn_w2',
             'L0_ffn_rms_w_s', 'L0_ffn_w1_s', 'L0_ffn_w2_s', 'L1_attn_w_q', 'L1_attn_w_k', 'L1_attn_w_v1',
             'L1_attn_w_v2', 'L1_ffn_ln_scale', 'L1_ffn_ln_bias', 'L1_ffn_gate_w', 'L1_ffn_Wg', 'L1_ffn_Wu',
             'L1_ffn_Wd', 'L1_ffn_sWg', 'L1_ffn_sWu', 'L1_ffn_sWd']


def kernel(**inputs):
    import numpy as np
    import concourse.bacc as bacc
    from concourse.bass_utils import run_bass_kernel_spmd

    nc = bacc.Bacc("TRN2", target_bir_lowering=False, num_devices=1)
    arrays, args = {}, {}
    for name in _IN_ORDER:
        a = np.ascontiguousarray(inputs[name])
        arrays[f"in_{name}"] = a
        args[name] = nc.dram_tensor(f"in_{name}", a.shape, mybir.dt.from_np(a.dtype), kind="ExternalInput").ap()
    shape = arrays["in_L0_attn_x"].shape
    out = nc.dram_tensor("out_x", shape, mybir.dt.float32, kind="ExternalOutput").ap()
    mamba_moe_attention_moe_kernel(nc, args, out)
    r = run_bass_kernel_spmd(nc, [arrays], core_ids=[0])
    return r.results[0]["out_x"]
```
